# Optimizing a Trainium2 kernel written in Bass

```python
import numpy as np
import jax
import jax.numpy as jnp

def _softmax(x, axis=-1):
    return jax.nn.softmax(x, axis=axis)

def _gelu(x):
    return jax.nn.gelu(x, approximate=True)

def _silu(x):
    return jax.nn.silu(x)

def _sigmoid(x):
    return jax.nn.sigmoid(x)

def _layernorm(x, axis=-1, eps=1e-05):
    m = jnp.mean(x, axis=axis, keepdims=True)
    v = jnp.var(x, axis=axis, keepdims=True)
    return (x - m) / jnp.sqrt(v + eps)

def _scatter_add(tgt, idx, src, axis=0):
    return tgt.at[idx].add(src)

def _segment_sum(src, seg, n):
    return jax.ops.segment_sum(src, seg, n)
kernel_name = 'mk_macaron_d4_jaxref_r8_a391ef'

def setup_inputs(seed: int=0):
    np.random.seed(seed)
    _w = jnp.asarray

    def _L0_attn_setup():
        import jax, jax.numpy as jnp
        import numpy as np
        N_HEADS = 16
        HEAD_DIM = 64
        ROPE_THETA = 10000.0

        def _rope_cos_sin(seq_len, dim, theta):
            inv_freq = 1.0 / theta ** (jnp.arange(0, dim, 2, dtype=jnp.float32) / dim)
            pos = jnp.arange(seq_len, dtype=jnp.float32)
            freqs = pos[:, None] * inv_freq[None, :]
            emb = jnp.concatenate([freqs, freqs], axis=-1)
            return (jnp.cos(emb), jnp.sin(emb))

        def _rotate_half(x):
            d = x.shape[-1] // 2
            return jnp.concatenate([-x[..., d:], x[..., :d]], axis=-1)
        key = jax.random.key(seed)
        ks = jax.random.split(key, 6)
        B, S, D_MODEL, LATENT = (1, 512, 128, 64)
        q_dim = N_HEADS * HEAD_DIM
        sd = lambda fan_in: 1.0 / np.sqrt(fan_in)
        return {'x': jax.random.normal(ks[0], (B, S, D_MODEL), jnp.float32), 'wq': jax.random.normal(ks[1], (q_dim, D_MODEL), jnp.float32) * sd(D_MODEL), 'w_kv_down': jax.random.normal(ks[2], (LATENT, D_MODEL), jnp.float32) * sd(D_MODEL), 'w_k_up': jax.random.normal(ks[3], (q_dim, LATENT), jnp.float32) * sd(LATENT), 'w_v_up': jax.random.normal(ks[4], (q_dim, LATENT), jnp.float32) * sd(LATENT), 'wo': jax.random.normal(ks[5], (D_MODEL, q_dim), jnp.float32) * sd(q_dim)}
    _L0_attn_in = _L0_attn_setup()

    def _L0_ffn_setup():
        import jax, jax.numpy as jnp
        import numpy as np
        DIM = 128
        NUM_EXPERTS = 6
        TOP_K = 2
        HIDDEN = DIM * 2
        key = jax.random.key(seed)
        ks = jax.random.split(key, 7)
        s_in = 1.0 / np.sqrt(DIM)
        s_h = 1.0 / np.sqrt(HIDDEN)
        x = jax.random.normal(ks[0], (4, 256, DIM), dtype=jnp.float32)
        Wg = jax.random.uniform(ks[1], (DIM, NUM_EXPERTS), jnp.float32, -s_in, s_in)
        bg = jax.random.uniform(ks[2], (NUM_EXPERTS,), jnp.float32, -s_in, s_in)
        W1 = jax.random.uniform(ks[3], (NUM_EXPERTS, DIM, HIDDEN), jnp.float32, -s_in, s_in)
        b1 = jax.random.uniform(ks[4], (NUM_EXPERTS, HIDDEN), jnp.float32, -s_in, s_in)
        W2 = jax.random.uniform(ks[5], (NUM_EXPERTS, HIDDEN, DIM), jnp.float32, -s_h, s_h)
        b2 = jax.random.uniform(ks[6], (NUM_EXPERTS, DIM), jnp.float32, -s_h, s_h)
        return {'x': x, 'Wg': Wg, 'bg': bg, 'W1': W1, 'b1': b1, 'W2': W2, 'b2': b2}
    _L0_ffn_in = _L0_ffn_setup()

    def _L1_attn_setup():
        import jax, jax.numpy as jnp
        import numpy as np
        H, D, CR, SEL_K = (8, 64, 32, 16)
        ROPE_DIM, THETA, WINDOW, GROUPS = (32, 10000.0, 64, 2)
        INTER, HID, QC = (64, 128, 32)
        NEG = -1e+30

        def _rope_cache(t):
            half = ROPE_DIM // 2
            inv = 1.0 / THETA ** (jnp.arange(half, dtype=jnp.float32) * 2.0 / ROPE_DIM)
            ang = jnp.arange(t, dtype=jnp.float32)[:, None] * inv[None, :]
            return (jnp.cos(ang), jnp.sin(ang))

        def _apply_partial_rope(x, cos, sin):
            half = ROPE_DIM // 2
            x1, x2, rest = (x[..., :half], x[..., half:ROPE_DIM], x[..., ROPE_DIM:])
            return jnp.concatenate([x1 * cos - x2 * sin, x1 * sin + x2 * cos, rest], -1)

        def _rmsnorm(x, g, eps=1e-06):
            return x * jax.lax.rsqrt(jnp.mean(x * x, -1, keepdims=True) + eps) * g
        key = jax.random.key(seed)
        ks = jax.random.split(key, 9)
        f = lambda k, shp, s: jax.random.normal(k, shp, jnp.float32) * s
        return {'h': f(ks[0], (1, 256, HID), 1.0), 'w_qc': f(ks[1], (HID, QC), QC ** (-0.5)), 'w_qup': f(ks[2], (QC, H * D), (H * D) ** (-0.5)), 'w_k': f(ks[3], (HID, D), HID ** (-0.5)), 'w_v': f(ks[4], (HID, D), HID ** (-0.5)), 'g_qnorm': jnp.ones((D,), jnp.float32), 'g_knorm': jnp.ones((D,), jnp.float32), 'w_gate': f(ks[5], (D, 3), 0.05), 'b_gate': jnp.zeros((3,), jnp.float32), 'sink_logit': f(ks[6], (H,), 0.1), 'w_out_group': f(ks[7], (GROUPS, H // GROUPS * D, INTER), 0.05), 'w_out': f(ks[8], (GROUPS * INTER, HID), 0.03)}
    _L1_attn_in = _L1_attn_setup()

    def _L1_ffn_setup():
        import jax, jax.numpy as jnp
        import numpy as np
        D_MODEL, D_FF, D2, DL = (128, 512, 64, 64)
        D1 = D_FF // D2
        BATCH, SEQ = (2, 128)
        KERNEL_SCALE = D2 ** 0.5
        key = jax.random.key(seed)
        ks = jax.random.split(key, 7)
        xav = lambda k, shape, fan: jax.random.normal(k, shape, jnp.float32) * (2.0 / sum(fan)) ** 0.5
        x = jax.random.normal(ks[0], (BATCH, SEQ, D_MODEL), jnp.float32)
        m1 = xav(ks[1], (D_MODEL, DL), (D_MODEL, DL))
        m2 = xav(ks[2], (DL, D1, D2), (DL, D_FF))
        mb = jax.random.normal(ks[3], (D1, D2), jnp.float32)
        w1 = xav(ks[4], (D_MODEL, D1, D2), (D_MODEL, D_FF))
        w2 = xav(ks[5], (D2, D1, D_MODEL), (D_FF, D_MODEL)) * KERNEL_SCALE
        b2 = jax.random.normal(ks[6], (D_MODEL,), jnp.float32)
        return {'x': x, 'm1': m1, 'm2': m2, 'mb': mb, 'w1': w1, 'w2': w2, 'b2': b2}
    _L1_ffn_in = _L1_ffn_setup()

    def _L2_attn_setup():
        import jax, jax.numpy as jnp
        import numpy as np
        DIM = 128
        HEADS = 16
        DIM_HEAD = 64
        SOFTCLAMP = 50.0

        def _rmsnorm(x, w):
            eps = jnp.finfo(x.dtype).eps
            var = jnp.mean(jnp.square(x), axis=-1, keepdims=True)
            return x * jax.lax.rsqrt(var + eps) * w

        def _head_rmsnorm(x, gamma):
            norm = jnp.linalg.norm(x, axis=-1, keepdims=True)
            normed = x / jnp.maximum(norm, 1e-12)
            scale = (gamma + 1.0) * DIM_HEAD ** 0.5
            return normed * scale[None, :, None, :]
        key = jax.random.key(seed)
        ks = jax.random.split(key, 7)
        b, n = (4, 256)
        di = HEADS * DIM_HEAD
        s = 0.02
        return {'tokens': jax.random.normal(ks[0], (b, n, DIM), dtype=jnp.float32), 'norm_w': jnp.ones((DIM,), dtype=jnp.float32), 'Wq': jax.random.normal(ks[1], (DIM, di), dtype=jnp.float32) * s, 'Wkv': jax.random.normal(ks[2], (DIM, 2 * di), dtype=jnp.float32) * s, 'Wo': jax.random.normal(ks[3], (di, DIM), dtype=jnp.float32) * s, 'q_gamma': jnp.zeros((HEADS, DIM_HEAD), dtype=jnp.float32), 'k_gamma': jnp.zeros((HEADS, DIM_HEAD), dtype=jnp.float32)}
    _L2_attn_in = _L2_attn_setup()

    def _L2_ffn_setup():
        import jax, jax.numpy as jnp
        import numpy as np
        D_MODEL = 128
        D_FF = 512
        N_EXPERTS = 8
        TOP_K = 2
        LN_EPS = 1e-06

        def _moe(x, router_w, w1, b1, w2, b2, gamma, beta):
            B, S, D = x.shape
            x_flat = x.reshape(-1, D)
            N = x_flat.shape[0]
            logits = x_flat @ router_w
            gate_vals, gate_idx = jax.lax.top_k(logits, TOP_K)
            gate_w = jax.nn.softmax(gate_vals, axis=-1)
            gates = jnp.zeros_like(logits).at[jnp.arange(N)[:, None], gate_idx].set(gate_w)
            h = jax.nn.gelu(jnp.einsum('nd,edf->enf', x_flat, w1) + b1[:, None, :], approximate=False)
            out = jnp.einsum('enf,efd->end', h, w2) + b2[:, None, :]
            res = x_flat[None, :, :] + out
            mu = jnp.mean(res, axis=-1, keepdims=True)
            var = jnp.mean(jnp.square(res - mu), axis=-1, keepdims=True)
            normed = (res - mu) * jax.lax.rsqrt(var + LN_EPS)
            expert_out = normed * gamma[:, None, :] + beta[:, None, :]
            y = jnp.einsum('end,ne->nd', expert_out, gates)
            return y.reshape(B, S, D)
        key = jax.random.key(seed)
        ks = jax.random.split(key, 8)
        x = jax.random.normal(ks[0], (2, 256, D_MODEL), dtype=jnp.float32)
        router_w = jax.random.normal(ks[1], (D_MODEL, N_EXPERTS), dtype=jnp.float32) * 0.02
        w1 = jax.random.normal(ks[2], (N_EXPERTS, D_MODEL, D_FF), dtype=jnp.float32) * 0.02
        b1 = jnp.zeros((N_EXPERTS, D_FF), dtype=jnp.float32)
        w2 = jax.random.normal(ks[3], (N_EXPERTS, D_FF, D_MODEL), dtype=jnp.float32) * 0.02
        b2 = jnp.zeros((N_EXPERTS, D_MODEL), dtype=jnp.float32)
        gamma = jnp.ones((N_EXPERTS, D_MODEL), dtype=jnp.float32)
        beta = jnp.zeros((N_EXPERTS, D_MODEL), dtype=jnp.float32)
        return {'x': x, 'router_w': router_w, 'w1': w1, 'b1': b1, 'w2': w2, 'b2': b2, 'gamma': gamma, 'beta': beta}
    _L2_ffn_in = _L2_ffn_setup()

    def _L3_attn_setup():
        import jax, jax.numpy as jnp
        import numpy as np
        LN_EPS = 1e-05

        def _min_gru(x, Wz, bz, Wh, bh):
            z = jax.nn.sigmoid(jnp.einsum('btd,de->bte', x, Wz) + bz)
            h_tilde = jnp.einsum('btd,de->bte', x, Wh) + bh
            a = 1.0 - z
            b = z * h_tilde

            def combine(c1, c2):
                a1, b1 = c1
                a2, b2 = c2
                return (a1 * a2, a2 * b1 + b2)
            _, h = jax.lax.associative_scan(combine, (a, b), axis=1)
            return h
        key = jax.random.key(seed)
        ks = jax.random.split(key, 4)
        B, T, D = (8, 256, 128)
        x = jax.random.normal(ks[0], (B, T, D), dtype=jnp.float32)
        Wz = jax.random.normal(ks[1], (D, D), dtype=jnp.float32) * (1.0 / np.sqrt(D))
        bz = jnp.zeros((D,), dtype=jnp.float32)
        Wh = jax.random.normal(ks[2], (D, D), dtype=jnp.float32) * (1.0 / np.sqrt(D))
        bh = jnp.zeros((D,), dtype=jnp.float32)
        swish_beta = jnp.float32(1.0)
        ln_gamma = jnp.ones((D,), dtype=jnp.float32)
        ln_beta = jnp.zeros((D,), dtype=jnp.float32)
        return {'x': x, 'Wz': Wz, 'bz': bz, 'Wh': Wh, 'bh': bh, 'swish_beta': swish_beta, 'ln_gamma': ln_gamma, 'ln_beta': ln_beta}
    _L3_attn_in = _L3_attn_setup()

    def _L3_ffn_setup():
        import jax, jax.numpy as jnp
        import numpy as np
        EPS = 1e-05
        NUM_HEADS = 16
        NUM_KV_HEADS = 4
        NUM_EXPERTS = 8
        TOP_K = 2

        def _layernorm(x, w, b):
            mu = jnp.mean(x, axis=-1, keepdims=True)
            var = jnp.mean((x - mu) ** 2, axis=-1, keepdims=True)
            return (x - mu) * jax.lax.rsqrt(var + EPS) * w + b
        key = jax.random.key(seed)
        ks = jax.random.split(key, 8)
        S, B, H = (128, 4, 128)
        F = 256
        hd = H // NUM_HEADS
        qkv_out = (NUM_HEADS + 2 * NUM_KV_HEADS) * hd
        w_scale = 0.02
        return {'hidden_states': jax.random.normal(ks[0], (S, B, H), jnp.float32), 'ln1_weight': jnp.ones((H,), jnp.float32), 'ln1_bias': jnp.zeros((H,), jnp.float32), 'ln2_weight': jnp.ones((H,), jnp.float32), 'ln2_bias': jnp.zeros((H,), jnp.float32), 'qkv_weight': jax.random.normal(ks[1], (qkv_out, H), jnp.float32) * w_scale, 'proj_weight': jax.random.normal(ks[2], (H, H), jnp.float32) * w_scale, 'router_weight': jax.random.normal(ks[3], (NUM_EXPERTS, H), jnp.float32) * w_scale, 'moe_w1': jax.random.normal(ks[4], (NUM_EXPERTS, H, F), jnp.float32) * w_scale, 'moe_w2': jax.random.normal(ks[5], (NUM_EXPERTS, F, H), jnp.float32) * w_scale}
    _L3_ffn_in = _L3_ffn_setup()
    _d = {'L0_attn_x': _L0_attn_in['x'], 'L0_attn_wq': _L0_attn_in['wq'], 'L0_attn_w_kv_down': _L0_attn_in['w_kv_down'], 'L0_attn_w_k_up': _L0_attn_in['w_k_up'], 'L0_attn_w_v_up': _L0_attn_in['w_v_up'], 'L0_attn_wo': _L0_attn_in['wo'], 'L0_ffn_Wg': _L0_ffn_in['Wg'], 'L0_ffn_bg': _L0_ffn_in['bg'], 'L0_ffn_W1': _L0_ffn_in['W1'], 'L0_ffn_b1': _L0_ffn_in['b1'], 'L0_ffn_W2': _L0_ffn_in['W2'], 'L0_ffn_b2': _L0_ffn_in['b2'], 'L1_attn_w_qc': _L1_attn_in['w_qc'], 'L1_attn_w_qup': _L1_attn_in['w_qup'], 'L1_attn_w_k': _L1_attn_in['w_k'], 'L1_attn_w_v': _L1_attn_in['w_v'], 'L1_attn_g_qnorm': _L1_attn_in['g_qnorm'], 'L1_attn_g_knorm': _L1_attn_in['g_knorm'], 'L1_attn_w_gate': _L1_attn_in['w_gate'], 'L1_attn_b_gate': _L1_attn_in['b_gate'], 'L1_attn_sink_logit': _L1_attn_in['sink_logit'], 'L1_attn_w_out_group': _L1_attn_in['w_out_group'], 'L1_attn_w_out': _L1_attn_in['w_out'], 'L1_ffn_m1': _L1_ffn_in['m1'], 'L1_ffn_m2': _L1_ffn_in['m2'], 'L1_ffn_mb': _L1_ffn_in['mb'], 'L1_ffn_w1': _L1_ffn_in['w1'], 'L1_ffn_w2': _L1_ffn_in['w2'], 'L1_ffn_b2': _L1_ffn_in['b2'], 'L2_attn_norm_w': _L2_attn_in['norm_w'], 'L2_attn_Wq': _L2_attn_in['Wq'], 'L2_attn_Wkv': _L2_attn_in['Wkv'], 'L2_attn_Wo': _L2_attn_in['Wo'], 'L2_attn_q_gamma': _L2_attn_in['q_gamma'], 'L2_attn_k_gamma': _L2_attn_in['k_gamma'], 'L2_ffn_router_w': _L2_ffn_in['router_w'], 'L2_ffn_w1': _L2_ffn_in['w1'], 'L2_ffn_b1': _L2_ffn_in['b1'], 'L2_ffn_w2': _L2_ffn_in['w2'], 'L2_ffn_b2': _L2_ffn_in['b2'], 'L2_ffn_gamma': _L2_ffn_in['gamma'], 'L2_ffn_beta': _L2_ffn_in['beta'], 'L3_attn_Wz': _L3_attn_in['Wz'], 'L3_attn_bz': _L3_attn_in['bz'], 'L3_attn_Wh': _L3_attn_in['Wh'], 'L3_attn_bh': _L3_attn_in['bh'], 'L3_attn_swish_beta': _L3_attn_in['swish_beta'], 'L3_attn_ln_gamma': _L3_attn_in['ln_gamma'], 'L3_attn_ln_beta': _L3_attn_in['ln_beta'], 'L3_ffn_ln1_weight': _L3_ffn_in['ln1_weight'], 'L3_ffn_ln1_bias': _L3_ffn_in['ln1_bias'], 'L3_ffn_ln2_weight': _L3_ffn_in['ln2_weight'], 'L3_ffn_ln2_bias': _L3_ffn_in['ln2_bias'], 'L3_ffn_qkv_weight': _L3_ffn_in['qkv_weight'], 'L3_ffn_proj_weight': _L3_ffn_in['proj_weight'], 'L3_ffn_router_weight': _L3_ffn_in['router_weight'], 'L3_ffn_moe_w1': _L3_ffn_in['moe_w1'], 'L3_ffn_moe_w2': _L3_ffn_in['moe_w2']}
    _x0 = _d['L0_attn_x']
    _d['L0_attn_x'] = jax.random.normal(jax.random.fold_in(jax.random.key(seed), 1), (2, 1024, 128), dtype=_x0.dtype)
    del _x0
    return _d

def reference(L0_attn_x, L0_attn_wq, L0_attn_w_kv_down, L0_attn_w_k_up, L0_attn_w_v_up, L0_attn_wo, L0_ffn_Wg, L0_ffn_bg, L0_ffn_W1, L0_ffn_b1, L0_ffn_W2, L0_ffn_b2, L1_attn_w_qc, L1_attn_w_qup, L1_attn_w_k, L1_attn_w_v, L1_attn_g_qnorm, L1_attn_g_knorm, L1_attn_w_gate, L1_attn_b_gate, L1_attn_sink_logit, L1_attn_w_out_group, L1_attn_w_out, L1_ffn_m1, L1_ffn_m2, L1_ffn_mb, L1_ffn_w1, L1_ffn_w2, L1_ffn_b2, L2_attn_norm_w, L2_attn_Wq, L2_attn_Wkv, L2_attn_Wo, L2_attn_q_gamma, L2_attn_k_gamma, L2_ffn_router_w, L2_ffn_w1, L2_ffn_b1, L2_ffn_w2, L2_ffn_b2, L2_ffn_gamma, L2_ffn_beta, L3_attn_Wz, L3_attn_bz, L3_attn_Wh, L3_attn_bh, L3_attn_swish_beta, L3_attn_ln_gamma, L3_attn_ln_beta, L3_ffn_ln1_weight, L3_ffn_ln1_bias, L3_ffn_ln2_weight, L3_ffn_ln2_bias, L3_ffn_qkv_weight, L3_ffn_proj_weight, L3_ffn_router_weight, L3_ffn_moe_w1, L3_ffn_moe_w2):

    def _L0_attn_ref(x, wq, w_kv_down, w_k_up, w_v_up, wo):
        import jax, jax.numpy as jnp
        import numpy as np
        N_HEADS = 16
        HEAD_DIM = 64
        ROPE_THETA = 10000.0

        def _rope_cos_sin(seq_len, dim, theta):
            inv_freq = 1.0 / theta ** (jnp.arange(0, dim, 2, dtype=jnp.float32) / dim)
            pos = jnp.arange(seq_len, dtype=jnp.float32)
            freqs = pos[:, None] * inv_freq[None, :]
            emb = jnp.concatenate([freqs, freqs], axis=-1)
            return (jnp.cos(emb), jnp.sin(emb))

        def _rotate_half(x):
            d = x.shape[-1] // 2
            return jnp.concatenate([-x[..., d:], x[..., :d]], axis=-1)
        B, S, _ = x.shape
        H, D = (N_HEADS, HEAD_DIM)
        q = jnp.einsum('bsd,qd->bsq', x, wq).reshape(B, S, H, D).transpose(0, 2, 1, 3)
        kv_latent = jnp.einsum('bsd,ld->bsl', x, w_kv_down)
        k = jnp.einsum('bsl,ql->bsq', kv_latent, w_k_up).reshape(B, S, H, D).transpose(0, 2, 1, 3)
        v = jnp.einsum('bsl,ql->bsq', kv_latent, w_v_up).reshape(B, S, H, D).transpose(0, 2, 1, 3)
        cos, sin = _rope_cos_sin(S, D, ROPE_THETA)
        cos = cos[None, None]
        sin = sin[None, None]
        q = q * cos + _rotate_half(q) * sin
        k = k * cos + _rotate_half(k) * sin
        scores = jnp.einsum('bhsd,bhtd->bhst', q, k) / jnp.sqrt(jnp.float32(D))
        causal = jnp.triu(jnp.full((S, S), -jnp.inf, dtype=jnp.float32), k=1)
        scores = scores + causal[None, None]
        probs = jax.nn.softmax(scores.astype(jnp.float32), axis=-1).astype(q.dtype)
        out = jnp.einsum('bhst,bhtd->bhsd', probs, v)
        out = out.transpose(0, 2, 1, 3).reshape(B, S, H * D)
        return jnp.einsum('bsq,dq->bsd', out, wo)

    def _L0_ffn_ref(x, Wg, bg, W1, b1, W2, b2):
        import jax, jax.numpy as jnp
        import numpy as np
        DIM = 128
        NUM_EXPERTS = 6
        TOP_K = 2
        HIDDEN = DIM * 2
        gate_logits = jnp.einsum('bsd,de->bse', x, Wg) + bg
        topk_w, topk_idx = jax.lax.top_k(gate_logits, TOP_K)
        topk_w = jax.nn.softmax(topk_w, axis=-1)
        combine = jnp.sum(jax.nn.one_hot(topk_idx, NUM_EXPERTS, dtype=x.dtype) * topk_w[..., None], axis=-2)
        h = jnp.einsum('bsd,edh->ebsh', x, W1) + b1[:, None, None, :]
        h = jax.nn.gelu(h, approximate=False)
        y = jnp.einsum('ebsh,ehd->ebsd', h, W2) + b2[:, None, None, :]
        out = jnp.einsum('ebsd,bse->bsd', y, combine)
        return out

    def _L1_attn_ref(h, w_qc, w_qup, w_k, w_v, g_qnorm, g_knorm, w_gate, b_gate, sink_logit, w_out_group, w_out):
        import jax, jax.numpy as jnp
        import numpy as np
        H, D, CR, SEL_K = (8, 64, 32, 16)
        ROPE_DIM, THETA, WINDOW, GROUPS = (32, 10000.0, 64, 2)
        INTER, HID, QC = (64, 128, 32)
        NEG = -1e+30

        def _rope_cache(t):
            half = ROPE_DIM // 2
            inv = 1.0 / THETA ** (jnp.arange(half, dtype=jnp.float32) * 2.0 / ROPE_DIM)
            ang = jnp.arange(t, dtype=jnp.float32)[:, None] * inv[None, :]
            return (jnp.cos(ang), jnp.sin(ang))

        def _apply_partial_rope(x, cos, sin):
            half = ROPE_DIM // 2
            x1, x2, rest = (x[..., :half], x[..., half:ROPE_DIM], x[..., ROPE_DIM:])
            return jnp.concatenate([x1 * cos - x2 * sin, x1 * sin + x2 * cos, rest], -1)

        def _rmsnorm(x, g, eps=1e-06):
            return x * jax.lax.rsqrt(jnp.mean(x * x, -1, keepdims=True) + eps) * g
        b, t, _ = h.shape
        cos, sin = _rope_cache(t)
        q = (h @ w_qc @ w_qup).reshape(b, t, H, D).transpose(0, 2, 1, 3)
        q = _rmsnorm(_apply_partial_rope(q, cos, sin), g_qnorm)
        k = _rmsnorm(_apply_partial_rope(h @ w_k, cos, sin), g_knorm)
        v = h @ w_v
        scale = 1.0 / np.sqrt(D).astype(np.float32)
        qpos = jnp.arange(t)
        sink = jnp.broadcast_to(sink_logit[None, :, None, None], (b, H, t, 1))
        nb = t // CR
        kc = k[:, :nb * CR].reshape(b, nb, CR, D).mean(2)
        vc = v[:, :nb * CR].reshape(b, nb, CR, D).mean(2)
        comp_valid = ((jnp.arange(nb) + 1) * CR - 1)[None, :] <= qpos[:, None]
        any_blk = comp_valid.any(-1, keepdims=True)
        safe = jnp.where(any_blk, comp_valid, True)
        sc_raw = jnp.einsum('bhqd,bnd->bhqn', q, kc) * scale
        pc = jax.nn.softmax(jnp.concatenate([jnp.where(safe, sc_raw, NEG), sink], -1), -1)
        comp_out = jnp.einsum('bhqn,bnd->bhqd', pc[..., :nb], vc)
        comp_out = jnp.where(any_blk[None, None], comp_out, 0.0)
        sel_sc = jnp.where(comp_valid, sc_raw, -jnp.inf)
        top_idx = jax.lax.top_k(sel_sc, min(SEL_K, nb))[1]
        sel_blocks = (top_idx[..., :, None] == jnp.arange(nb)).any(-2)
        block_of = jnp.minimum(qpos // CR, nb - 1)
        causal = qpos[:, None] >= qpos[None, :]
        in_range = qpos < nb * CR
        tok_sel = sel_blocks[..., block_of] & (causal & in_range[None, :])[None, None]
        scores_full = jnp.einsum('bhqd,bkd->bhqk', q, k) * scale
        ps = jax.nn.softmax(jnp.where(tok_sel, scores_full, NEG), -1)
        sel_out = jnp.einsum('bhqk,bkd->bhqd', ps, v)
        sw = causal & (qpos[:, None] - qpos[None, :] < WINDOW)
        pw = jax.nn.softmax(jnp.concatenate([jnp.where(sw[None, None], scores_full, NEG), sink], -1), -1)
        sw_out = jnp.einsum('bhqk,bkd->bhqd', pw[..., :t], v)
        g = jax.nn.sigmoid(q @ w_gate + b_gate)
        g = g / jnp.clip(g.sum(-1, keepdims=True), 1e-06)
        mixed = g[..., 0:1] * comp_out + g[..., 1:2] * sel_out + g[..., 2:3] * sw_out
        x = mixed.transpose(0, 2, 1, 3).reshape(b, t, GROUPS, H // GROUPS * D)
        y = jnp.einsum('btgf,gfi->btgi', x, w_out_group).reshape(b, t, GROUPS * INTER)
        return y @ w_out

    def _L1_ffn_ref(x, m1, m2, mb, w1, w2, b2):
        import jax, jax.numpy as jnp
        import numpy as np
        D_MODEL, D_FF, D2, DL = (128, 512, 64, 64)
        D1 = D_FF // D2
        BATCH, SEQ = (2, 128)
        KERNEL_SCALE = D2 ** 0.5
        x_shape = x.shape
        xf = x.reshape(-1, x_shape[-1])
        d1 = w1.shape[1]
        lr = xf @ m1
        mask_logits = jnp.einsum('bl,lxy->bxy', lr, m2) + mb
        quant_mask = jnp.argmax(mask_logits, axis=-1)
        w1p = jnp.transpose(w1, (1, 2, 0))
        w2p = jnp.transpose(w2, (1, 0, 2))
        j = jnp.arange(d1)[None, :]
        w = w1p[j, quant_mask]
        mid = jnp.einsum('ai,aji->aj', xf, w)
        relu = jax.nn.relu(mid)
        v = w2p[j, quant_mask]
        res = jnp.einsum('ai,aij->aj', relu, v) + b2
        return res.reshape(x_shape)

    def _L2_attn_ref(tokens, norm_w, Wq, Wkv, Wo, q_gamma, k_gamma):
        import jax, jax.numpy as jnp
        import numpy as np
        DIM = 128
        HEADS = 16
        DIM_HEAD = 64
        SOFTCLAMP = 50.0

        def _rmsnorm(x, w):
            eps = jnp.finfo(x.dtype).eps
            var = jnp.mean(jnp.square(x), axis=-1, keepdims=True)
            return x * jax.lax.rsqrt(var + eps) * w

        def _head_rmsnorm(x, gamma):
            norm = jnp.linalg.norm(x, axis=-1, keepdims=True)
            normed = x / jnp.maximum(norm, 1e-12)
            scale = (gamma + 1.0) * DIM_HEAD ** 0.5
            return normed * scale[None, :, None, :]
        b, n, _ = tokens.shape
        x = _rmsnorm(tokens, norm_w)
        q = x @ Wq
        kv = x @ Wkv
        k, v = jnp.split(kv, 2, axis=-1)
        split = lambda t: t.reshape(b, n, HEADS, DIM_HEAD).transpose(0, 2, 1, 3)
        q, k, v = (split(q), split(k), split(v))
        q = _head_rmsnorm(q, q_gamma)
        k = _head_rmsnorm(k, k_gamma)
        sim = jnp.einsum('bhid,bhjd->bhij', q, k)
        sim = jnp.tanh(sim / SOFTCLAMP) * SOFTCLAMP
        sim = sim * DIM_HEAD ** (-0.5)
        attn = jax.nn.softmax(sim, axis=-1)
        out = jnp.einsum('bhij,bhjd->bhid', attn, v)
        out = out.transpose(0, 2, 1, 3).reshape(b, n, HEADS * DIM_HEAD)
        return out @ Wo

    def _L2_ffn_ref(x, router_w, w1, b1, w2, b2, gamma, beta):
        import jax, jax.numpy as jnp
        import numpy as np
        D_MODEL = 128
        D_FF = 512
        N_EXPERTS = 8
        TOP_K = 2
        LN_EPS = 1e-06

        def _moe(x, router_w, w1, b1, w2, b2, gamma, beta):
            B, S, D = x.shape
            x_flat = x.reshape(-1, D)
            N = x_flat.shape[0]
            logits = x_flat @ router_w
            gate_vals, gate_idx = jax.lax.top_k(logits, TOP_K)
            gate_w = jax.nn.softmax(gate_vals, axis=-1)
            gates = jnp.zeros_like(logits).at[jnp.arange(N)[:, None], gate_idx].set(gate_w)
            h = jax.nn.gelu(jnp.einsum('nd,edf->enf', x_flat, w1) + b1[:, None, :], approximate=False)
            out = jnp.einsum('enf,efd->end', h, w2) + b2[:, None, :]
            res = x_flat[None, :, :] + out
            mu = jnp.mean(res, axis=-1, keepdims=True)
            var = jnp.mean(jnp.square(res - mu), axis=-1, keepdims=True)
            normed = (res - mu) * jax.lax.rsqrt(var + LN_EPS)
            expert_out = normed * gamma[:, None, :] + beta[:, None, :]
            y = jnp.einsum('end,ne->nd', expert_out, gates)
            return y.reshape(B, S, D)
        return _moe(x, router_w, w1, b1, w2, b2, gamma, beta)

    def _L3_attn_ref(x, Wz, bz, Wh, bh, swish_beta, ln_gamma, ln_beta):
        import jax, jax.numpy as jnp
        import numpy as np
        LN_EPS = 1e-05

        def _min_gru(x, Wz, bz, Wh, bh):
            z = jax.nn.sigmoid(jnp.einsum('btd,de->bte', x, Wz) + bz)
            h_tilde = jnp.einsum('btd,de->bte', x, Wh) + bh
            a = 1.0 - z
            b = z * h_tilde

            def combine(c1, c2):
                a1, b1 = c1
                a2, b2 = c2
                return (a1 * a2, a2 * b1 + b2)
            _, h = jax.lax.associative_scan(combine, (a, b), axis=1)
            return h
        h = _min_gru(x, Wz, bz, Wh, bh)
        s = swish_beta * h
        y = s * jax.nn.sigmoid(s)
        mu = jnp.mean(y, axis=-1, keepdims=True)
        var = jnp.mean(jnp.square(y - mu), axis=-1, keepdims=True)
        out = (y - mu) * jax.lax.rsqrt(var + LN_EPS) * ln_gamma + ln_beta
        return out

    def _L3_ffn_ref(hidden_states, ln1_weight, ln1_bias, ln2_weight, ln2_bias, qkv_weight, proj_weight, router_weight, moe_w1, moe_w2):
        import jax, jax.numpy as jnp
        import numpy as np
        EPS = 1e-05
        NUM_HEADS = 16
        NUM_KV_HEADS = 4
        NUM_EXPERTS = 8
        TOP_K = 2

        def _layernorm(x, w, b):
            mu = jnp.mean(x, axis=-1, keepdims=True)
            var = jnp.mean((x - mu) ** 2, axis=-1, keepdims=True)
            return (x - mu) * jax.lax.rsqrt(var + EPS) * w + b
        S, B, H = hidden_states.shape
        hd = H // NUM_HEADS
        rep = NUM_HEADS // NUM_KV_HEADS
        scale = 1.0 / hd ** 0.5
        ln1_out = _layernorm(hidden_states, ln1_weight, ln1_bias)
        qkv = jnp.einsum('sbh,oh->sbo', ln1_out, qkv_weight)
        q = qkv[..., :NUM_HEADS * hd].reshape(S, B, NUM_HEADS, hd)
        k = qkv[..., NUM_HEADS * hd:(NUM_HEADS + NUM_KV_HEADS) * hd].reshape(S, B, NUM_KV_HEADS, hd)
        v = qkv[..., (NUM_HEADS + NUM_KV_HEADS) * hd:].reshape(S, B, NUM_KV_HEADS, hd)
        k = jnp.repeat(k, rep, axis=2)
        v = jnp.repeat(v, rep, axis=2)
        scores = jnp.einsum('sbhd,tbhd->bhst', q, k) * scale
        causal = jnp.tril(jnp.ones((S, S), bool))
        scores = jnp.where(causal, scores, jnp.finfo(scores.dtype).min)
        probs = jax.nn.softmax(scores, axis=-1)
        attn = jnp.einsum('bhst,tbhd->sbhd', probs, v).reshape(S, B, H)
        proj_out = jnp.einsum('sbh,oh->sbo', attn, proj_weight)
        hidden_after_attn = hidden_states + proj_out
        ln2_out = _layernorm(hidden_after_attn, ln2_weight, ln2_bias)
        x = ln2_out.reshape(-1, H)
        logits = jnp.einsum('th,eh->te', x, router_weight)
        gate = jax.nn.softmax(logits, axis=-1)
        top_probs, top_idx = jax.lax.top_k(gate, TOP_K)
        h_mid = jax.nn.gelu(jnp.einsum('th,ehf->etf', x, moe_w1))
        expert_out = jnp.einsum('etf,efh->eth', h_mid, moe_w2)
        e_ids = jnp.arange(NUM_EXPERTS)[:, None, None]
        weights = jnp.sum(jnp.where(top_idx[None] == e_ids, top_probs[None], 0.0), axis=-1)
        moe_out = jnp.einsum('eth,et->th', expert_out, weights).reshape(S, B, H)
        return hidden_after_attn + moe_out
    x = L0_attn_x
    x = x + 0.5 * _L0_ffn_ref(_layernorm(x, axis=-1), L0_ffn_Wg, L0_ffn_bg, L0_ffn_W1, L0_ffn_b1, L0_ffn_W2, L0_ffn_b2)
    x = x + _L0_attn_ref(_layernorm(x, axis=-1), L0_attn_wq, L0_attn_w_kv_down, L0_attn_w_k_up, L0_attn_w_v_up, L0_attn_wo)
    x = x + 0.5 * _L0_ffn_ref(_layernorm(x, axis=-1), L0_ffn_Wg, L0_ffn_bg, L0_ffn_W1, L0_ffn_b1, L0_ffn_W2, L0_ffn_b2)
    x = x + 0.5 * _L1_ffn_ref(_layernorm(x, axis=-1), L1_ffn_m1, L1_ffn_m2, L1_ffn_mb, L1_ffn_w1, L1_ffn_w2, L1_ffn_b2)
    x = x + _L1_attn_ref(_layernorm(x, axis=-1), L1_attn_w_qc, L1_attn_w_qup, L1_attn_w_k, L1_attn_w_v, L1_attn_g_qnorm, L1_attn_g_knorm, L1_attn_w_gate, L1_attn_b_gate, L1_attn_sink_logit, L1_attn_w_out_group, L1_attn_w_out)
    x = x + 0.5 * _L1_ffn_ref(_layernorm(x, axis=-1), L1_ffn_m1, L1_ffn_m2, L1_ffn_mb, L1_ffn_w1, L1_ffn_w2, L1_ffn_b2)
    x = x + 0.5 * _L2_ffn_ref(_layernorm(x, axis=-1), L2_ffn_router_w, L2_ffn_w1, L2_ffn_b1, L2_ffn_w2, L2_ffn_b2, L2_ffn_gamma, L2_ffn_beta)
    x = x + _L2_attn_ref(_layernorm(x, axis=-1), L2_attn_norm_w, L2_attn_Wq, L2_attn_Wkv, L2_attn_Wo, L2_attn_q_gamma, L2_attn_k_gamma)
    x = x + 0.5 * _L2_ffn_ref(_layernorm(x, axis=-1), L2_ffn_router_w, L2_ffn_w1, L2_ffn_b1, L2_ffn_w2, L2_ffn_b2, L2_ffn_gamma, L2_ffn_beta)
    x = x + 0.5 * _L3_ffn_ref(_layernorm(x, axis=-1), L3_ffn_ln1_weight, L3_ffn_ln1_bias, L3_ffn_ln2_weight, L3_ffn_ln2_bias, L3_ffn_qkv_weight, L3_ffn_proj_weight, L3_ffn_router_weight, L3_ffn_moe_w1, L3_ffn_moe_w2)
    x = x + _L3_attn_ref(_layernorm(x, axis=-1), L3_attn_Wz, L3_attn_bz, L3_attn_Wh, L3_attn_bh, L3_attn_swish_beta, L3_attn_ln_gamma, L3_attn_ln_beta)
    x = x + 0.5 * _L3_ffn_ref(_layernorm(x, axis=-1), L3_ffn_ln1_weight, L3_ffn_ln1_bias, L3_ffn_ln2_weight, L3_ffn_ln2_bias, L3_ffn_qkv_weight, L3_ffn_proj_weight, L3_ffn_router_weight, L3_ffn_moe_w1, L3_ffn_moe_w2)
    return x

_drawn_inputs = setup_inputs


def setup_inputs(seed=0):
    import zlib

    import numpy as np

    out = dict(_drawn_inputs(seed))
    spreads = {'L1_attn_g_qnorm': (1.0, 0.6),
     'L1_attn_g_knorm': (1.0, 0.6),
     'L1_attn_b_gate': (0.0, 2.0),
     'L2_attn_norm_w': (1.0, 0.6),
     'L2_attn_q_gamma': (0.0, 2.0),
     'L2_attn_k_gamma': (0.0, 2.0),
     'L2_ffn_b1': (0.0, 0.8),
     'L2_ffn_b2': (0.0, 0.1),
     'L2_ffn_gamma': (1.0, 0.2),
     'L2_ffn_beta': (0.0, 0.1),
     'L3_attn_bz': (0.0, 0.8),
     'L3_attn_bh': (0.0, 0.278),
     'L3_attn_ln_gamma': (1.0, 0.2),
     'L3_attn_ln_beta': (0.0, 0.322),
     'L3_ffn_ln1_weight': (1.0, 0.6),
     'L3_ffn_ln1_bias': (0.0, 0.8),
     'L3_ffn_ln2_weight': (1.0, 0.6),
     'L3_ffn_ln2_bias': (0.0, 0.8)}
    factors = {'L1_attn_w_gate': 6.279,
     'L1_attn_sink_logit': 24.974,
     'L2_attn_Wq': 8.0,
     'L2_ffn_w1': 3.21,
     'L2_ffn_w2': 2.961,
     'L3_ffn_qkv_weight': 4.69,
     'L3_ffn_proj_weight': 4.546,
     'L3_ffn_router_weight': 8.0,
     'L3_ffn_moe_w1': 8.0,
     'L3_ffn_moe_w2': 8.0}
    for name, (base, spread) in spreads.items():
        noise = np.random.default_rng([zlib.crc32(name.encode()), seed]).standard_normal(out[name].shape)
        drawn = base * np.exp(spread * noise) if base else spread * noise
        out[name] = jnp.asarray(drawn.astype(out[name].dtype))
    for name, factor in factors.items():
        out[name] = (out[name] * factor).astype(out[name].dtype)
    return out
```

```python
import math
from contextlib import ExitStack, contextmanager

import numpy as np

import concourse.bass as bass
from concourse import mybir

FP32 = mybir.dt.float32
BF16 = mybir.dt.bfloat16
U32 = mybir.dt.uint32
ALU = mybir.AluOpType
ACT = mybir.ActivationFunctionType
AX = mybir.AxisListType

P = 128
D = 128
B, S = 2, 1024
TOKENS = B * S
TILES = TOKENS // P
TPB = S // P
CH = 512
CHUNKS = TOKENS // CH
SUB = CH // P
NEG = -1e30
STAGE_SEMAPHORES = 120
START = 1


class Steps:

    def __init__(self, eng, sem):
        self.eng, self.sem, self.n, self.base = eng, sem, 0, 0

    def done(self, instruction):
        instruction.then_inc(self.sem, 1)
        self.n += 1
        self.eng.wait_ge(self.sem, START + self.base + self.n)

    @contextmanager
    def loop(self, count, per_turn):
        before, outer, start = self.n, self.base, self.n
        with self.eng.Fori(0, count) as i:
            self.base, self.n = outer + i * per_turn, before
            yield i
            assert self.n - before == per_turn, f"{self.n - before} steps in a turn, not {per_turn}"
        self.base, self.n = outer, start + count * per_turn


class Stage:

    def __init__(self, nc, ctx, name, cleared):
        self.nc, self.ctx, self.name, self.cleared, self.semaphores = nc, ctx, name, cleared, []

    def sb(self, name, shape, dt=FP32):
        return self.ctx.enter_context(self.nc.sbuf_tensor(self.name + name, shape, dt))

    def bank(self, name, columns=512):
        return self.ctx.enter_context(self.nc.psum_tensor(self.name + name, [P, columns], FP32))

    def sem(self, name):
        self.semaphores.append(self.cleared.pop(0))
        return self.semaphores[-1]

    def sems(self, name, n):
        return [self.sem(f"{name}{i}") for i in range(n)]


class Core:

    def __init__(self, nc, ctx, args):
        self.nc, self.ctx, self.a = nc, ctx, args
        self.x = self.sb("x_tokens", [P, TILES, D])
        self.kept = self.sb("kept_tokens", [P, TILES, D])
        self.xT = self.sb("xT", [P, TOKENS])
        self.ident = self.sb("ident", [P, P])
        self.ident16 = self.sb("ident16", [P, P], BF16)
        self.causal16 = self.sb("causal16", [P, P], BF16)
        self.ones_row = self.sb("ones_row", [1, P])
        self.ones_col = self.sb("ones_col", [P, 1])
        self.w, self.w_sem, self.w_value = {}, {}, {}
        self.mean = self.sb("ln_mean", [P, TILES])
        self.rstd = self.sb("ln_rstd", [P, TILES])
        self.iota8 = self.sb("iota8", [P, TILES, 8])
        self.logits = self.sb("logits", [P, TILES, 8])
        self.gates = self.sb("gates", [P, TILES, 8])
        self.stages = 0
        self.cleared = [self.sem(f"stage_sem{i}") for i in range(STAGE_SEMAPHORES)]
        for semaphore in self.cleared:
            nc.gpsimd.sem_inc(semaphore, START)
        with nc.Block():
            pass
        self.just_cleared = []

    def sb(self, name, shape, dt=FP32, ctx=None):
        return (ctx or self.ctx).enter_context(self.nc.sbuf_tensor(name, shape, dt))

    def sem(self, name, ctx=None):
        return (ctx or self.ctx).enter_context(self.nc.semaphore(name))

    @contextmanager
    def stage(self, tag):
        self.stages += 1
        name = f"{tag}{self.stages}_"
        with ExitStack() as ctx:
            st = Stage(self.nc, ctx, name, self.cleared)
            with self.nc.Block() as st.block:
                yield st
        for semaphore in st.semaphores:
            self.nc.gpsimd.sem_clear(semaphore)
            self.nc.gpsimd.sem_inc(semaphore, START)
        self.cleared += self.just_cleared
        self.just_cleared = st.semaphores

    def place_weights(self, groups, arena):
        loads, at = [], 0
        for key, src in self.a.items():
            group, _, name = key.partition(".")
            if group not in groups:
                continue
            shape = list(src.shape)
            if name.endswith("_rep"):
                shape[0] = P
                src = src.to_broadcast(shape)
            size = math.prod(shape[1:])
            view = arena[0:shape[0], at:at + size]
            at += size
            if len(shape) == 3:
                view = view.rearrange("p (a b) -> p a b", a=shape[1])
            elif len(shape) == 4:
                view = view.rearrange("p (a b c) -> p a b c", a=shape[1], b=shape[2])
            if group not in self.w_sem:
                self.w_sem[group], self.w_value[group] = self.sem(group + "_loaded"), 0
            self.w_value[group] += 16
            self.w[key] = view
            loads.append((view, src, self.w_sem[group]))
        return loads


def load_everything(core, loads):
    nc, a = core.nc, core.a
    with core.stage("load") as st:
        x_loaded = st.sem("x_loaded")
        made = st.sem("constants_made")

        @st.block.sync
        def _(sp):
            sp.dma_start(core.x[:], a["x"].rearrange("b (t p) d -> p (b t) d", p=P)).then_inc(x_loaded, 16)
            for dst, src, sem in loads:
                sp.dma_start(dst, src).then_inc(sem, 16)
            sp.wait_ge(x_loaded, START + 16)

        @st.block.gpsimd
        def _(pool):
            nc.gpsimd.memset(core.ident[:], 0.0)
            nc.gpsimd.memset(core.ident16[:], 0.0)
            nc.gpsimd.memset(core.causal16[:], 0.0)
            nc.gpsimd.memset(core.ones_row[:], 1.0)
            nc.gpsimd.memset(core.ones_col[:], 1.0)
            nc.gpsimd.memset(core.logits[:], -3e38).then_inc(made, 1)
            pool.wait_ge(made, START + 1)
            nc.gpsimd.affine_select(out=core.ident[:], in_=core.ident[:], compare_op=ALU.not_equal, fill=1.0,
                                    base=0, pattern=[[-1, P]], channel_multiplier=1).then_inc(made, 1)
            nc.gpsimd.affine_select(out=core.ident16[:], in_=core.ident16[:], compare_op=ALU.not_equal, fill=1.0,
                                    base=0, pattern=[[-1, P]], channel_multiplier=1).then_inc(made, 1)
            nc.gpsimd.affine_select(out=core.causal16[:], in_=core.causal16[:], compare_op=ALU.is_ge, fill=NEG,
                                    base=0, pattern=[[-1, P]], channel_multiplier=1).then_inc(made, 1)
            nc.gpsimd.iota(core.iota8[:], pattern=[[0, TILES], [1, 8]], base=0, channel_multiplier=0,
                           allow_small_or_imprecise_dtypes=True).then_inc(made, 1)
            pool.wait_ge(made, START + 5)


def load_weights(core, loads):
    with core.stage("load") as st:
        @st.block.sync
        def _(sp):
            for dst, src, sem in loads:
                sp.dma_start(dst, src).then_inc(sem, 16)


def token_statistics(nc, step, src, eps, bn, work, mean, rstd, stats_done, variance_ready, root_ready, rms_eps=None):
    dve = step.eng
    for t in range(TILES):
        nc.vector.bn_stats(bn[:, t, :], src[:, t, :]).then_inc(stats_done, 1)
    dve.wait_ge(stats_done, START + TILES)
    nc.vector.tensor_tensor(work[:, 0, :], bn[:, :, 1], bn[:, :, 4], ALU.add)
    nc.vector.tensor_tensor(work[:, 1, :], bn[:, :, 1], bn[:, :, 4], ALU.subtract)
    step.done(nc.vector.tensor_tensor(work[:, 2, :], bn[:, :, 2], bn[:, :, 5], ALU.add))
    nc.vector.tensor_scalar(mean, work[:, 0, :], 0.5, None, ALU.mult)
    nc.vector.tensor_scalar(work[:, 2, :], work[:, 2, :], 1.0 / D, None, ALU.mult)
    step.done(nc.vector.scalar_tensor_tensor(work[:, 3, :], work[:, 1, :], 0.25, work[:, 1, :],
                                             op0=ALU.mult, op1=ALU.mult))
    nc.vector.scalar_tensor_tensor(work[:, 4, :], work[:, 2, :], eps, work[:, 3, :], op0=ALU.add, op1=ALU.add
                                   ).then_inc(variance_ready, 1)
    if rms_eps is None:
        dve.wait_ge(root_ready, START + 1)
        step.done(nc.vector.reciprocal(rstd, work[:, 5, :]))
        return
    step.done(nc.vector.tensor_tensor(work[:, 3, :], work[:, 2, :], work[:, 3, :], ALU.add))
    step.done(nc.vector.reciprocal(work[:, 0, :], work[:, 4, :]))
    step.done(nc.vector.tensor_tensor(work[:, 0, :], work[:, 0, :], work[:, 3, :], ALU.mult))
    nc.vector.tensor_scalar(work[:, 7, :], work[:, 0, :], rms_eps, None, ALU.add).then_inc(variance_ready, 1)
    dve.wait_ge(root_ready, START + 2)
    step.done(nc.vector.tensor_tensor(work[:, 0, :], work[:, 5, :], work[:, 6, :], ALU.mult))
    step.done(nc.vector.reciprocal(rstd, work[:, 0, :]))


def root_of_variances(nc, act, work, variance_ready, root_ready, rms_eps=None):
    for k in range(1 if rms_eps is None else 2):
        act.wait_ge(variance_ready, START + k + 1)
        nc.scalar.activation(work[:, 5 + k, :], work[:, 7 if k else 4, :], ACT.Sqrt).then_inc(root_ready, 1)


def layer_norm_stats(core, src, eps, tag):
    nc = core.nc
    with core.stage(tag) as st:
        bn = st.sb("bn", [P, TILES, 6])
        work = st.sb("work", [P, 8, TILES])
        stats_done, steps_done = st.sem("stats_done"), st.sem("steps_done")
        variance_ready, root_ready = st.sem("variance_ready"), st.sem("root_ready")

        @st.block.vector
        def _(dve):
            token_statistics(nc, Steps(dve, steps_done), src, eps, bn, work, core.mean[:], core.rstd[:], stats_done,
                             variance_ready, root_ready)

        @st.block.scalar
        def _(act):
            root_of_variances(nc, act, work, variance_ready, root_ready)


def layer_norm_and_transpose(core, src, eps, tag, keep=False, keep_plain=False, gain=None, shift=None,
                             small=None, gain_sem=None, gain_value=0, rms_eps=None):
    nc = core.nc
    with core.stage(tag) as st:
        bn = st.sb("bn", [P, TILES, 6])
        work = st.sb("work", [P, 8, TILES])
        normed = core.kept if keep else st.sb("normed", [P, TILES, D])
        turned = [st.bank(f"turned{s}") for s in range(2)]
        stats_done, steps_done = st.sem("stats_done"), st.sem("steps_done")
        variance_ready, root_ready = st.sem("variance_ready"), st.sem("root_ready")
        normed_ready, turned_ready, stored = st.sem("normed_ready"), st.sem("turned_ready"), st.sem("stored")
        product_ready, product_read = st.sem("product_ready"), st.sem("product_read")
        if small:
            weights, bias, small_out, small_sem, small_value = small
            n = weights.shape[-1]
            per_bank = min(TILES, 1 << (CH // n).bit_length() - 1)
            product = [st.bank(f"product{k}") for k in range(min(4, TILES // per_bank))]

        @st.block.vector
        def _(dve):
            step = Steps(dve, steps_done)
            token_statistics(nc, step, src, eps, bn, work, core.mean[:], core.rstd[:], stats_done, variance_ready,
                             root_ready, rms_eps)
            for t in range(TILES):
                ins = nc.vector.tensor_scalar(normed[:, t, :], src[:, t, :], core.mean[:, t:t + 1],
                                              core.rstd[:, t:t + 1], ALU.subtract, ALU.mult)
                if t % SUB == SUB - 1:
                    ins.then_inc(normed_ready, 1)
            if keep_plain:
                step.done(nc.vector.reciprocal(work[:, 0, :], work[:, 5, :]))
                for t in range(TILES):
                    nc.vector.tensor_scalar(core.kept[:, t, :], src[:, t, :], core.mean[:, t:t + 1],
                                            work[:, 0, t:t + 1], ALU.subtract, ALU.mult)
            if small:
                dve.wait_ge(small_sem, small_value)
                for k in range(TILES // per_bank):
                    dve.wait_ge(product_ready, START + k + 1)
                    columns = product[k % len(product)][:, :per_bank * n].rearrange("p (t n) -> p t n", n=n)
                    into = small_out[:, k * per_bank:(k + 1) * per_bank, 0:n]
                    if bias is None:
                        ins = nc.vector.tensor_copy(into, columns)
                    else:
                        ins = nc.vector.tensor_tensor(into, columns, bias.unsqueeze(1).to_broadcast([P, per_bank, n]),
                                                      ALU.add)
                    ins.then_inc(product_read, 1)

        @st.block.tensor
        def _(pe):
            if small:
                pe.wait_ge(small_sem, small_value)

            def multiply(c):
                pe.wait_ge(stored, START + c + 1)
                for t in range(c * SUB, (c + 1) * SUB):
                    k, i = divmod(t, per_bank)
                    if i == 0 and k >= len(product):
                        pe.wait_ge(product_read, START + k - len(product) + 1)
                    mm = nc.tensor.matmul(product[k % len(product)][:, i * n:(i + 1) * n],
                                          core.xT[:, t * P:(t + 1) * P], weights, start=True, stop=True)
                    if i == per_bank - 1:
                        mm.then_inc(product_ready, 1)

            for c in range(CHUNKS):
                pe.wait_ge(normed_ready, START + c + 1)
                if c >= 2:
                    pe.wait_ge(stored, START + c - 1)
                for i in range(SUB):
                    mm = nc.tensor.transpose(turned[c % 2][:, i * P:(i + 1) * P], normed[:, c * SUB + i, :],
                                             core.ident[:])
                mm.then_inc(turned_ready, 1)
                if small and c >= 1:
                    multiply(c - 1)
            if small:
                multiply(CHUNKS - 1)

        @st.block.scalar
        def _(act):
            root_of_variances(nc, act, work, variance_ready, root_ready, rms_eps)
            if gain_sem is not None:
                act.wait_ge(gain_sem, gain_value)
            for c in range(CHUNKS):
                act.wait_ge(turned_ready, START + c + 1)
                part = core.xT[:, c * CH:(c + 1) * CH]
                if gain is not None:
                    ins = nc.scalar.activation(part, turned[c % 2][:], ACT.Identity, bias=shift, scale=gain)
                else:
                    ins = nc.scalar.activation(part, turned[c % 2][:], ACT.Copy)
                ins.then_inc(stored, 1)


def top2_gates(core, tag, experts, softmax_over_all):
    nc = core.nc
    with core.stage(tag) as st:
        best = st.sb("best", [P, TILES, 8])
        place = st.sb("place", [P, TILES, 8], U32)
        place_f = st.sb("place_f", [P, TILES, 2])
        hot = st.sb("hot", [P, 2, TILES, 8])
        w = st.sb("w", [P, 4, TILES])
        e = st.sb("e", [P, TILES, 8])
        dve_done, to_exp, exp_done = st.sem("dve_done"), st.sem("to_exp"), st.sem("exp_done")
        full = [P, TILES, 8]
        per_token = lambda ap: ap.unsqueeze(2).to_broadcast(full)

        @st.block.vector
        def _(dve):
            step = Steps(dve, dve_done)
            scores = core.logits
            if softmax_over_all:
                step.done(nc.vector.tensor_reduce(w[:, 0, :], core.logits[:], AX.X, ALU.max))
                nc.vector.tensor_tensor(e[:], core.logits[:], per_token(w[:, 0, :]), ALU.subtract).then_inc(to_exp, 1)
                dve.wait_ge(exp_done, START + 1)
                step.done(nc.vector.tensor_reduce(w[:, 1, :], e[:], AX.X, ALU.add))
                step.done(nc.vector.reciprocal(w[:, 2, :], w[:, 1, :]))
                step.done(nc.vector.tensor_tensor(e[:], e[:], per_token(w[:, 2, :]), ALU.mult))
                scores = e
            for t in range(TILES):
                ins = nc.vector.max(best[:, t, :], scores[:, t, :])
            step.done(ins)
            for t in range(TILES):
                ins = nc.vector.max_index(place[:, t, :], best[:, t, :], scores[:, t, :])
            step.done(ins)
            if softmax_over_all:
                nc.vector.tensor_scalar(w[:, 2, :], best[:, :, 0], 0.5, None, ALU.mult)
                nc.vector.tensor_scalar(w[:, 3, :], best[:, :, 1], 0.5, None, ALU.mult)
            else:
                nc.vector.tensor_tensor(w[:, 0, :], best[:, :, 1], best[:, :, 0], ALU.subtract).then_inc(to_exp, 1)
                dve.wait_ge(exp_done, START + 1)
                step.done(nc.vector.tensor_scalar(w[:, 0, :], w[:, 1, :], 1.0, 2.0, ALU.add, ALU.mult))
                step.done(nc.vector.reciprocal(w[:, 2, :], w[:, 0, :]))
                nc.vector.tensor_tensor(w[:, 3, :], w[:, 1, :], w[:, 2, :], ALU.mult)
            step.done(nc.vector.tensor_copy(place_f[:], place[:, :, 0:2]))
            for k in range(2):
                ins = nc.vector.tensor_tensor(hot[:, k], core.iota8[:], per_token(place_f[:, :, k]), ALU.is_equal)
            step.done(ins)
            for k in range(2):
                ins = nc.vector.tensor_tensor(hot[:, k], hot[:, k], per_token(w[:, 2 + k, :]), ALU.mult)
            step.done(ins)
            step.done(nc.vector.tensor_tensor(core.gates[:], hot[:, 0], hot[:, 1], ALU.add))

        @st.block.scalar
        def _(act):
            act.wait_ge(to_exp, START + 1)
            if softmax_over_all:
                nc.scalar.activation(e[:], e[:], ACT.Exp).then_inc(exp_done, 1)
            else:
                nc.scalar.activation(w[:, 1, :], w[:, 0, :], ACT.Exp).then_inc(exp_done, 1)


def experts_ffn(core, tag, experts, hidden, function, w1, w2, weights_sem, weights_value, b1=None, b2=None,
                normed=None):
    nc = core.nc
    blocks = hidden // P
    per_chunk = experts * blocks
    assert per_chunk % 4 == 0 and experts % 2 == 0
    with core.stage(tag) as st:
        hidden_ps = [st.bank(f"hidden_ps{i}") for i in range(4)]
        out_ps = [st.bank(f"out_ps{i}") for i in range(2)]
        hT = [st.sb(f"hT{i}", [P, blocks, CH]) for i in range(2)]
        hidden_ready, hidden_active = st.sem("hidden_ready"), st.sem("hidden_active")
        out_ready, out_read = st.sem("out_ready"), st.sem("out_read")
        added = st.sem("added")

        @st.block.tensor
        def _(pe):
            pe.wait_ge(weights_sem, weights_value)
            with pe.Fori(0, CHUNKS) as c:
                def up(e):
                    for f in range(blocks):
                        k = e * blocks + f
                        pe.wait_ge(hidden_active, START + c * per_chunk + (k - 3 if k >= 4 else 0))
                        nc.tensor.matmul(hidden_ps[k % 4][:], w1[:, e, f * P:(f + 1) * P],
                                         core.xT[:, bass.ds(c * CH, CH)], start=True, stop=True
                                         ).then_inc(hidden_ready, 1)

                def down(e):
                    pe.wait_ge(hidden_active, START + c * per_chunk + (e + 1) * blocks)
                    pe.wait_ge(out_read, START + c * experts + (e - 1 if e >= 2 else 0))
                    for sub in range(SUB):
                        for f in range(blocks):
                            mm = nc.tensor.matmul(out_ps[e % 2][:, sub * P:(sub + 1) * P],
                                                  hT[e % 2][:, f, sub * P:(sub + 1) * P], w2[:, e, f, :],
                                                  start=f == 0, stop=f == blocks - 1)
                    mm.then_inc(out_ready, 1)

                up(0)
                for e in range(experts):
                    if e + 1 < experts:
                        up(e + 1)
                    down(e)

        if normed is None:
            plain_consumer(core, st, experts, out_ps, out_ready, out_read, added, b2, weights_sem, weights_value)
        else:
            normed_consumer(core, st, experts, out_ps, out_ready, out_read, added, b2, weights_sem,
                            weights_value, *normed)

        @st.block.scalar
        def _(act):
            if b1 is not None:
                act.wait_ge(weights_sem, weights_value)
            with act.Fori(0, CHUNKS) as c:
                for e in range(experts):
                    act.wait_ge(out_ready, START + c * experts + (e - 1 if e >= 2 else 0))
                    for f in range(blocks):
                        k = e * blocks + f
                        act.wait_ge(hidden_ready, START + c * per_chunk + k + 1)
                        nc.scalar.activation(hT[e % 2][:, f, :], hidden_ps[k % 4][:], function,
                                             bias=0.0 if b1 is None else b1[:, e, f:f + 1]
                                             ).then_inc(hidden_active, 1)
                if normed is not None:
                    variance, variance_ready, root_ready = core.root_of_variance
                    act.wait_ge(variance_ready, START + c + 1)
                    nc.scalar.activation(variance[:, 5, :], variance[:, 4, :], ACT.Sqrt).then_inc(root_ready, 1)


def plain_consumer(core, st, experts, out_ps, out_ready, out_read, added, b2, weights_sem, weights_value):
    nc = core.nc
    biased = [st.sb(f"biased{i}", [P, SUB, D]) for i in range(2)]

    @st.block.vector
    def _(dve):
        if b2 is not None:
            dve.wait_ge(weights_sem, weights_value)
        with dve.Fori(0, CHUNKS) as c:
            for e in range(experts):
                dve.wait_ge(out_ready, START + c * experts + e + 1)
                out = out_ps[e % 2][:].rearrange("p (s d) -> p s d", s=SUB)
                if b2 is not None:
                    nc.vector.tensor_tensor(biased[e % 2][:], out, b2[:, e, :].unsqueeze(1).to_broadcast([P, SUB, D]),
                                            ALU.add).then_inc(out_read, 1)
                    dve.wait_ge(out_read, START + c * experts + e + 1)
                    out = biased[e % 2]
                dve.wait_ge(added if b2 is not None else out_read, START + c * experts + e)
                for sub in range(SUB):
                    tile = c * SUB + sub
                    last = nc.vector.scalar_tensor_tensor(core.x[:, bass.ds(tile, 1), :], out[:, sub:sub + 1, :],
                                                          core.gates[:, bass.ds(tile, 1), e],
                                                          core.x[:, bass.ds(tile, 1), :], op0=ALU.mult, op1=ALU.add)
                last.then_inc(added if b2 is not None else out_read, 1)


def normed_consumer(core, st, experts, out_ps, out_ready, out_read, added, b2, weights_sem, weights_value,
                    gamma, eps):
    nc = core.nc
    n = experts * SUB
    with_bias = [st.sb(f"with_bias{i}", [P, SUB, D]) for i in range(2)]
    result = st.sb("result", [P, experts, SUB, D])
    scaled = [st.sb(f"scaled{i}", [P, SUB, D]) for i in range(2)]
    bn = st.sb("bn", [P, n, 6])
    w = st.sb("w", [P, 8, n])
    bias_added, passed, dve_done = st.sem("bias_added"), st.sem("passed"), st.sem("dve_done")
    variance_ready, root_ready = st.sem("variance_ready"), st.sem("root_ready")
    core.root_of_variance = (w, variance_ready, root_ready)

    @st.block.gpsimd
    def _(pool):
        pool.wait_ge(weights_sem, weights_value)
        with pool.Fori(0, CHUNKS) as c:
            for e in range(experts):
                pool.wait_ge(out_read, START + c * experts + (e - 1 if e >= 2 else 0))
                pool.sem_inc(passed, 1)
                nc.gpsimd.tensor_tensor(with_bias[e % 2][:], core.kept[:, bass.ds(c * SUB, SUB), :],
                                        b2[:, e, :].unsqueeze(1).to_broadcast([P, SUB, D]), ALU.add
                                        ).then_inc(bias_added, 1)

    @st.block.vector
    def _(dve):
        step = Steps(dve, dve_done)
        dve.wait_ge(weights_sem, weights_value)
        with step.loop(CHUNKS, 5 + 2 * experts) as c:
            for e in range(experts):
                dve.wait_ge(out_ready, START + c * experts + e + 1)
                dve.wait_ge(bias_added, START + c * experts + e + 1)
                nc.vector.tensor_tensor(result[:, e], out_ps[e % 2][:].rearrange("p (s d) -> p s d", s=SUB),
                                        with_bias[e % 2][:], ALU.add).then_inc(out_read, 1)
                dve.wait_ge(out_read, START + c * experts + e + 1)
                for sub in range(SUB):
                    ins = nc.vector.bn_stats(bn[:, e * SUB + sub, :], result[:, e, sub, :])
            step.done(ins)
            nc.vector.tensor_tensor(w[:, 1, :], bn[:, :, 1], bn[:, :, 4], ALU.add)
            nc.vector.tensor_tensor(w[:, 2, :], bn[:, :, 1], bn[:, :, 4], ALU.subtract)
            step.done(nc.vector.tensor_tensor(w[:, 3, :], bn[:, :, 2], bn[:, :, 5], ALU.add))
            nc.vector.tensor_scalar(w[:, 0, :], w[:, 1, :], 0.5, None, ALU.mult)
            nc.vector.tensor_scalar(w[:, 4, :], w[:, 3, :], 1.0 / D, eps, ALU.mult, ALU.add)
            step.done(nc.vector.scalar_tensor_tensor(w[:, 5, :], w[:, 2, :], 0.25, w[:, 2, :],
                                                     op0=ALU.mult, op1=ALU.mult))
            nc.vector.tensor_tensor(w[:, 4, :], w[:, 4, :], w[:, 5, :], ALU.add).then_inc(variance_ready, 1)
            dve.wait_ge(root_ready, START + c + 1)
            step.done(nc.vector.reciprocal(w[:, 6, :], w[:, 5, :]))
            step.done(nc.vector.tensor_tensor(
                w[:, 7, :].rearrange("p (e s) -> p e s", s=SUB), w[:, 6, :].rearrange("p (e s) -> p e s", s=SUB),
                core.gates[:, bass.ds(c * SUB, SUB), 0:experts].rearrange("p s e -> p e s"), ALU.mult))
            for e in range(experts):
                for sub in range(SUB):
                    k = e * SUB + sub
                    ins = nc.vector.tensor_scalar(scaled[e % 2][:, sub, :], result[:, e, sub, :], w[:, 0, k:k + 1],
                                                  w[:, 7, k:k + 1], ALU.subtract, ALU.mult)
                step.done(ins)
                step.done(nc.vector.tensor_tensor(scaled[e % 2][:], scaled[e % 2][:],
                                                  gamma[:, e, :].unsqueeze(1).to_broadcast([P, SUB, D]), ALU.mult))
                nc.vector.tensor_tensor(core.x[:, bass.ds(c * SUB, SUB), :], core.x[:, bass.ds(c * SUB, SUB), :],
                                        scaled[e % 2][:], ALU.add).then_inc(added, 1)


def add_gated_rows(core, tag, rows, weights_sem, weights_value):
    nc = core.nc
    with core.stage(tag) as st:
        gate = [st.sb(f"gate{s}", [P, 8]) for s in range(2)]
        gateT = [st.sb(f"gateT{s}", [8, P]) for s in range(2)]
        turned = [st.bank(f"turned{s}") for s in range(2)]
        product = [st.bank(f"product{s}") for s in range(2)]
        gate_ready, turned_ready = st.sems("gate_ready", 2), st.sems("turned_ready", 2)
        gateT_ready, product_ready = st.sems("gateT_ready", 2), st.sems("product_ready", 2)
        added = st.sems("added", 2)

        @st.block.gpsimd
        def _(pool):
            with pool.Fori(0, TILES // 2) as u:
                for s in range(2):
                    pool.wait_ge(turned_ready[s], START + u)
                    nc.gpsimd.tensor_copy(gate[s][:], core.gates[:, 2 * u + s, :]).then_inc(gate_ready[s], 1)

        @st.block.tensor
        def _(pe):
            pe.wait_ge(weights_sem, weights_value)
            with pe.Fori(0, TILES // 2) as u:
                for s in range(2):
                    pe.wait_ge(gate_ready[s], START + u + 1)
                    pe.wait_ge(gateT_ready[s], START + u)
                    nc.tensor.transpose(turned[s][0:8, :P], gate[s][:], core.ident[:]).then_inc(turned_ready[s], 1)
                for s in range(2):
                    pe.wait_ge(gateT_ready[s], START + u + 1)
                    pe.wait_ge(added[s], START + u)
                    nc.tensor.matmul(product[s][:, :D], gateT[s][:], rows, start=True, stop=True
                                     ).then_inc(product_ready[s], 1)

        @st.block.vector
        def _(dve):
            with dve.Fori(0, TILES // 2) as u:
                for s in range(2):
                    dve.wait_ge(turned_ready[s], START + u + 1)
                    dve.wait_ge(product_ready[s], START + u)
                    nc.vector.tensor_copy(gateT[s][:], turned[s][0:8, :P]).then_inc(gateT_ready[s], 1)
                for s in range(2):
                    dve.wait_ge(product_ready[s], START + u + 1)
                    x = core.x[:, 2 * u + s, :]
                    nc.vector.tensor_tensor(x, product[s][:, :D], x, ALU.add).then_inc(added[s], 1)


def project_tokens(core, tag, src, tiles, weights, weights_sem, weights_value, out_tiles):
    nc = core.nc
    n = weights.shape[1]
    banks, groups = tiles * n // 4, tiles // SUB
    with core.stage(tag) as st:
        turned_sb = [st.sb(f"turned_sb{i}", [P, 4, P]) for i in range(4)]
        turned = [st.bank(f"turned{i}") for i in range(4)]
        product = [st.bank(f"product{i}") for i in range(2)]
        turned_ready, stored = st.sem("turned_ready"), st.sems("stored", 2)
        used, added = st.sem("used"), st.sem("added")

        def store(eng, b):
            eng.wait_ge(turned_ready, START + b + 1)
            if b >= 4:
                eng.wait_ge(used, START + b - 3)
            into, bank = turned_sb[b % 4][:].rearrange("p k d -> p (k d)"), turned[b % 4][:]
            if b % 2 == 0:
                nc.scalar.activation(into, bank, ACT.Copy).then_inc(stored[0], 1)
            else:
                nc.vector.tensor_copy(into, bank).then_inc(stored[1], 1)

        @st.block.tensor
        def _(pe):
            pe.wait_ge(weights_sem, weights_value)

            def multiply(b):
                pe.wait_ge(stored[b % 2], START + b // 2 + 1)
                for i in range(4):
                    t, k = divmod(4 * b + i, n)
                    if k == 0 and t % SUB == 0 and t // SUB >= 2:
                        pe.wait_ge(added, START + t // SUB - 1)
                    mm = nc.tensor.matmul(product[t // SUB % 2][:, t % SUB * D:(t % SUB + 1) * D],
                                          turned_sb[b % 4][:, i, :], weights[:, k, :], start=k == 0, stop=k == n - 1)
                mm.then_inc(used, 1)

            for b in range(banks):
                if b >= 4:
                    pe.wait_ge(stored[b % 2], START + b // 2 - 1)
                for i in range(4):
                    t, k = divmod(4 * b + i, n)
                    mm = nc.tensor.transpose(turned[b % 4][:, i * P:(i + 1) * P], src[:, t, k * P:(k + 1) * P],
                                             core.ident[:])
                mm.then_inc(turned_ready, 1)
                if b >= 1:
                    multiply(b - 1)
            multiply(banks - 1)

        @st.block.scalar
        def _(act):
            for b in range(0, banks, 2):
                store(act, b)

        @st.block.vector
        def _(dve):
            def add(g):
                dve.wait_ge(used, START + (g + 1) * n)
                out = out_tiles(g * SUB, (g + 1) * SUB)
                nc.vector.tensor_tensor(out, product[g % 2][:].rearrange("p (t d) -> p t d", t=SUB), out, ALU.add
                                        ).then_inc(added, 1)

            done = 0
            for b in range(1, banks, 2):
                store(dve, b)
                if b >= (done + 1) * n + 1:
                    add(done)
                    done += 1
            for g in range(done, groups):
                add(g)


def l0_ffn(core):
    w, sem, value = core.w, core.w_sem["l0_ffn"], core.w_value["l0_ffn"]
    layer_norm_and_transpose(core, core.x, 1e-5, "norm",
                            small=(w["l0_ffn.wg"], w["l0_ffn.bg_rep"], core.logits, sem, value))
    top2_gates(core, "gates", 6, softmax_over_all=False)
    experts_ffn(core, "ffn", 6, 256, ACT.Gelu, w["l0_ffn.w1"], w["l0_ffn.w2"], sem, value,
                b1=w["l0_ffn.b1"], b2=w["l0_ffn.b2_rep"])


def l0_attn(core):
    w, sem, value = core.w, core.w_sem["l0_attn"], core.w_value["l0_attn"]
    heads, hd = 16, 64
    layer_norm_and_transpose(core, core.x, 1e-5, "norm")
    for b in range(B):
        with ExitStack() as ctx:
            mixed = core.sb(f"mixed{core.stages}", [P, TPB, heads * hd], ctx=ctx)
            latent_attention(core, b, mixed, heads, hd)
            project_tokens(core, "wo", mixed, TPB, w["l0_attn.wo"], sem, value,
                           lambda t, end: core.x[:, b * TPB + t:b * TPB + end, :])


def latent_attention(core, b, mixed, heads, hd):
    nc, w, sem, value = core.nc, core.w, core.w_sem["l0_attn"], core.w_value["l0_attn"]
    halves = S // CH
    with core.stage("l0attn") as st:
        latT = st.sb("latT", [hd, S])
        wq = [st.sb(f"wq{i}", [D, 2 * hd]) for i in range(2)]
        wk = [st.sb(f"wk{i}", [hd, 2 * hd]) for i in range(2)]
        qT = [st.sb(f"qT{i}", [P, S]) for i in range(2)]
        kT = [st.sb(f"kT{i}", [P, S]) for i in range(2)]
        k_parts = core.kept[:].rearrange("p t d -> p (t d)")[:, 0:S]
        v = [st.sb(f"v{i}", [P, TPB, hd]) for i in range(2)]
        probs = [st.sb(f"probs{i}", [P, S]) for i in range(2)]
        probsT = [st.sb(f"probsT{i}", [P, TPB, P]) for i in range(2)]
        neg_max = st.sb("neg_max", [P, 4])
        total = st.sb("total", [P, 4])
        inverse = st.sb("inverse", [P, 4])
        scores_ps = [st.bank(f"scores_ps{i}", S) for i in range(2)]
        side_ps, out_ps = st.bank("side_ps"), st.bank("out_ps")
        turned_ps = [st.bank(f"turned_ps{i}") for i in range(2)]
        loaded = st.sems("loaded", 2)
        lat_ready, lat_stored = st.sem("lat_ready"), st.sem("lat_stored")
        side_ready, side_read = st.sem("side_ready"), st.sem("side_read")
        scores_ready, max_ready, probs_ready = st.sem("scores_ready"), st.sem("max_ready"), st.sem("probs_ready")
        turned, stored0, stored1 = st.sem("turned"), st.sem("stored0"), st.sem("stored1")
        out_ready, inverted, out_read, passed = (st.sem("out_ready"), st.sem("inverted"), st.sem("out_read"),
                                                 st.sem("passed"))
        side_steps = 7
        at_unit = [[0], [1], [2], [3], [4], [5, 6], [], []]
        second_before = [max(0, i - 4) for i in range(TPB + 1)]
        seconds = second_before[TPB]
        banks_before = [i + second_before[i] for i in range(TPB + 1)]
        banks = banks_before[TPB]

        def bank_count(head, i):
            return head * banks + (banks_before[i] if i <= TPB else banks + banks_before[i - TPB])

        assert banks % 2 == 0

        @st.block.sync
        def _(sp):
            for h in range(2):
                sp.dma_start(wq[h][:], core.a["stream_l0.wq"][h]).then_inc(loaded[h], 16)
                sp.dma_start(wk[h][:], core.a["stream_l0.wk"][h]).then_inc(loaded[h], 16)
            with sp.Fori(0, heads // 2) as u:
                for s in range(2):
                    head = 2 * u + s
                    sp.wait_ge(side_ready, START + side_steps * (head + 1))
                    for dst, name in ((wq, "wq"), (wk, "wk")):
                        src = core.a[f"stream_l0.{name}"][bass.ds(head + 2, 1)].rearrange("h k c -> (h k) c")
                        sp.dma_start(dst[s][:], src).then_inc(loaded[s], 16)
            for s in range(2):
                sp.wait_ge(loaded[s], START + 32 * (heads // 2 + 1))

        @st.block.tensor
        def _(pe):
            pe.wait_ge(core.w_sem["l0_attn"], value)
            for half in range(halves):
                pe.wait_ge(lat_stored, START + half)
                nc.tensor.matmul(side_ps[0:hd, :], w["l0_attn.w_down"], core.xT[:, b * S + half * CH:b * S + (half + 1) * CH],
                                 start=True, stop=True).then_inc(lat_ready, 1)
            pe.wait_ge(lat_stored, START + halves)

            def side(slot, k, number, head, weights):
                half = slice(k % 2 * CH, (k % 2 + 1) * CH)
                if k == 0:
                    pe.wait_ge(loaded[slot], START + weights)
                pe.wait_ge(side_read, START + number)
                pe.sem_inc(passed, 1)
                if k < 2:
                    mm = nc.tensor.matmul(side_ps[:], wq[slot][:], core.xT[:, b * S + half.start:b * S + half.stop],
                                          start=True, stop=True)
                elif k < 4:
                    mm = nc.tensor.matmul(side_ps[:], wk[slot][:], latT[:, half], start=True, stop=True)
                elif k < 6:
                    mm = nc.tensor.matmul(side_ps[:], w["l0_attn.add_halves"], k_parts[:, half], start=True, stop=True)
                else:
                    for t in range(TPB):
                        mm = nc.tensor.matmul(side_ps[:, t * hd:(t + 1) * hd], latT[:, t * P:(t + 1) * P],
                                              w["l0_attn.w_v"][:, bass.ds(head * hd, hd)], start=True, stop=True)
                mm.then_inc(side_ready, 1)

            def scores(slot, i):
                keys = (i + 1) * P
                for at in range(0, keys, CH):
                    end = min(keys, at + CH)
                    mm = nc.tensor.matmul(scores_ps[i % 2][:, at:end], qT[slot][:, i * P:(i + 1) * P],
                                          kT[slot][:, at:end], start=True, stop=end < keys)
                nc.tensor.matmul(scores_ps[i % 2][:, i * P:(i + 1) * P], core.ident16[:], core.causal16[:],
                                 start=False, stop=True).then_inc(scores_ready, 1)

            for k in range(side_steps):
                side(0, k, k, 0, 32)
            pe.wait_ge(side_read, START + side_steps)
            scores(0, 0)
            scores(0, 1)
            with pe.Fori(0, heads // 2) as u:
                for s in range(2):
                    head = 2 * u + s
                    for i in range(TPB):
                        unit = head * TPB + i
                        pe.wait_ge(probs_ready, START + unit + 1)
                        for g, at in enumerate(range(0, i + 1, 4)):
                            before = banks_before[i] + g
                            if g == 1:
                                pe.wait_ge(stored0, START + unit)
                                pe.wait_ge(stored1, START + head * seconds + second_before[i])
                            else:
                                pe.wait_ge(stored0, START + unit)
                                pe.wait_ge(stored1, START + head * seconds + second_before[i])
                            for j in range(at, min(at + 4, i + 1)):
                                mm = nc.tensor.transpose(turned_ps[before % 2][:, (j - at) * P:(j - at + 1) * P],
                                                         probs[i % 2][:, j * P:(j + 1) * P], core.ident[:])
                            mm.then_inc(turned, 1)
                        if i < TPB - 2:
                            scores(s, i + 2)
                        else:
                            if i == TPB - 2:
                                pe.wait_ge(side_read, START + (head + 2) * side_steps)
                            scores(1 - s, i + 2 - TPB)
                        for k in at_unit[i]:
                            side(1 - s, k, side_steps * (head + 1) + k, head + 1, 32 * (u + 1 + s))
                        pe.wait_ge(stored0, START + unit + 1)
                        pe.wait_ge(out_read, START + unit)
                        for j in range(i + 1):
                            if j == 4:
                                pe.wait_ge(stored1, START + head * seconds + second_before[i] + 1)
                            mm = nc.tensor.matmul(out_ps[:, :hd], probsT[i % 2][:, j, :], v[s][:, j, :], start=j == 0,
                                                  stop=j == i)
                        mm.then_inc(out_ready, 1)

        @st.block.scalar
        def _(act):
            for half in range(halves):
                act.wait_ge(lat_ready, START + half + 1)
                nc.scalar.activation(latT[:, half * CH:(half + 1) * CH], side_ps[0:hd, :], ACT.Copy
                                     ).then_inc(lat_stored, 1)

            def exponentials(i, unit):
                keys = (i + 1) * P
                act.wait_ge(max_ready, START + unit + 1)
                nc.scalar.activation(probs[i % 2][:, 0:keys], scores_ps[i % 2][:, 0:keys], ACT.Exp,
                                     bias=neg_max[:, i % 4:i % 4 + 1], accum_out=total[:, i % 4:i % 4 + 1]
                                     ).then_inc(probs_ready, 1)

            exponentials(0, 0)
            with act.Fori(0, heads // 2) as u:
                for s in range(2):
                    head = 2 * u + s
                    for i in range(TPB):
                        unit = head * TPB + i
                        act.wait_ge(turned, START + head * banks + banks_before[i])
                        act.wait_ge(out_read, START + unit - 2 if s or i >= 2 else 2 * u * TPB)
                        exponentials((i + 1) % TPB, unit + 1)
                        act.wait_ge(turned, START + head * banks + banks_before[i] + 1)
                        act.wait_ge(out_ready, START + unit - 1 if s or i >= 1 else 2 * u * TPB)
                        last = min(4, i + 1)
                        nc.scalar.activation(probsT[i % 2][:, 0:last, :].rearrange("p j q -> p (j q)"),
                                             turned_ps[banks_before[i] % 2][:, 0:last * P], ACT.Copy).then_inc(stored0, 1)

        @st.block.vector
        def _(dve):
            dve.wait_ge(core.w_sem["l0_attn"], value)

            def read_side(slot, k, number):
                half = slice(k % 2 * CH, (k % 2 + 1) * CH)
                dve.wait_ge(side_ready, START + number + 1)
                if k < 2:
                    ins = nc.vector.scalar_tensor_tensor(qT[slot][:, half], side_ps[:], hd ** -0.5,
                                                         w["l0_attn.rope"][:, half], op0=ALU.mult, op1=ALU.mult)
                elif k < 4:
                    ins = nc.vector.tensor_tensor(k_parts[:, half], side_ps[:], w["l0_attn.rope"][:, half], ALU.mult)
                elif k < 6:
                    ins = nc.vector.tensor_copy(kT[slot][:, half], side_ps[:])
                else:
                    ins = nc.vector.tensor_copy(v[slot][:].rearrange("p t d -> p (t d)"), side_ps[:])
                ins.then_inc(side_read, 1)

            def maximum(i, unit):
                dve.wait_ge(scores_ready, START + unit + 1)
                nc.vector.tensor_reduce(neg_max[:, i % 4:i % 4 + 1], scores_ps[i % 2][:, 0:(i + 1) * P], AX.X, ALU.max,
                                        negate=True).then_inc(max_ready, 1)

            for k in range(side_steps):
                read_side(0, k, k)
            maximum(0, 0)
            maximum(1, 1)
            with dve.Fori(0, heads // 2) as u:
                for s in range(2):
                    head = 2 * u + s
                    for i in range(TPB):
                        unit = head * TPB + i
                        maximum((i + 2) % TPB, unit + 2)
                        for k in at_unit[i]:
                            read_side(1 - s, k, side_steps * (head + 1) + k)
                        if i >= 4:
                            dve.wait_ge(turned, START + head * banks + banks_before[i] + 2)
                            dve.wait_ge(out_ready, START + unit - 1)
                            nc.vector.tensor_copy(probsT[i % 2][:, 4:i + 1, :].rearrange("p j q -> p (j q)"),
                                                  turned_ps[(banks_before[i] + 1) % 2][:, 0:(i - 3) * P]
                                                  ).then_inc(stored1, 1)
                        dve.wait_ge(probs_ready, START + unit + 1)
                        nc.vector.reciprocal(inverse[:, i % 4:i % 4 + 1], total[:, i % 4:i % 4 + 1]).then_inc(inverted, 1)
                        dve.wait_ge(inverted, START + unit + 1)
                        dve.wait_ge(out_ready, START + unit + 1)
                        nc.vector.tensor_scalar(mixed[:, i, bass.ds(head * hd, hd)], out_ps[:, :hd],
                                                inverse[:, i % 4:i % 4 + 1], None, ALU.mult).then_inc(out_read, 1)


def l1_ffn(core):
    nc, w, sem, value = core.nc, core.w, core.w_sem["l1_ffn"], core.w_value["l1_ffn"]
    layer_norm_stats(core, core.x, 1e-5, "stats")
    groups, width = 8, 64
    with core.stage("maskffn") as st:
        normed = [st.sb(f"normed{s}", [P, D]) for s in range(2)]
        xt = [st.sb(f"xt{s}", [P, P]) for s in range(2)]
        low = [st.sb(f"low{s}", [width + 1, P]) for s in range(2)]
        top = [st.sb(f"top{s}", [P, groups]) for s in range(2)]
        hot = [st.sb(f"hot{s}", [P, groups, width]) for s in range(2)]
        kept = [st.sb(f"kept{s}", [P, groups * width]) for s in range(2)]
        keptT = [st.sb(f"keptT{s}", [P, 4, P]) for s in range(2)]
        x_bias = [st.sb(f"x_bias{s}", [P, D]) for s in range(2)]
        half_b2 = st.sb("half_b2", [P, D])
        small_ps = [st.bank(f"small_ps{s}") for s in range(2)]
        logits_ps = [st.bank(f"logits_ps{s}") for s in range(2)]
        mid_ps = [st.bank(f"mid_ps{s}") for s in range(2)]
        keptT_ps = [st.bank(f"keptT_ps{s}") for s in range(2)]
        set_up, half_ready = st.sem("set_up"), st.sem("half_ready")
        normed_ready, turned_ready = st.sems("normed_ready", 2), st.sems("turned_ready", 2)
        xt_ready, low_ps_ready, low_ready = st.sems("xt_ready", 2), st.sems("low_ps_ready", 2), st.sems("low_ready", 2)
        mid_ready, top_ready = st.sems("mid_ready", 2), st.sems("top_ready", 2)
        hot_ready, kept_ready = st.sems("hot_ready", 2), st.sems("kept_ready", 2)
        keptT_ps_ready, keptT_ready = st.sems("keptT_ps_ready", 2), st.sems("keptT_ready", 2)
        result_ready, x_done, bias_ready = st.sems("result_ready", 2), st.sems("x_done", 2), st.sems("bias_ready", 2)

        @st.block.gpsimd
        def _(pool):
            nc.gpsimd.memset(low[0][width:width + 1, :], 1.0)
            nc.gpsimd.memset(low[1][width:width + 1, :], 1.0).then_inc(set_up, 1)
            pool.wait_ge(set_up, START + 1)
            pool.wait_ge(core.w_sem["l1_ffn"], value)
            nc.gpsimd.tensor_scalar(half_b2[:], w["l1_ffn.b2_rep"][:, :], 0.5, None, ALU.mult).then_inc(half_ready, 1)
            pool.wait_ge(half_ready, START + 1)
            with pool.Fori(0, TILES // 2) as u:
                for s in range(2):
                    pool.wait_ge(x_done[s], START + u)
                    pool.wait_ge(half_ready, START + 1)
                    nc.gpsimd.tensor_tensor(x_bias[s][:], core.x[:, 2 * u + s, :], half_b2[:], ALU.add
                                            ).then_inc(bias_ready[s], 1)

        @st.block.vector
        def _(dve):
            with dve.Fori(0, TILES // 2) as u:
                for s in range(2):
                    t = 2 * u + s
                    dve.wait_ge(turned_ready[s], START + u)
                    nc.vector.tensor_scalar(normed[s][:], core.x[:, t, :], core.mean[:, bass.ds(t, 1)],
                                            core.rstd[:, bass.ds(t, 1)], ALU.subtract, ALU.mult
                                            ).then_inc(normed_ready[s], 1)
                for s in range(2):
                    dve.wait_ge(mid_ready[s], START + u + 1)
                    logits = logits_ps[s][:].rearrange("p (g w) -> p g w", g=groups)
                    nc.vector.tensor_reduce(top[s][:], logits, AX.X, ALU.max).then_inc(top_ready[s], 1)
                    dve.wait_ge(top_ready[s], START + u + 1)
                    nc.vector.tensor_tensor(hot[s][:], logits, top[s][:].unsqueeze(2).to_broadcast([P, groups, width]),
                                            ALU.is_equal).then_inc(hot_ready[s], 1)
                    dve.wait_ge(hot_ready[s], START + u + 1)
                    dve.wait_ge(keptT_ps_ready[s], START + u)
                    nc.vector.scalar_tensor_tensor(kept[s][:], mid_ps[s][:], 0.0,
                                                   hot[s][:].rearrange("p g w -> p (g w)"), op0=ALU.max, op1=ALU.mult
                                                   ).then_inc(kept_ready[s], 1)
                for s in range(2):
                    dve.wait_ge(result_ready[s], START + u + 1)
                    dve.wait_ge(bias_ready[s], START + u + 1)
                    nc.vector.scalar_tensor_tensor(core.x[:, 2 * u + s, :], small_ps[s][:, 256:384], 0.5, x_bias[s][:],
                                                   op0=ALU.mult, op1=ALU.add).then_inc(x_done[s], 1)

        @st.block.tensor
        def _(pe):
            pe.wait_ge(core.w_sem["l1_ffn"], value)
            pe.wait_ge(set_up, START + 1)
            with pe.Fori(0, TILES // 2) as u:
                for s in range(2):
                    pe.wait_ge(normed_ready[s], START + u + 1)
                    pe.wait_ge(x_done[s], START + u)
                    nc.tensor.transpose(small_ps[s][:, 0:P], normed[s][:], core.ident[:]).then_inc(turned_ready[s], 1)
                for s in range(2):
                    pe.wait_ge(xt_ready[s], START + u + 1)
                    nc.tensor.matmul(small_ps[s][0:width, P:2 * P], w["l1_ffn.m1"], xt[s][:], start=True, stop=True
                                     ).then_inc(low_ps_ready[s], 1)
                for s in range(2):
                    pe.wait_ge(low_ready[s], START + u + 1)
                    pe.wait_ge(kept_ready[s], START + u)
                    nc.tensor.matmul(logits_ps[s][:], low[s][:], w["l1_ffn.m2"], start=True, stop=True)
                    nc.tensor.matmul(mid_ps[s][:], xt[s][:], w["l1_ffn.w1"], start=True, stop=True
                                     ).then_inc(mid_ready[s], 1)
                for s in range(2):
                    pe.wait_ge(kept_ready[s], START + u + 1)
                    pe.wait_ge(keptT_ready[s], START + u)
                    for k in range(4):
                        mm = nc.tensor.transpose(keptT_ps[s][:, k * P:(k + 1) * P], kept[s][:, k * P:(k + 1) * P],
                                                 core.ident[:])
                    mm.then_inc(keptT_ps_ready[s], 1)
                for s in range(2):
                    pe.wait_ge(keptT_ready[s], START + u + 1)
                    for k in range(4):
                        mm = nc.tensor.matmul(small_ps[s][:, 256:384], keptT[s][:, k, :], w["l1_ffn.w2"][:, k, :],
                                              start=k == 0, stop=k == 3)
                    mm.then_inc(result_ready[s], 1)

        @st.block.scalar
        def _(act):
            with act.Fori(0, TILES // 2) as u:
                for s in range(2):
                    act.wait_ge(turned_ready[s], START + u + 1)
                    act.wait_ge(mid_ready[s], START + u)
                    nc.scalar.activation(xt[s][:], small_ps[s][:, 0:P], ACT.Copy).then_inc(xt_ready[s], 1)
                for s in range(2):
                    act.wait_ge(low_ps_ready[s], START + u + 1)
                    nc.scalar.activation(low[s][0:width, :], small_ps[s][0:width, P:2 * P], ACT.Copy
                                         ).then_inc(low_ready[s], 1)
                for s in range(2):
                    act.wait_ge(keptT_ps_ready[s], START + u + 1)
                    act.wait_ge(result_ready[s], START + u)
                    nc.scalar.activation(keptT[s][:].rearrange("p k d -> p (k d)"), keptT_ps[s][:], ACT.Copy
                                         ).then_inc(keptT_ready[s], 1)


def l1_attn(core):
    w, sem, value = core.w, core.w_sem["l1_attn"], core.w_value["l1_attn"]
    heads, hd = 8, 64
    layer_norm_and_transpose(core, core.x, 1e-5, "norm")
    for b in range(B):
        with ExitStack() as ctx:
            mixed = core.sb(f"mixed{core.stages}", [P, TPB, heads * hd], ctx=ctx)
            grouped = core.sb(f"grouped{core.stages}", [P, TPB, D], ctx=ctx)
            sparse_attention(core, b, mixed, grouped, heads, hd)
            project_tokens(core, "groups", mixed, TPB, w["l1_attn.w_group"], sem, value, lambda t, end: grouped[:, t:end, :])
            project_tokens(core, "w_out", grouped, TPB, w["l1_attn.w_out"].unsqueeze(1), sem, value,
                           lambda t, end: core.x[:, b * TPB + t:b * TPB + end, :])


SIDE_CHAIN = 12


def sparse_attention(core, b, mixed, grouped, heads, hd):
    nc, w, sem, value = core.nc, core.w, core.w_sem["l1_attn"], core.w_value["l1_attn"]
    halves, blocks = S // CH, 32
    qk_heads = heads + 1
    with core.stage("l1attn") as st:
        lowT = st.sb("lowT", [32, S])
        qk = st.sb("qk", [P, TPB, qk_heads, hd])
        v = st.sb("v", [P, TPB, hd])
        rotated = [st.sb(f"rotated{i}", [P, qk_heads, 32]) for i in range(2)]
        square = [st.sb(f"square{i}", [P, qk_heads, hd]) for i in range(2)]
        mean_sq = st.sb("mean_sq", [P, TPB, qk_heads])
        rms_inv = st.sb("rms_inv", [P, TPB, qk_heads])
        kT = st.sb("kT", [hd, S])
        kcT = st.sb("kcT", [hd, blocks])
        vc = st.sb("vc", [blocks, hd])
        q_tiles = st.sb("q_tiles", [P, TPB, hd])
        qT = [st.sb(f"qT{i}", [hd, S]) for i in range(2)]
        block_scores = st.sb("block_scores", [P, TPB, blocks + 1])
        block_max = st.sb("block_max", [P, TPB])
        shifted = st.sb("shifted", [P, TPB, blocks + 1])
        block_sum = st.sb("block_sum", [P, TPB])
        gate_in = st.sb("gate_in", [P, TPB, 3])
        gate_sum = st.sb("gate_sum", [P, TPB])
        gate_inv = st.sb("gate_inv", [P, TPB])
        best = st.sb("best", [P, 4, 8])
        rest = st.sb("rest", [P, 4, blocks])
        gate = [st.sb(f"gate{i}", [P, TPB, 3]) for i in range(2)]
        block_probs = [st.sb(f"block_probs{i}", [P, TPB, blocks]) for i in range(2)]
        unselected = [st.sb(f"unselected{i}", [P, 4, blocks]) for i in range(2)]
        selected = [st.sb(f"selected{i}", [P, S]) for i in range(2)]
        window = [st.sb(f"window{i}", [P, 2 * P + 1]) for i in range(2)]
        probs = [st.sb(f"probs{i}", [P, S]) for i in range(2)]
        window_probs = [st.sb(f"window_probs{i}", [P, 2 * P + 1]) for i in range(2)]
        probsT = [st.sb(f"probsT{i}", [P, TPB + 3, P]) for i in range(2)]
        neg_max = st.sb("neg_max", [P, 4, 2])
        total = st.sb("total", [P, 4, 2])
        factor = st.sb("factor", [P, 4, 2])
        part = [st.sb(f"part{i}", [P, hd]) for i in range(2)]
        scores_ps = [st.bank(f"scores_ps{i}", S) for i in range(2)]
        side_ps, out_ps = st.bank("side_ps"), st.bank("out_ps")
        turned_ps = [st.bank(f"turned_ps{i}") for i in range(2)]
        low_ready, low_stored, raw_ready, rotated_ready = (st.sem("low_ready"), st.sem("low_stored"), st.sem("raw_ready"),
                                                           st.sem("rotated_ready"))
        rest_stored, squared, summed, root_ready = (st.sem("rest_stored"), st.sem("squared"), st.sem("summed"),
                                                    st.sem("root_ready"))
        normalised, kT_ps_ready, kT_ready, vc_ready = (st.sem("normalised"), st.sem("kT_ps_ready"), st.sem("kT_ready"),
                                                       st.sem("vc_ready"))
        copied, block_exp_in, block_exp = st.sem("copied"), st.sem("block_exp_in"), st.sem("block_exp")
        side_ready, side_read, side_done = st.sem("side_ready"), st.sem("side_read"), st.sem("side_done")
        dve_done = st.sem("dve_done")
        scores_ready, max_ready, probs_ready = st.sem("scores_ready"), st.sem("max_ready"), st.sem("probs_ready")
        turned, stored0, stored1 = st.sem("turned"), st.sem("stored0"), st.sem("stored1")
        out_ready, out_read, passed = st.sem("out_ready"), st.sem("out_read"), st.sem("passed")
        passed_dve = st.sem("passed_dve")
        side_steps = 3
        at_unit = [[0], [1], [], [2], [], [], [], []]
        sink = w["l1_attn.sink_rep"]

        def columns(i):
            return ([("block", 0)] + [("selected", j) for j in range(i + 1)]
                    + [("window", j) for j in range(max(i - 1, 0), i + 1)])

        n_banks = [-(-len(columns(i)) // 4) for i in range(TPB)]
        banks_before = [sum(n_banks[:i]) for i in range(TPB + 1)]
        firsts_before = [sum(min(n, 2) for n in n_banks[:i]) for i in range(TPB + 1)]
        thirds_before = [sum(max(n - 2, 0) for n in n_banks[:i]) for i in range(TPB + 1)]
        banks, firsts, thirds = banks_before[TPB], firsts_before[TPB], thirds_before[TPB]
        assert banks % 2 == 0

        @st.block.tensor
        def _(pe):
            pe.wait_ge(core.w_sem["l1_attn"], value)
            for half in range(halves):
                pe.wait_ge(low_stored, START + half)
                nc.tensor.matmul(side_ps[0:32, :], w["l1_attn.w_qc"], core.xT[:, b * S + half * CH:b * S + (half + 1) * CH],
                                 start=True, stop=True).then_inc(low_ready, 1)
            pe.wait_ge(low_stored, START + halves)
            for t in range(TPB):
                if t >= 2:
                    pe.wait_ge(rotated_ready, START + t - 1)
                    pe.wait_ge(rest_stored, START + t - 1)
                nc.tensor.matmul(scores_ps[t % 2][:, 0:CH], lowT[:, t * P:(t + 1) * P], w["l1_attn.w_qup"], start=True,
                                 stop=True)
                nc.tensor.matmul(scores_ps[t % 2][:, CH:CH + 2 * hd], core.xT[:, (b * TPB + t) * P:(b * TPB + t + 1) * P],
                                 w["l1_attn.w_kv"], start=True, stop=True).then_inc(raw_ready, 1)
            pe.wait_ge(normalised, START + 1)
            for t in range(TPB):
                mm = nc.tensor.transpose(turned_ps[t // 4][0:hd, t % 4 * P:(t % 4 + 1) * P], qk[:, t, heads, :],
                                         core.ident[:])
            mm.then_inc(kT_ps_ready, 1)
            for t in range(TPB):
                mm = nc.tensor.matmul(out_ps[0:blocks, 0:hd], w["l1_attn.block_mean"][:, t, :], v[:, t, :],
                                      start=t == 0, stop=t == TPB - 1)
            mm.then_inc(vc_ready, 1)
            pe.wait_ge(kT_ready, START + 2)

            def side(slot, k, number, head):
                pe.wait_ge(side_read, START + number)
                if k < 2:
                    pe.wait_ge(copied, START + head + 1)
                    pe.sem_inc(passed, 1)
                    for i in range(4):
                        mm = nc.tensor.transpose(side_ps[0:hd, i * P:(i + 1) * P], q_tiles[:, 4 * k + i, :],
                                                 core.ident[:])
                else:
                    for t in range(TPB):
                        nc.tensor.matmul(side_ps[:, t * blocks:(t + 1) * blocks], qT[slot][:, t * P:(t + 1) * P],
                                         kcT[:], start=True, stop=True)
                        mm = nc.tensor.matmul(side_ps[:, 256 + 3 * t:259 + 3 * t], qT[slot][:, t * P:(t + 1) * P],
                                              w["l1_attn.w_gate"], start=True, stop=True)
                mm.then_inc(side_ready, 1)

            def scores(slot, i):
                keys = (i + 1) * P
                for at in range(0, keys, CH):
                    end = min(keys, at + CH)
                    nc.tensor.matmul(scores_ps[i % 2][:, at:end], qT[slot][:, i * P:(i + 1) * P], kT[:, at:end],
                                     start=True, stop=end < keys)
                nc.tensor.matmul(scores_ps[i % 2][:, i * P:(i + 1) * P], core.ident16[:], core.causal16[:],
                                 start=False, stop=True).then_inc(scores_ready, 1)

            for k in range(side_steps):
                side(0, k, k, 0)
            pe.wait_ge(side_read, START + side_steps)
            scores(0, 0)
            scores(0, 1)
            with pe.Fori(0, heads // 2) as u:
                for s in range(2):
                    head = 2 * u + s
                    for i in range(TPB):
                        unit = head * TPB + i
                        pe.wait_ge(probs_ready, START + unit + 1)
                        if i == 0:
                            pe.wait_ge(side_done, START + head + 1)
                        todo = columns(i)

                        def ahead():
                            if i < TPB - 2:
                                scores(s, i + 2)
                            else:
                                if i == TPB - 2:
                                    pe.wait_ge(side_read, START + (head + 2) * side_steps)
                                scores(1 - s, i + 2 - TPB)

                        for g in range(n_banks[i]):
                            if g == 2:
                                ahead()
                            bank = (banks_before[i] + g) % 2
                            pe.wait_ge(stored0, START + head * firsts + firsts_before[i] + (1 if g == 2 else 0))
                            pe.wait_ge(stored1, START + head * thirds + thirds_before[i])
                            if g == 2:
                                pe.sem_inc(passed, 1)
                            for c, (kind, j) in enumerate(todo[4 * g:4 * g + 4]):
                                if kind == "block":
                                    dst, src = turned_ps[bank][0:blocks, 0:P], block_probs[s][:, i, :]
                                else:
                                    dst = turned_ps[bank][:, c * P:(c + 1) * P]
                                    src = (probs[i % 2][:, j * P:(j + 1) * P] if kind == "selected" else
                                           window_probs[i % 2][:, (j - i + 1) * P:(j - i + 2) * P])
                                if c == 0:
                                    pe.sem_inc(passed, 1)
                                mm = nc.tensor.transpose(dst, src, core.ident[:])
                            mm.then_inc(turned, 1)
                        if n_banks[i] < 3:
                            ahead()
                        for k in at_unit[i]:
                            side(1 - s, k, side_steps * (head + 1) + k, head + 1)
                        pe.wait_ge(stored0, START + head * firsts + firsts_before[i + 1])
                        pe.wait_ge(stored1, START + head * thirds + thirds_before[i + 1])
                        pe.wait_ge(out_read, START + unit)
                        pe.sem_inc(passed, 1)
                        for kind, at in (("selected", 0), ("window", hd)):
                            group = [(c, j) for c, (k, j) in enumerate(todo) if k == kind]
                            for c, j in group:
                                nc.tensor.matmul(out_ps[:, at:at + hd], probsT[i % 2][:, c, :], v[:, j, :],
                                                 start=(c, j) == group[0], stop=(c, j) == group[-1])
                        nc.tensor.matmul(out_ps[:, 2 * hd:3 * hd], probsT[i % 2][0:blocks, 0, :], vc[:], start=True,
                                         stop=True).then_inc(out_ready, 1)

        @st.block.scalar
        def _(act):
            for half in range(halves):
                act.wait_ge(low_ready, START + half + 1)
                nc.scalar.activation(lowT[:, half * CH:(half + 1) * CH], side_ps[0:32, :], ACT.Copy
                                     ).then_inc(low_stored, 1)
            for t in range(TPB):
                act.wait_ge(raw_ready, START + t + 1)
                act.wait_ge(rotated_ready, START + t + 1)
                raw = scores_ps[t % 2][:, 0:qk_heads * hd].rearrange("p (h d) -> p h d", d=hd)
                nc.scalar.activation(qk[:, t, :, 32:hd], raw[:, :, 32:hd], ACT.Copy)
                nc.scalar.activation(v[:, t, :], scores_ps[t % 2][:, qk_heads * hd:(qk_heads + 1) * hd], ACT.Copy
                                     ).then_inc(rest_stored, 1)
                act.wait_ge(rest_stored, START + t + 1)
                if t >= 2:
                    act.wait_ge(summed, START + t - 1)
                nc.scalar.activation(square[t % 2][:], qk[:, t], ACT.Square).then_inc(squared, 1)
            act.wait_ge(summed, START + TPB + 1)
            nc.scalar.activation(mean_sq[:], mean_sq[:], ACT.Sqrt).then_inc(root_ready, 1)
            act.wait_ge(kT_ps_ready, START + 1)
            for half in range(halves):
                ins = nc.scalar.activation(kT[:, half * CH:(half + 1) * CH], turned_ps[half][0:hd, :], ACT.Copy)
            ins.then_inc(kT_ready, 1)

            def exponentials(i, unit):
                keys, first = (i + 1) * P, P if i == 0 else 0
                act.wait_ge(max_ready, START + unit + 1)
                nc.scalar.activation(probs[i % 2][:, 0:keys], (selected if i >= 4 else scores_ps)[i % 2][:, 0:keys],
                                     ACT.Exp, bias=neg_max[:, i % 4, 0:1], accum_out=total[:, i % 4, 0:1])
                nc.scalar.activation(window_probs[i % 2][:, first:], window[i % 2][:, first:], ACT.Exp,
                                     bias=neg_max[:, i % 4, 1:2], accum_out=total[:, i % 4, 1:2]).then_inc(probs_ready, 1)

            def side_exponentials(number):
                act.wait_ge(block_exp_in, START + number)
                nc.scalar.activation(shifted[:], shifted[:], ACT.Exp)
                nc.scalar.activation(gate_in[:], gate_in[:], ACT.Exp, scale=-1.0).then_inc(block_exp, 1)

            side_exponentials(1)
            exponentials(0, 0)
            with act.Fori(0, heads // 2) as u:
                for s in range(2):
                    head = 2 * u + s
                    for i in range(TPB):
                        unit = head * TPB + i
                        act.wait_ge(turned, START + head * banks + banks_before[i])
                        act.wait_ge(out_read, START + unit - 2 if s or i >= 2 else 2 * u * TPB)
                        exponentials((i + 1) % TPB, unit + 1)
                        todo = columns(i)
                        for g in range(min(n_banks[i], 2)):
                            act.wait_ge(turned, START + head * banks + banks_before[i] + g + 1)
                            if g == 0:
                                act.wait_ge(out_ready, START + unit - 1 if s or i >= 1 else 2 * u * TPB)
                            end = min(4 * g + 4, len(todo))
                            first = max(4 * g, 1)
                            bank = turned_ps[(banks_before[i] + g) % 2]
                            if g == 0:
                                nc.scalar.activation(probsT[i % 2][0:blocks, 0, :], bank[0:blocks, 0:P], ACT.Copy)
                            nc.scalar.activation(probsT[i % 2][:, first:end, :].rearrange("p j q -> p (j q)"),
                                                 bank[:, (first - 4 * g) * P:(end - 4 * g) * P], ACT.Copy
                                                 ).then_inc(stored0, 1)
                        if i == 3:
                            side_exponentials(head + 2)

        @st.block.gpsimd
        def _(pool):
            pool.wait_ge(normalised, START + 1)
            nc.gpsimd.tensor_copy(q_tiles[:], qk[:, :, 0, :]).then_inc(copied, 1)
            nc.gpsimd.memset(grouped[:], 0.0)
            with pool.Fori(0, heads // 2) as u:
                for s in range(2):
                    head = 2 * u + s
                    pool.wait_ge(side_ready, START + side_steps * head + 2)
                    nc.gpsimd.tensor_copy(q_tiles[:], qk[:, :, head + 1, :]).then_inc(copied, 1)

        @st.block.vector
        def _(dve):
            step = Steps(dve, dve_done)
            dve.wait_ge(core.w_sem["l1_attn"], value)
            for t in range(TPB):
                dve.wait_ge(raw_ready, START + t + 1)
                raw = scores_ps[t % 2][:, 0:qk_heads * hd].rearrange("p (h d) -> p h d", d=hd)
                for i in range(2):
                    ins = nc.vector.tensor_tensor(
                        rotated[i][:].rearrange("p h (c d) -> p h c d", c=2),
                        raw[:, :, 16 * i:16 * i + 16].unsqueeze(2).to_broadcast([P, qk_heads, 2, 16]),
                        w["l1_attn.rope"][:, i, t, :].rearrange("p (c d) -> p c d", c=2).unsqueeze(1)
                        .to_broadcast([P, qk_heads, 2, 16]), ALU.mult)
                step.done(ins)
                step.done(nc.vector.tensor_tensor(qk[:, t, :, 0:32], rotated[0][:], rotated[1][:], ALU.add))
                nc.vector.tensor_copy(block_max[:, 0:1], w["l1_attn.sink_rep"][:, 0:1]).then_inc(rotated_ready, 1)
                dve.wait_ge(squared, START + t + 1)
                nc.vector.tensor_reduce(mean_sq[:, t, :], square[t % 2][:], AX.X, ALU.add).then_inc(summed, 1)
            dve.wait_ge(summed, START + TPB)
            nc.vector.tensor_scalar(mean_sq[:], mean_sq[:], 1.0 / hd, 1e-6, ALU.mult, ALU.add).then_inc(summed, 1)
            dve.wait_ge(root_ready, START + 1)
            step.done(nc.vector.reciprocal(rms_inv[:], mean_sq[:]))
            for t in range(TPB):
                ins = nc.vector.tensor_tensor(qk[:, t], qk[:, t],
                                              rms_inv[:, t, :].unsqueeze(2).to_broadcast([P, qk_heads, hd]), ALU.mult)
            step.done(ins)
            for t in range(TPB):
                nc.vector.tensor_tensor(qk[:, t, 0:heads, :], qk[:, t, 0:heads, :],
                                        w["l1_attn.g_q_rep"].unsqueeze(1).to_broadcast([P, heads, hd]), ALU.mult)
                ins = nc.vector.scalar_tensor_tensor(qk[:, t, heads, :], qk[:, t, heads, :], hd ** -0.5,
                                                     w["l1_attn.g_k_rep"], op0=ALU.mult, op1=ALU.mult)
            ins.then_inc(normalised, 1)
            dve.wait_ge(vc_ready, START + 1)
            nc.vector.tensor_copy(vc[:], out_ps[0:blocks, 0:hd])
            dve.wait_ge(kT_ready, START + 1)
            step.done(nc.vector.tensor_reduce(kcT[:], kT[:].rearrange("p (n c) -> p n c", c=S // blocks), AX.X, ALU.add))
            nc.vector.tensor_scalar(kcT[:], kcT[:], blocks / S, None, ALU.mult).then_inc(kT_ready, 1)


            def read_side(slot, k, number, head):
                dve.wait_ge(side_ready, START + number + 1)
                if k < 2:
                    nc.vector.tensor_copy(qT[slot][:, k * CH:(k + 1) * CH], side_ps[0:hd, :]).then_inc(side_read, 1)
                    return
                before = step.n
                nc.vector.tensor_tensor(block_scores[:, :, 0:blocks], side_ps[:, 0:256].rearrange("p (t n) -> p t n", n=blocks),
                                        w["l1_attn.block_mask"], ALU.add)
                nc.vector.tensor_copy(block_scores[:, :, blocks], sink[:, bass.ds(head, 1)].to_broadcast([P, TPB]))
                nc.vector.tensor_tensor(gate_in[:], side_ps[:, 256:280].rearrange("p (t n) -> p t n", n=3),
                                        w["l1_attn.b_gate_rep"].unsqueeze(1).to_broadcast([P, TPB, 3]), ALU.add
                                        ).then_inc(side_read, 1)
                dve.wait_ge(side_read, START + number + 1)
                step.done(nc.vector.tensor_reduce(block_max[:], block_scores[:], AX.X, ALU.max))
                nc.vector.tensor_tensor(shifted[:], block_scores[:],
                                        block_max[:].unsqueeze(2).to_broadcast([P, TPB, blocks + 1]), ALU.subtract
                                        ).then_inc(block_exp_in, 1)
                for t in range(4):
                    ins = nc.vector.max(best[:, t, :], block_scores[:, 4 + t, 0:blocks])
                step.done(ins)
                dve.sem_inc(passed_dve, 1)
                for t in range(4):
                    ins = nc.vector.match_replace(rest[:, t, :], best[:, t, :], block_scores[:, 4 + t, 0:blocks], -3e38)
                step.done(ins)
                dve.sem_inc(passed_dve, 1)
                for t in range(4):
                    ins = nc.vector.max(best[:, t, :], rest[:, t, :])
                step.done(ins)
                step.done(nc.vector.tensor_tensor(unselected[slot][:], block_scores[:, 4:, 0:blocks],
                                                  best[:, :, 7:8].to_broadcast([P, 4, blocks]), ALU.is_lt))
                nc.vector.tensor_scalar(unselected[slot][:], unselected[slot][:], NEG, None, ALU.mult)
                dve.wait_ge(block_exp, START + head + 1)
                step.done(nc.vector.tensor_scalar(gate_in[:], gate_in[:], 1.0, None, ALU.add))
                nc.vector.tensor_reduce(block_sum[:], shifted[:], AX.X, ALU.add)
                step.done(nc.vector.reciprocal(gate[slot][:], gate_in[:]))
                step.done(nc.vector.tensor_reduce(gate_sum[:], gate[slot][:], AX.X, ALU.add))
                step.done(nc.vector.tensor_scalar(gate_sum[:], gate_sum[:], 1e-6, None, ALU.max))
                nc.vector.reciprocal(block_max[:], block_sum[:])
                step.done(nc.vector.reciprocal(gate_inv[:], gate_sum[:]))
                step.done(nc.vector.tensor_tensor(gate[slot][:], gate[slot][:],
                                                  gate_inv[:].unsqueeze(2).to_broadcast([P, TPB, 3]), ALU.mult))
                step.done(nc.vector.tensor_tensor(block_max[:], block_max[:], gate[slot][:, :, 0], ALU.mult))
                nc.vector.tensor_tensor(block_probs[slot][:], shifted[:, :, 0:blocks],
                                        block_max[:].unsqueeze(2).to_broadcast([P, TPB, blocks]), ALU.mult
                                        ).then_inc(side_done, 1)
                dve.wait_ge(side_done, START + head + 1)
                assert step.n - before == SIDE_CHAIN, step.n - before

            def maxima(slot, i, unit, head):
                keys, first = (i + 1) * P, P if i == 0 else 0
                dve.wait_ge(scores_ready, START + unit + 1)
                seen = scores_ps[i % 2]
                if i >= 4:
                    nc.vector.tensor_tensor(selected[i % 2][:, 0:keys].rearrange("p (n c) -> p n c", c=32),
                                            seen[:, 0:keys].rearrange("p (n c) -> p n c", c=32),
                                            unselected[slot][:, i - 4, 0:keys // 32].unsqueeze(2)
                                            .to_broadcast([P, keys // 32, 32]), ALU.add)
                    seen = selected[i % 2]
                nc.vector.tensor_tensor(window[i % 2][:, first:2 * P], scores_ps[i % 2][:, (i - 1) * P + first:keys],
                                        w["l1_attn.window_mask"][:, first:], ALU.add)
                step.done(nc.vector.tensor_copy(window[i % 2][:, 2 * P:], sink[:, bass.ds(head, 1)]))
                nc.vector.tensor_reduce(neg_max[:, i % 4, 0:1], seen[:, 0:keys], AX.X, ALU.max, negate=True)
                nc.vector.tensor_reduce(neg_max[:, i % 4, 1:2], window[i % 2][:, first:], AX.X, ALU.max, negate=True
                                        ).then_inc(max_ready, 1)

            for k in range(side_steps):
                read_side(0, k, k, 0)
            maxima(0, 0, 0, 0)
            maxima(0, 1, 1, 0)
            with step.loop(heads // 2, 2 * (SIDE_CHAIN + 5 * TPB)) as u:
                for s in range(2):
                    head = 2 * u + s
                    for i in range(TPB):
                        unit = head * TPB + i
                        if i < TPB - 2:
                            maxima(s, i + 2, unit + 2, head)
                        else:
                            maxima(1 - s, i + 2 - TPB, unit + 2, head + 1)
                        for k in at_unit[i]:
                            read_side(1 - s, k, side_steps * (head + 1) + k, head + 1)
                        if n_banks[i] == 3:
                            todo = columns(i)
                            dve.wait_ge(turned, START + head * banks + banks_before[i] + 3)
                            dve.wait_ge(out_ready, START + unit - 1)
                            nc.vector.tensor_copy(probsT[i % 2][:, 8:len(todo), :].rearrange("p j q -> p (j q)"),
                                                  turned_ps[banks_before[i] % 2][:, 0:(len(todo) - 8) * P]
                                                  ).then_inc(stored1, 1)
                        dve.wait_ge(probs_ready, START + unit + 1)
                        step.done(nc.vector.reciprocal(factor[:, i % 4, :], total[:, i % 4, :]))
                        step.done(nc.vector.tensor_tensor(factor[:, i % 4, :], factor[:, i % 4, :], gate[s][:, i, 1:3],
                                                          ALU.mult))
                        dve.wait_ge(out_ready, START + unit + 1)
                        step.done(nc.vector.tensor_scalar(part[0][:], out_ps[:, 0:hd], factor[:, i % 4, 0:1], None,
                                                          ALU.mult))
                        step.done(nc.vector.scalar_tensor_tensor(part[1][:], out_ps[:, hd:2 * hd],
                                                                 factor[:, i % 4, 1:2], part[0][:], op0=ALU.mult,
                                                                 op1=ALU.add))
                        nc.vector.tensor_tensor(mixed[:, i, bass.ds(head * hd, hd)], out_ps[:, 2 * hd:3 * hd], part[1][:],
                                                ALU.add).then_inc(out_read, 1)


def l2_ffn(core):
    w, sem, value = core.w, core.w_sem["l2_ffn"], core.w_value["l2_ffn"]
    layer_norm_and_transpose(core, core.x, 1e-5, "norm", keep=True,
                            small=(w["l2_ffn.wg"], None, core.logits, sem, value))
    top2_gates(core, "gates", 8, softmax_over_all=False)
    add_gated_rows(core, "beta", w["l2_ffn.beta"], sem, value)
    experts_ffn(core, "ffn", 8, 512, ACT.Gelu, w["l2_ffn.w1"], w["l2_ffn.w2"], sem, value,
                b1=w["l2_ffn.b1"], b2=w["l2_ffn.b2_rep"], normed=(w["l2_ffn.gamma_rep"], 1e-6))


def l2_attn(core):
    nc, w, sem, value = core.nc, core.w, core.w_sem["l2_attn"], core.w_value["l2_attn"]
    heads, hd = 16, 64
    layer_norm_and_transpose(core, core.x, 1e-5, "norm", rms_eps=float(np.finfo(np.float32).eps),
                             gain=w["l2_attn.norm_w"][:, 0:1], shift=0.0, gain_sem=sem, gain_value=value)
    for b in range(B):
        with ExitStack() as ctx:
            mixed = core.sb(f"mixed{core.stages}", [P, TPB, heads * hd], ctx=ctx)
            softclamped_attention(core, b, mixed, heads, hd)
            project_tokens(core, "wo", mixed, TPB, w["l2_attn.wo"], sem, value,
                           lambda t, end: core.x[:, b * TPB + t:b * TPB + end, :])


def softclamped_attention(core, b, mixed, heads, hd):
    nc, w, sem, value = core.nc, core.w, core.w_sem["l2_attn"], core.w_value["l2_attn"]
    halves = S // CH
    with core.stage("l2attn") as st:
        norms = st.sb("norms", [P, TPB, heads, 2])
        inverse = st.sb("inverse", [P, TPB, heads + 1, 2])
        square = [st.sb(f"square{i}", [P, 2, 2 * hd]) for i in range(2)]
        gain = st.sb("gain", [hd, heads + 1])
        gain1 = st.sb("gain1", [hd, 2, heads])
        qk_slot = st.sb("qk_slot", [P, TPB, 2 * hd])
        v_slot = [st.sb(f"v_slot{i}", [P, TPB, hd + 1]) for i in range(2)]
        qT = [st.sb(f"qT{i}", [hd, S]) for i in range(2)]
        kT = [st.sb(f"kT{i}", [hd, S]) for i in range(2)]
        clamped = [st.sb(f"clamped{i}", [P, S]) for i in range(2)]
        probs = [st.sb(f"probs{i}", [P, S]) for i in range(2)]
        sums = st.sb("sums", [P, 2, 4])
        scores_ps = [st.bank(f"scores_ps{i}", S) for i in range(2)]
        out_ps = [st.bank(f"out_ps{i}") for i in range(halves)]
        side_ps = [st.bank(f"side_ps{i}") for i in range(2)]
        raw_ready, squared, summed, root_ready = (st.sem("raw_ready"), st.sem("squared"), st.sem("summed"),
                                                  st.sem("root_ready"))
        dve_done, passed = st.sem("dve_done"), st.sem("passed")
        side_ready, side_read = st.sem("side_ready"), st.sem("side_read")
        scores_ready, clamped_ready, probs_ready = st.sem("scores_ready"), st.sem("clamped_ready"), st.sem("probs_ready")
        probs_used, out_read, summed_out = st.sem("probs_used"), st.sem("out_read"), st.sem("summed_out")
        pairs = TPB // 2
        next_head = pairs + 4
        per_head = next_head
        tiles_T = lambda t: core.xT[:, (b * TPB + t) * P:(b * TPB + t + 1) * P]

        @st.block.tensor
        def _(pe):
            pe.wait_ge(core.w_sem["l2_attn"], value)
            for t in range(TPB):
                for g in range(heads // 2):
                    n = t * heads // 2 + g
                    if n >= 2:
                        pe.wait_ge(squared, START + n - 1)
                    nc.tensor.matmul(side_ps[n % 2][:, :4 * hd], tiles_T(t), w["l2_attn.wqkv"][:, 2 * g:2 * g + 2, 0:2 * hd],
                                     start=True, stop=True).then_inc(raw_ready, 1)
            pe.wait_ge(squared, START + TPB * heads // 2)

            def side_bank(number):
                pe.wait_ge(side_read, START + number - 1)

            def project(head, pair, number):
                side_bank(number)
                for i in range(2):
                    mm = nc.tensor.matmul(side_ps[pair % 2][:, i * 192:(i + 1) * 192], tiles_T(2 * pair + i),
                                          w["l2_attn.wqkv"][:, bass.ds(head, 1), :], start=True, stop=True)
                mm.then_inc(side_ready, 1)

            def turn(group, number, projected):
                half, part = divmod(group, 2)
                pe.wait_ge(side_read, START + projected)
                side_bank(number)
                pe.sem_inc(passed, 1)
                for i in range(4):
                    mm = nc.tensor.transpose(side_ps[group % 2][0:hd, i * P:(i + 1) * P],
                                             qk_slot[:, half * 4 + i, part * hd:(part + 1) * hd], core.ident[:])
                mm.then_inc(side_ready, 1)

            def scores(slot, j, unit, prepared):
                pe.wait_ge(side_read, START + prepared)
                pe.wait_ge(clamped_ready, START + unit)
                for half in range(halves):
                    mm = nc.tensor.matmul(scores_ps[j % 2][:, half * CH:(half + 1) * CH],
                                          kT[slot][:, j * P:(j + 1) * P], qT[slot][:, half * CH:(half + 1) * CH],
                                          start=True, stop=True)
                mm.then_inc(scores_ready, 1)

            for pair in range(pairs):
                project(0, pair, max(pair, 1))
            for group in range(4):
                turn(group, pairs + group, pairs)
            scores(0, 0, 0, next_head)
            with pe.Fori(0, heads // 2) as u:
                for s in range(2):
                    head = 2 * u + s
                    before = next_head + head * per_head
                    for j in range(TPB):
                        unit = head * TPB + j
                        if j < TPB - 1:
                            scores(s, j + 1, unit, before)
                        else:
                            scores(1 - s, 0, unit, before + next_head)
                        if j < pairs:
                            project(head + 1, j, before + j)
                        elif j < pairs + 2:
                            for group in (2 * (j - pairs), 2 * (j - pairs) + 1):
                                turn(group, before + pairs + group, before + pairs)
                        pe.wait_ge(probs_ready, START + unit + 1)
                        if j == 0:
                            pe.wait_ge(out_read, START + head)
                        for i in range(TPB):
                            mm = nc.tensor.matmul(out_ps[i // 4][:, i % 4 * (hd + 1):(i % 4 + 1) * (hd + 1)],
                                                  probs[j % 2][:, i * P:(i + 1) * P], v_slot[s][:, j, :],
                                                  start=j == 0 and i % 4 == 0, stop=j == TPB - 1,
                                                  skip_group_check=True)
                        mm.then_inc(probs_used, 1)

        @st.block.scalar
        def _(act):
            for n in range(TPB * heads // 2):
                act.wait_ge(raw_ready, START + n + 1)
                if n >= 2:
                    act.wait_ge(summed, START + n - 1)
                nc.scalar.activation(square[n % 2][:].rearrange("p h c -> p (h c)"), side_ps[n % 2][:, :4 * hd],
                                     ACT.Square).then_inc(squared, 1)
            act.wait_ge(summed, START + TPB * heads // 2)
            nc.scalar.activation(norms[:].rearrange("p t h c -> p (t h c)"),
                                 norms[:].rearrange("p t h c -> p (t h c)"), ACT.Sqrt).then_inc(root_ready, 1)
            with act.Fori(0, heads // 2) as u:
                for s in range(2):
                    for j in range(TPB):
                        unit = (2 * u + s) * TPB + j
                        act.wait_ge(scores_ready, START + unit + 1)
                        nc.scalar.activation(clamped[j % 2][:], scores_ps[j % 2][:], ACT.Tanh, scale=1.0 / 50.0
                                             ).then_inc(clamped_ready, 1)
                        act.wait_ge(clamped_ready, START + unit + 1)
                        act.wait_ge(probs_used, START + unit - 1 if s or j >= 1 else 2 * u * TPB)
                        nc.scalar.activation(probs[j % 2][:], clamped[j % 2][:], ACT.Exp, scale=50.0 * hd ** -0.5
                                             ).then_inc(probs_ready, 1)

        @st.block.vector
        def _(dve):
            step = Steps(dve, dve_done)
            dve.wait_ge(core.w_sem["l2_attn"], value)
            nc.vector.memset(gain[:, heads:heads + 1], 0.0)
            nc.vector.memset(inverse[:, :, heads, :], 0.0)
            for i in range(2):
                nc.vector.memset(v_slot[i][:, :, hd:hd + 1], 1.0)
            step.done(nc.vector.tensor_scalar(gain1[:], w["l2_attn.gammas"], 1.0, float(hd) ** 0.5, ALU.add, ALU.mult))
            step.done(nc.vector.tensor_tensor(gain[:, 0:heads], gain1[:, 0, :], gain1[:, 1, :], ALU.mult))
            for t in range(TPB):
                for g in range(heads // 2):
                    n = t * heads // 2 + g
                    dve.wait_ge(squared, START + n + 1)
                    nc.vector.tensor_reduce(norms[:, t, 2 * g:2 * (g + 1), :],
                                            square[n % 2][:].rearrange("p h (c d) -> p h c d", c=2), AX.X, ALU.add
                                            ).then_inc(summed, 1)
            dve.wait_ge(root_ready, START + 1)
            step.done(nc.vector.tensor_scalar(norms[:], norms[:], 1e-12, None, ALU.max))
            step.done(nc.vector.reciprocal(inverse[:, :, 0:heads, :], norms[:]))

            def read_projected(slot, pair, number, head):
                dve.wait_ge(side_ready, START + number + 1)
                raw = side_ps[pair % 2][:, :384].rearrange("p (t c) -> p t c", t=2)
                for i in range(2):
                    t = 2 * pair + i
                    nc.vector.tensor_tensor(qk_slot[:, t, :].rearrange("p (c d) -> p c d", c=2),
                                            raw[:, i, 0:2 * hd].rearrange("p (c d) -> p c d", c=2),
                                            inverse[:, t, bass.ds(head, 1), :].rearrange("p h c -> p (h c)")
                                            .unsqueeze(2).to_broadcast([P, 2, hd]), ALU.mult)
                nc.vector.tensor_copy(v_slot[slot][:, 2 * pair:2 * pair + 2, 0:hd], raw[:, :, 2 * hd:3 * hd]
                                      ).then_inc(side_read, 1)

            def read_turned(slot, group, number, head):
                half, part = divmod(group, 2)
                dve.wait_ge(side_ready, START + number + 1)
                src, part_of = side_ps[group % 2][0:hd, :], slice(half * CH, (half + 1) * CH)
                if part == 0:
                    nc.vector.tensor_scalar(qT[slot][:, part_of], src, gain[:, bass.ds(head, 1)], None, ALU.mult
                                            ).then_inc(side_read, 1)
                else:
                    nc.vector.tensor_copy(kT[slot][:, part_of], src).then_inc(side_read, 1)

            for pair in range(pairs):
                read_projected(0, pair, pair, 0)
            for group in range(4):
                read_turned(0, group, pairs + group, 0)
            with dve.Fori(0, heads // 2) as u:
                for s in range(2):
                    head = 2 * u + s
                    before = next_head + head * per_head
                    for pair in range(pairs):
                        read_projected(1 - s, pair, before + pair, head + 1)
                    for group in range(4):
                        read_turned(1 - s, group, before + pairs + group, head + 1)
                    dve.wait_ge(probs_used, START + (head + 1) * TPB)
                    for half in range(halves):
                        out = out_ps[half][:, :4 * (hd + 1)].rearrange("p (t c) -> p t c", t=4)
                        nc.vector.reciprocal(sums[:, half, :], out[:, :, hd]).then_inc(summed_out, 1)
                    dve.wait_ge(summed_out, START + head * 2 + 2)
                    for half in range(halves):
                        out = out_ps[half][:, :4 * (hd + 1)].rearrange("p (t c) -> p t c", t=4)
                        ins = nc.vector.tensor_tensor(mixed[:, 4 * half:4 * half + 4, bass.ds(head * hd, hd)],
                                                      out[:, :, 0:hd],
                                                      sums[:, half, :].unsqueeze(2).to_broadcast([P, 4, hd]), ALU.mult)
                    ins.then_inc(out_read, 1)


def l3_ffn(core):
    nc, w, sem, value = core.nc, core.w, core.w_sem["l3_ffn"], core.w_value["l3_ffn"]
    column = lambda i: w["l3_ffn.columns"][:, i:i + 1]
    heads, kv_heads, hd = 16, 4, 8
    with ExitStack() as ctx:
        qkv = core.sb(f"qkv{core.stages}", [P, TILES, 192], ctx=ctx)
        mixed = core.sb(f"mixed{core.stages}", [P, TILES, D], ctx=ctx)
        layer_norm_and_transpose(core, core.x, 1e-5, "ln1", keep_plain=True, rms_eps=1e-5, gain=column(0),
                                 shift=column(1), gain_sem=sem, gain_value=value,
                                 small=(w["l3_ffn.wqkv"], None, qkv, sem, value))
        with core.stage("pairs") as st:
            product = st.sb("product", [P, 2, TPB, heads, hd])
            scores = st.sb("scores", [P, 2, TPB, heads])
            work = st.sb("work", [P, 2, TPB, heads])
            dve_done, to_exp, exp_done = st.sem("dve_done"), st.sem("to_exp"), st.sem("exp_done")
            rep = heads // kv_heads
            late = slice(TPB, 2 * TPB)

            def kv(position, first, k):
                at = position * TPB
                return qkv[:, at:at + TPB, first + k * hd:first + (k + 1) * hd].unsqueeze(2).to_broadcast(
                    [P, TPB, rep, hd])

            @st.block.vector
            def _(dve):
                step = Steps(dve, dve_done)
                for position in range(2):
                    for k in range(kv_heads):
                        q = qkv[:, late, k * rep * hd:(k + 1) * rep * hd].rearrange("p t (r d) -> p t r d", r=rep)
                        ins = nc.vector.tensor_tensor(product[:, position, :, k * rep:(k + 1) * rep, :], q,
                                                      kv(position, D, k), ALU.mult)
                step.done(ins)
                for position in range(2):
                    ins = nc.vector.tensor_reduce(scores[:, position], product[:, position], AX.X, ALU.add)
                step.done(ins)
                step.done(nc.vector.tensor_tensor(work[:, 0], scores[:, 0], scores[:, 1], ALU.max))
                for position in range(2):
                    ins = nc.vector.tensor_tensor(scores[:, position], scores[:, position], work[:, 0], ALU.subtract)
                ins.then_inc(to_exp, 1)
                dve.wait_ge(exp_done, START + 1)
                step.done(nc.vector.tensor_tensor(work[:, 0], scores[:, 0], scores[:, 1], ALU.add))
                step.done(nc.vector.reciprocal(work[:, 1], work[:, 0]))
                for position in range(2):
                    ins = nc.vector.tensor_tensor(scores[:, position], scores[:, position], work[:, 1], ALU.mult)
                step.done(ins)
                for position in range(2):
                    for k in range(kv_heads):
                        p = scores[:, position, :, k * rep:(k + 1) * rep].unsqueeze(3).to_broadcast([P, TPB, rep, hd])
                        ins = nc.vector.tensor_tensor(product[:, position, :, k * rep:(k + 1) * rep, :], p,
                                                      kv(position, D + kv_heads * hd, k), ALU.mult)
                step.done(ins)
                nc.vector.tensor_tensor(mixed[:, late, :], product[:, 0].rearrange("p t h d -> p t (h d)"),
                                        product[:, 1].rearrange("p t h d -> p t (h d)"), ALU.add)
                for k in range(kv_heads):
                    nc.vector.tensor_copy(mixed[:, 0:TPB, k * rep * hd:(k + 1) * rep * hd].rearrange(
                        "p t (r d) -> p t r d", r=rep), kv(0, D + kv_heads * hd, k))

            @st.block.scalar
            def _(act):
                act.wait_ge(to_exp, START + 1)
                nc.scalar.activation(scores[:], scores[:], ACT.Exp, scale=hd ** -0.5).then_inc(exp_done, 1)

        project_tokens(core, "proj", mixed, TILES, w["l3_ffn.wproj"].unsqueeze(1), sem, value,
                       lambda t, end: core.kept[:, t:end, :])
    layer_norm_and_transpose(core, core.kept, 1e-5, "ln2", gain=column(2), shift=column(3), gain_sem=sem,
                             gain_value=value,
                             small=(w["l3_ffn.wg"], None, core.logits, sem, value))
    top2_gates(core, "gates", 8, softmax_over_all=True)
    with core.stage("residual") as st:
        @st.block.vector
        def _(dve):
            nc.vector.scalar_tensor_tensor(core.x[:].rearrange("p t d -> p (t d)"),
                                           core.kept[:].rearrange("p t d -> p (t d)"), 0.5,
                                           core.x[:].rearrange("p t d -> p (t d)"), op0=ALU.mult, op1=ALU.add)
    experts_ffn(core, "ffn", 8, 256, ACT.Gelu_apprx_tanh, w["l3_ffn.w1"], w["l3_ffn.w2"], sem, value)


def l3_attn(core):
    nc, w, sem, value = core.nc, core.w, core.w_sem["l3_attn"], core.w_value["l3_attn"]
    layer_norm_and_transpose(core, core.x, 1e-5, "norm")
    with core.stage("gru") as st:
        z = st.sb("z", [P, TOKENS])
        a = st.sb("a", [P, TOKENS])
        b = st.sb("b", [P, TOKENS])
        h = st.sb("h", [P, TOKENS])
        gate_ps = [st.bank(f"gate_ps{i}") for i in range(2)]
        value_ps = [st.bank(f"value_ps{i}") for i in range(2)]
        y_ps = [st.bank(f"y_ps{i}") for i in range(4)]
        gate_ready, value_ready = st.sem("gate_ready"), st.sem("value_ready")
        z_ready, b_ready, h_ready = st.sem("z_ready"), st.sem("b_ready"), st.sem("h_ready")
        swish_ready, y_ready, y_turned, y_stored = (st.sem("swish_ready"), st.sem("y_ready"), st.sem("y_turned"),
                                                    st.sem("y_stored"))
        bz, bh = w["l3_attn.columns"][:, 0:1], w["l3_attn.columns"][:, 1:2]
        beta = w["l3_attn.swish_rep"][:, 0:1]

        @st.block.tensor
        def _(pe):
            pe.wait_ge(core.w_sem["l3_attn"], value)
            with pe.Fori(0, CHUNKS // 2) as u:
                for s in range(2):
                    pe.wait_ge(b_ready, START + 2 * u)
                    xt = core.xT[:, bass.ds((2 * u + s) * CH, CH)]
                    nc.tensor.matmul(gate_ps[s][:], w["l3_attn.wz"], xt, start=True, stop=True).then_inc(gate_ready, 1)
                    nc.tensor.matmul(value_ps[s][:], w["l3_attn.wh"], xt, start=True, stop=True
                                     ).then_inc(value_ready, 1)
            for t in range(TILES):
                if t % TPB == 0:
                    pe.wait_ge(y_ready, START + t // TPB + 1)
                mm = nc.tensor.transpose(y_ps[t // 4][:, t % 4 * P:(t % 4 + 1) * P], core.xT[:, t * P:(t + 1) * P],
                                         core.ident[:])
                if t % 4 == 3:
                    mm.then_inc(y_turned, 1)

        @st.block.scalar
        def _(act):
            act.wait_ge(core.w_sem["l3_attn"], value)
            with act.Fori(0, CHUNKS // 2) as u:
                for s in range(2):
                    act.wait_ge(gate_ready, START + 2 * u + s + 1)
                    nc.scalar.activation(z[:, bass.ds((2 * u + s) * CH, CH)], gate_ps[s][:], ACT.Sigmoid, bias=bz
                                         ).then_inc(z_ready, 1)
            for i in range(B):
                act.wait_ge(h_ready, START + i + 1)
                nc.scalar.activation(z[:, i * S:(i + 1) * S], h[:, i * S:(i + 1) * S], ACT.Sigmoid, scale=beta
                                     ).then_inc(swish_ready, 1)
            for i in range(4):
                act.wait_ge(y_turned, START + i + 1)
                nc.scalar.activation(core.kept[:, 4 * i:4 * i + 4, :].rearrange("p t d -> p (t d)"), y_ps[i][:],
                                     ACT.Copy)

        @st.block.vector
        def _(dve):
            dve.wait_ge(core.w_sem["l3_attn"], value)
            with dve.Fori(0, CHUNKS // 2) as u:
                for s in range(2):
                    c = 2 * u + s
                    dve.wait_ge(z_ready, START + c + 1)
                    dve.wait_ge(value_ready, START + c + 1)
                    nc.vector.tensor_scalar(a[:, bass.ds(c * CH, CH)], z[:, bass.ds(c * CH, CH)], -1.0, 1.0, ALU.mult,
                                            ALU.add)
                    nc.vector.scalar_tensor_tensor(b[:, bass.ds(c * CH, CH)], value_ps[s][:], bh,
                                                   z[:, bass.ds(c * CH, CH)], op0=ALU.add, op1=ALU.mult
                                                   ).then_inc(b_ready, 1)
            dve.wait_ge(b_ready, START + CHUNKS)
            for i in range(B):
                part = slice(i * S, (i + 1) * S)
                nc.vector.tensor_tensor_scan(h[:, part], a[:, part], b[:, part], 0.0, ALU.mult, ALU.add
                                             ).then_inc(h_ready, 1)
            for i in range(B):
                part = slice(i * S, (i + 1) * S)
                dve.wait_ge(swish_ready, START + i + 1)
                nc.vector.scalar_tensor_tensor(core.xT[:, part], h[:, part], beta, z[:, part], op0=ALU.mult,
                                               op1=ALU.mult).then_inc(y_ready, 1)
    layer_norm_stats(core, core.kept, 1e-5, "stats")
    with core.stage("affine") as st:
        normed = [st.sb(f"normed{s}", [P, D]) for s in range(2)]
        scaled = [st.sb(f"scaled{s}", [P, D]) for s in range(2)]
        normed_ready, scaled_ready, moved, x_done = (st.sems("normed_ready", 2), st.sems("scaled_ready", 2),
                                                     st.sems("moved", 2), st.sems("x_done", 2))
        gamma, shift = w["l3_attn.affine_rep"][:, 0, :], w["l3_attn.affine_rep"][:, 1, :]

        @st.block.gpsimd
        def _(pool):
            with pool.Fori(0, TILES // 2) as u:
                for s in range(2):
                    nc.gpsimd.tensor_tensor(core.x[:, 2 * u + s, :], core.x[:, 2 * u + s, :], shift, ALU.add
                                            ).then_inc(moved[s], 1)

        @st.block.vector
        def _(dve):
            with dve.Fori(0, TILES // 2) as u:
                for s in range(2):
                    t = 2 * u + s
                    nc.vector.tensor_scalar(normed[s][:], core.kept[:, t, :], core.mean[:, bass.ds(t, 1)],
                                            core.rstd[:, bass.ds(t, 1)], ALU.subtract, ALU.mult
                                            ).then_inc(normed_ready[s], 1)
                for s in range(2):
                    dve.wait_ge(normed_ready[s], START + u + 1)
                    dve.wait_ge(x_done[s], START + u)
                    nc.vector.tensor_tensor(scaled[s][:], normed[s][:], gamma, ALU.mult).then_inc(scaled_ready[s], 1)
                for s in range(2):
                    dve.wait_ge(scaled_ready[s], START + u + 1)
                    dve.wait_ge(moved[s], START + u + 1)
                    nc.vector.tensor_tensor(core.x[:, 2 * u + s, :], core.x[:, 2 * u + s, :], scaled[s][:], ALU.add
                                            ).then_inc(x_done[s], 1)


SUBLAYERS = [l0_ffn, l0_attn, l0_ffn, l1_ffn, l1_attn, l1_ffn, l2_ffn, l2_attn, l2_ffn, l3_ffn, l3_attn, l3_ffn]
LOAD_SECOND = 5
LOAD_LAST = 6


def heads_beside_rolled(w, heads, rows):
    w = w.T.reshape(rows, heads, 64)
    both = np.concatenate([w, np.concatenate([w[:, :, 32:], w[:, :, :32]], 2)], 2)
    return np.concatenate([both, np.zeros((rows, 2, 128), w.dtype)], 1)


def rope_tables():
    f32 = np.float32
    inv = (f32(1.0) / (f32(10000.0) ** (np.arange(0, 64, 2, dtype=f32) / f32(64)))).astype(f32)
    angle = np.arange(S, dtype=f32)[None, :] * inv[:, None]
    cos, sin = np.cos(angle), np.sin(angle)
    full = np.concatenate([cos, cos, -sin, sin]).astype(f32)
    inv = (f32(1.0) / f32(10000.0) ** (np.arange(16, dtype=f32) * f32(2.0) / f32(32))).astype(f32)
    angle = np.arange(S, dtype=f32)[:, None] * inv[None, :]
    partial = np.stack([np.cos(angle), np.sin(angle)], 1).astype(f32)
    return full, partial.reshape(TPB, P, 2, 16).transpose(1, 0, 2, 3)


def lay_out(v):
    blocks = lambda w: w.reshape(w.shape[0], -1, P, w.shape[-1]).transpose(2, 0, 1, 3)
    full_rope, partial_rope = rope_tables()
    out = {"x": v["L0_attn_x"]}
    out["l0_ffn.wg"] = v["L0_ffn_Wg"]
    out["l0_ffn.bg_rep"] = v["L0_ffn_bg"][None]
    out["l0_ffn.w1"] = v["L0_ffn_W1"].transpose(1, 0, 2)
    out["l0_ffn.w2"] = blocks(v["L0_ffn_W2"])
    out["l0_ffn.b1"] = v["L0_ffn_b1"].reshape(6, 2, P).transpose(2, 0, 1)
    out["l0_ffn.b2_rep"] = v["L0_ffn_b2"][None]
    out["stream_l0.wq"] = heads_beside_rolled(v["L0_attn_wq"], 16, D).transpose(1, 0, 2)
    out["stream_l0.wk"] = heads_beside_rolled(v["L0_attn_w_k_up"], 16, 64).transpose(1, 0, 2)
    out["l0_attn.w_down"] = v["L0_attn_w_kv_down"].T
    out["l0_attn.w_v"] = np.concatenate([v["L0_attn_w_v_up"].T, np.zeros((64, 64), np.float32)], 1)
    halves = np.tile(np.eye(64, dtype=np.float32), (2, 2))
    out["l0_attn.add_halves"] = halves
    out["l0_attn.wo"] = v["L0_attn_wo"].T.reshape(8, P, D).transpose(1, 0, 2)
    out["l0_attn.rope"] = full_rope
    out["l1_ffn.m1"] = v["L1_ffn_m1"]
    out["l1_ffn.m2"] = np.concatenate([v["L1_ffn_m2"].reshape(64, 512), v["L1_ffn_mb"].reshape(1, 512)])
    out["l1_ffn.w1"] = v["L1_ffn_w1"].reshape(D, 512)
    out["l1_ffn.w2"] = v["L1_ffn_w2"].transpose(1, 0, 2).reshape(4, P, D).transpose(1, 0, 2)
    out["l1_ffn.b2_rep"] = v["L1_ffn_b2"][None]
    out["l1_attn.w_qc"] = v["L1_attn_w_qc"]
    out["l1_attn.w_qup"] = v["L1_attn_w_qup"]
    out["l1_attn.w_kv"] = np.concatenate([v["L1_attn_w_k"], v["L1_attn_w_v"]], 1)
    out["l1_attn.g_q_rep"] = v["L1_attn_g_qnorm"][None]
    out["l1_attn.g_k_rep"] = v["L1_attn_g_knorm"][None]
    query, block, key = np.arange(P), np.arange(32), np.arange(2 * P)
    tile = np.arange(TPB)
    position = tile[None, :, None] * P + query[:, None, None]
    out["l1_attn.block_mask"] = np.where((block + 1) * 32 - 1 <= position, 0.0, NEG).astype(np.float32)
    behind = query[:, None] + P - key[None, :]
    out["l1_attn.window_mask"] = np.where((behind >= 0) & (behind < 64), 0.0, NEG).astype(np.float32)
    out["l1_attn.block_mean"] = np.where(block == (4 * tile[None, :, None] + query[:, None, None] // 32), 1 / 32, 0.0
                                         ).astype(np.float32)
    out["l1_attn.w_gate"] = v["L1_attn_w_gate"]
    out["l1_attn.b_gate_rep"] = v["L1_attn_b_gate"][None]
    out["l1_attn.sink_rep"] = np.concatenate([v["L1_attn_sink_logit"], np.zeros(2, np.float32)])[None]
    group = v["L1_attn_w_out_group"]
    zeros = np.zeros((256, 64), group.dtype)
    diagonal = np.concatenate([np.concatenate([group[0], zeros], 1), np.concatenate([zeros, group[1]], 1)])
    out["l1_attn.w_group"] = diagonal.reshape(4, P, D).transpose(1, 0, 2)
    out["l1_attn.w_out"] = v["L1_attn_w_out"]
    cos, sin = partial_rope[:, :, 0], partial_rope[:, :, 1]
    out["l1_attn.rope"] = np.stack([np.stack([cos, sin], 2), np.stack([-sin, cos], 2)], 1).reshape(P, 2, TPB, 32)
    wkv = v["L2_attn_Wkv"]
    heads = np.concatenate([w.reshape(D, 16, 64) for w in (v["L2_attn_Wq"], wkv[:, :1024], wkv[:, 1024:])], 2)
    out["l2_attn.wqkv"] = np.concatenate([heads, np.zeros((D, 1, 192), heads.dtype)], 1)
    out["l2_attn.wo"] = v["L2_attn_Wo"].reshape(8, P, D).transpose(1, 0, 2)
    out["l2_attn.norm_w"] = v["L2_attn_norm_w"][:, None]
    out["l2_attn.gammas"] = np.stack([v["L2_attn_q_gamma"].T, v["L2_attn_k_gamma"].T], 1)
    out["l2_ffn.wg"] = v["L2_ffn_router_w"]
    out["l2_ffn.w1"] = v["L2_ffn_w1"].transpose(1, 0, 2)
    out["l2_ffn.w2"] = blocks(v["L2_ffn_w2"])
    out["l2_ffn.b1"] = v["L2_ffn_b1"].reshape(8, 4, P).transpose(2, 0, 1)
    out["l2_ffn.b2_rep"] = v["L2_ffn_b2"][None]
    out["l2_ffn.gamma_rep"] = v["L2_ffn_gamma"][None]
    out["l2_ffn.beta"] = v["L2_ffn_beta"]
    out["l3_attn.wz"] = v["L3_attn_Wz"]
    out["l3_attn.wh"] = v["L3_attn_Wh"]
    out["l3_attn.columns"] = np.stack([v["L3_attn_bz"], v["L3_attn_bh"]], 1)
    out["l3_attn.swish_rep"] = v["L3_attn_swish_beta"].reshape(1, 1)
    out["l3_attn.affine_rep"] = np.stack([v["L3_attn_ln_gamma"], v["L3_attn_ln_beta"]])[None]
    out["l3_ffn.columns"] = np.stack([v[f"L3_ffn_{n}"] for n in ("ln1_weight", "ln1_bias", "ln2_weight", "ln2_bias")], 1)
    out["l3_ffn.wqkv"] = v["L3_ffn_qkv_weight"].T
    out["l3_ffn.wproj"] = v["L3_ffn_proj_weight"].T
    out["l3_ffn.wg"] = v["L3_ffn_router_weight"].T
    out["l3_ffn.w1"] = v["L3_ffn_moe_w1"].transpose(1, 0, 2)
    out["l3_ffn.w2"] = blocks(v["L3_ffn_moe_w2"])
    return out


def store_everything(core, out):
    with core.stage("store") as st:
        stored = st.sem("stored")

        @st.block.sync
        def _(sp):
            sp.dma_start(out.rearrange("b (t p) d -> p (b t) d", p=P), core.x[:]).then_inc(stored, 16)
            sp.wait_ge(stored, START + 16)


def build(nc, a, out):
    with ExitStack() as ctx:
        core = Core(nc, ctx, a)
        used = {layer.__name__ for layer in SUBLAYERS}
        first, second, last = [[n for n in names if n in used] for names in (
            ["l0_ffn", "l0_attn", "l1_ffn", "l1_attn"], ["l2_ffn", "l2_attn"], ["l3_ffn", "l3_attn"])]
        size = lambda groups: sum(math.prod(ap.shape[1:]) for key, ap in a.items() if key.partition(".")[0] in groups)
        arena = core.sb("arena", [P, max(size(first), size(last), 1)])
        load_everything(core, core.place_weights(first, arena))
        for n, layer in enumerate(SUBLAYERS):
            if n == LOAD_SECOND:
                arena2 = core.sb("arena2", [P, max(size(second), 1)])
                load_weights(core, core.place_weights(second, arena2))
            if n == LOAD_LAST:
                load_weights(core, core.place_weights(last, arena))
            layer(core)
        store_everything(core, out)


def kernel(**inputs):
    import concourse.bacc as _bacc
    from concourse.bass_utils import run_bass_kernel_spmd as _run

    laid_out = lay_out({k: np.asarray(v) for k, v in inputs.items()})
    nc = _bacc.Bacc("TRN2", target_bir_lowering=False, num_devices=1)
    arrays, aps = {}, {}
    for name, array in laid_out.items():
        arrays[f"in_{name.replace('.', '_')}"] = np.ascontiguousarray(array)
        aps[name] = nc.dram_tensor(f"in_{name.replace('.', '_')}", array.shape, mybir.dt.from_np(array.dtype),
                                   kind="ExternalInput").ap()
    out = nc.dram_tensor("out_tokens", (B, S, D), FP32, kind="ExternalOutput").ap()
    build(nc, aps, out)
    return _run(nc, [arrays], core_ids=[0]).results[0]["out_tokens"]
```

```python
import math
from contextlib import ExitStack, contextmanager

import numpy as np

import concourse.bass as bass
from concourse import mybir

FP32 = mybir.dt.float32
BF16 = mybir.dt.bfloat16
U32 = mybir.dt.uint32
ALU = mybir.AluOpType
ACT = mybir.ActivationFunctionType
AX = mybir.AxisListType

P = 128
D = 128
B, S = 2, 1024
TOKENS = B * S
TILES = TOKENS // P
TPB = S // P
CH = 512
CHUNKS = TOKENS // CH
SUB = CH // P
NEG = -1e30
STAGE_SEMAPHORES = 120
START = 1


class Steps:

    def __init__(self, eng, sem):
        self.eng, self.sem, self.n, self.base = eng, sem, 0, 0

    def done(self, instruction):
        instruction.then_inc(self.sem, 1)
        self.n += 1
        self.eng.wait_ge(self.sem, START + self.base + self.n)

    @contextmanager
    def loop(self, count, per_turn):
        before, outer, start = self.n, self.base, self.n
        with self.eng.Fori(0, count) as i:
            self.base, self.n = outer + i * per_turn, before
            yield i
            assert self.n - before == per_turn, f"{self.n - before} steps in a turn, not {per_turn}"
        self.base, self.n = outer, start + count * per_turn


class Stage:

    def __init__(self, nc, ctx, name, cleared):
        self.nc, self.ctx, self.name, self.cleared, self.semaphores = nc, ctx, name, cleared, []

    def sb(self, name, shape, dt=FP32):
        return self.ctx.enter_context(self.nc.sbuf_tensor(self.name + name, shape, dt))

    def bank(self, name, columns=512):
        return self.ctx.enter_context(self.nc.psum_tensor(self.name + name, [P, columns], FP32))

    def sem(self, name):
        self.semaphores.append(self.cleared.pop(0))
        return self.semaphores[-1]

    def sems(self, name, n):
        return [self.sem(f"{name}{i}") for i in range(n)]


class Core:

    def __init__(self, nc, ctx, args):
        self.nc, self.ctx, self.a = nc, ctx, args
        self.x = self.sb("x_tokens", [P, TILES, D])
        self.kept = self.sb("kept_tokens", [P, TILES, D])
        self.xT = self.sb("xT", [P, TOKENS])
        self.ident = self.sb("ident", [P, P])
        self.ident16 = self.sb("ident16", [P, P], BF16)
        self.causal16 = self.sb("causal16", [P, P], BF16)
        self.w, self.w_sem, self.w_value = {}, {}, {}
        self.mean = self.sb("ln_mean", [P, TILES])
        self.rstd = self.sb("ln_rstd", [P, TILES])
        self.iota8 = self.sb("iota8", [P, TILES, 8])
        self.logits = self.sb("logits", [P, TILES, 8])
        self.gates = self.sb("gates", [P, TILES, 8])
        self.stages = 0
        self.cleared = [self.sem(f"stage_sem{i}") for i in range(STAGE_SEMAPHORES)]
        for semaphore in self.cleared:
            nc.gpsimd.sem_inc(semaphore, START)
        with nc.Block():
            pass
        self.just_cleared = []

    def sb(self, name, shape, dt=FP32, ctx=None):
        return (ctx or self.ctx).enter_context(self.nc.sbuf_tensor(name, shape, dt))

    def sem(self, name, ctx=None):
        return (ctx or self.ctx).enter_context(self.nc.semaphore(name))

    @contextmanager
    def stage(self, tag):
        self.stages += 1
        name = f"{tag}{self.stages}_"
        with ExitStack() as ctx:
            st = Stage(self.nc, ctx, name, self.cleared)
            with self.nc.Block() as st.block:
                yield st
        for semaphore in st.semaphores:
            self.nc.gpsimd.sem_clear(semaphore)
            self.nc.gpsimd.sem_inc(semaphore, START)
        self.cleared += self.just_cleared
        self.just_cleared = st.semaphores

    def place_weights(self, groups, arena):
        loads, at = [], 0
        for key, src in self.a.items():
            group, _, name = key.partition(".")
            if group not in groups:
                continue
            shape = list(src.shape)
            if name.endswith("_rep"):
                shape[0] = P
                src = src.to_broadcast(shape)
            size = math.prod(shape[1:])
            view = arena[0:shape[0], at:at + size]
            at += size
            if len(shape) == 3:
                view = view.rearrange("p (a b) -> p a b", a=shape[1])
            elif len(shape) == 4:
                view = view.rearrange("p (a b c) -> p a b c", a=shape[1], b=shape[2])
            if group not in self.w_sem:
                self.w_sem[group], self.w_value[group] = self.sem(group + "_loaded"), 0
            self.w_value[group] += 16
            self.w[key] = view
            loads.append((view, src, self.w_sem[group]))
        return loads


def load_everything(core, loads):
    nc, a = core.nc, core.a
    with core.stage("load") as st:
        x_loaded = st.sem("x_loaded")
        made = st.sem("constants_made")

        @st.block.sync
        def _(sp):
            sp.dma_start(core.x[:], a["x"].rearrange("b (t p) d -> p (b t) d", p=P)).then_inc(x_loaded, 16)
            for dst, src, sem in loads:
                sp.dma_start(dst, src).then_inc(sem, 16)
            sp.wait_ge(x_loaded, START + 16)

        @st.block.gpsimd
        def _(pool):
            nc.gpsimd.memset(core.ident[:], 0.0)
            nc.gpsimd.memset(core.ident16[:], 0.0)
            nc.gpsimd.memset(core.causal16[:], 0.0)
            nc.gpsimd.memset(core.logits[:], -3e38).then_inc(made, 1)
            pool.wait_ge(made, START + 1)
            nc.gpsimd.affine_select(out=core.ident[:], in_=core.ident[:], compare_op=ALU.not_equal, fill=1.0,
                                    base=0, pattern=[[-1, P]], channel_multiplier=1).then_inc(made, 1)
            nc.gpsimd.affine_select(out=core.ident16[:], in_=core.ident16[:], compare_op=ALU.not_equal, fill=1.0,
                                    base=0, pattern=[[-1, P]], channel_multiplier=1).then_inc(made, 1)
            nc.gpsimd.affine_select(out=core.causal16[:], in_=core.causal16[:], compare_op=ALU.is_ge, fill=NEG,
                                    base=0, pattern=[[-1, P]], channel_multiplier=1).then_inc(made, 1)
            nc.gpsimd.iota(core.iota8[:], pattern=[[0, TILES], [1, 8]], base=0, channel_multiplier=0,
                           allow_small_or_imprecise_dtypes=True).then_inc(made, 1)
            pool.wait_ge(made, START + 5)


def load_weights(core, loads):
    with core.stage("load") as st:
        @st.block.sync
        def _(sp):
            for dst, src, sem in loads:
                sp.dma_start(dst, src).then_inc(sem, 16)


def token_statistics(nc, step, src, eps, bn, work, mean, rstd, stats_done, variance_ready, root_ready, rms_eps=None):
    dve = step.eng
    for t in range(TILES):
        nc.vector.bn_stats(bn[:, t, :], src[:, t, :]).then_inc(stats_done, 1)
    dve.wait_ge(stats_done, START + TILES)
    nc.vector.tensor_tensor(work[:, 0, :], bn[:, :, 1], bn[:, :, 4], ALU.add)
    nc.vector.tensor_tensor(work[:, 1, :], bn[:, :, 1], bn[:, :, 4], ALU.subtract)
    step.done(nc.vector.tensor_tensor(work[:, 2, :], bn[:, :, 2], bn[:, :, 5], ALU.add))
    nc.vector.tensor_scalar(mean, work[:, 0, :], 0.5, None, ALU.mult)
    nc.vector.tensor_scalar(work[:, 2, :], work[:, 2, :], 1.0 / D, None, ALU.mult)
    step.done(nc.vector.scalar_tensor_tensor(work[:, 3, :], work[:, 1, :], 0.25, work[:, 1, :],
                                             op0=ALU.mult, op1=ALU.mult))
    nc.vector.scalar_tensor_tensor(work[:, 4, :], work[:, 2, :], eps, work[:, 3, :], op0=ALU.add, op1=ALU.add
                                   ).then_inc(variance_ready, 1)
    if rms_eps is None:
        dve.wait_ge(root_ready, START + 1)
        step.done(nc.vector.reciprocal(rstd, work[:, 5, :]))
        return
    step.done(nc.vector.tensor_tensor(work[:, 3, :], work[:, 2, :], work[:, 3, :], ALU.add))
    step.done(nc.vector.reciprocal(work[:, 0, :], work[:, 4, :]))
    step.done(nc.vector.tensor_tensor(work[:, 0, :], work[:, 0, :], work[:, 3, :], ALU.mult))
    nc.vector.tensor_scalar(work[:, 7, :], work[:, 0, :], rms_eps, None, ALU.add).then_inc(variance_ready, 1)
    dve.wait_ge(root_ready, START + 2)
    step.done(nc.vector.tensor_tensor(work[:, 0, :], work[:, 5, :], work[:, 6, :], ALU.mult))
    step.done(nc.vector.reciprocal(rstd, work[:, 0, :]))


def root_of_variances(nc, act, work, variance_ready, root_ready, rms_eps=None):
    for k in range(1 if rms_eps is None else 2):
        act.wait_ge(variance_ready, START + k + 1)
        nc.scalar.activation(work[:, 5 + k, :], work[:, 7 if k else 4, :], ACT.Sqrt).then_inc(root_ready, 1)


def layer_norm_stats(core, src, eps, tag):
    nc = core.nc
    with core.stage(tag) as st:
        bn = st.sb("bn", [P, TILES, 6])
        work = st.sb("work", [P, 8, TILES])
        stats_done, steps_done = st.sem("stats_done"), st.sem("steps_done")
        variance_ready, root_ready = st.sem("variance_ready"), st.sem("root_ready")

        @st.block.vector
        def _(dve):
            token_statistics(nc, Steps(dve, steps_done), src, eps, bn, work, core.mean[:], core.rstd[:], stats_done,
                             variance_ready, root_ready)

        @st.block.scalar
        def _(act):
            root_of_variances(nc, act, work, variance_ready, root_ready)


def layer_norm_and_transpose(core, src, eps, tag, keep=False, keep_plain=False, gain=None, shift=None,
                             small=None, gain_sem=None, gain_value=0, rms_eps=None):
    nc = core.nc
    with core.stage(tag) as st:
        bn = st.sb("bn", [P, TILES, 6])
        work = st.sb("work", [P, 8, TILES])
        normed = core.kept if keep else st.sb("normed", [P, TILES, D])
        turned = [st.bank(f"turned{s}") for s in range(2)]
        stats_done, steps_done = st.sem("stats_done"), st.sem("steps_done")
        variance_ready, root_ready = st.sem("variance_ready"), st.sem("root_ready")
        normed_ready, turned_ready, stored = st.sem("normed_ready"), st.sem("turned_ready"), st.sem("stored")
        product_ready, product_read = st.sem("product_ready"), st.sem("product_read")
        if small:
            weights, bias, small_out, small_sem, small_value = small
            n = weights.shape[-1]
            per_bank = min(TILES, 1 << (CH // n).bit_length() - 1)
            product = [st.bank(f"product{k}") for k in range(min(4, TILES // per_bank))]

        @st.block.vector
        def _(dve):
            step = Steps(dve, steps_done)
            token_statistics(nc, step, src, eps, bn, work, core.mean[:], core.rstd[:], stats_done, variance_ready,
                             root_ready, rms_eps)
            for t in range(TILES):
                ins = nc.vector.tensor_scalar(normed[:, t, :], src[:, t, :], core.mean[:, t:t + 1],
                                              core.rstd[:, t:t + 1], ALU.subtract, ALU.mult)
                if t % SUB == SUB - 1:
                    ins.then_inc(normed_ready, 1)
            if keep_plain:
                step.done(nc.vector.reciprocal(work[:, 0, :], work[:, 5, :]))
                for t in range(TILES):
                    nc.vector.tensor_scalar(core.kept[:, t, :], src[:, t, :], core.mean[:, t:t + 1],
                                            work[:, 0, t:t + 1], ALU.subtract, ALU.mult)
            if small:
                dve.wait_ge(small_sem, small_value)
                for k in range(TILES // per_bank):
                    dve.wait_ge(product_ready, START + k + 1)
                    columns = product[k % len(product)][:, :per_bank * n].rearrange("p (t n) -> p t n", n=n)
                    into = small_out[:, k * per_bank:(k + 1) * per_bank, 0:n]
                    if bias is None:
                        ins = nc.vector.tensor_copy(into, columns)
                    else:
                        ins = nc.vector.tensor_tensor(into, columns, bias.unsqueeze(1).to_broadcast([P, per_bank, n]),
                                                      ALU.add)
                    ins.then_inc(product_read, 1)

        @st.block.tensor
        def _(pe):
            if small:
                pe.wait_ge(small_sem, small_value)

            def multiply(c):
                pe.wait_ge(stored, START + c + 1)
                for t in range(c * SUB, (c + 1) * SUB):
                    k, i = divmod(t, per_bank)
                    if i == 0 and k >= len(product):
                        pe.wait_ge(product_read, START + k - len(product) + 1)
                    mm = nc.tensor.matmul(product[k % len(product)][:, i * n:(i + 1) * n],
                                          core.xT[:, t * P:(t + 1) * P], weights, start=True, stop=True)
                    if i == per_bank - 1:
                        mm.then_inc(product_ready, 1)

            for c in range(CHUNKS):
                pe.wait_ge(normed_ready, START + c + 1)
                if c >= 2:
                    pe.wait_ge(stored, START + c - 1)
                for i in range(SUB):
                    mm = nc.tensor.transpose(turned[c % 2][:, i * P:(i + 1) * P], normed[:, c * SUB + i, :],
                                             core.ident[:])
                mm.then_inc(turned_ready, 1)
                if small and c >= 1:
                    multiply(c - 1)
            if small:
                multiply(CHUNKS - 1)

        @st.block.scalar
        def _(act):
            root_of_variances(nc, act, work, variance_ready, root_ready, rms_eps)
            if gain_sem is not None:
                act.wait_ge(gain_sem, gain_value)
            for c in range(CHUNKS):
                act.wait_ge(turned_ready, START + c + 1)
                part = core.xT[:, c * CH:(c + 1) * CH]
                if gain is not None:
                    ins = nc.scalar.activation(part, turned[c % 2][:], ACT.Identity, bias=shift, scale=gain)
                else:
                    ins = nc.scalar.activation(part, turned[c % 2][:], ACT.Copy)
                ins.then_inc(stored, 1)


def top2_gates(core, tag, experts, softmax_over_all):
    nc = core.nc
    with core.stage(tag) as st:
        best = st.sb("best", [P, TILES, 8])
        place = st.sb("place", [P, TILES, 8], U32)
        place_f = st.sb("place_f", [P, TILES, 2])
        hot = st.sb("hot", [P, 2, TILES, 8])
        w = st.sb("w", [P, 4, TILES])
        e = st.sb("e", [P, TILES, 8])
        steps_done, to_exp, exp_done = st.sem("steps_done"), st.sem("to_exp"), st.sem("exp_done")
        full = [P, TILES, 8]
        per_token = lambda ap: ap.unsqueeze(2).to_broadcast(full)

        @st.block.vector
        def _(dve):
            step = Steps(dve, steps_done)
            scores = core.logits
            if softmax_over_all:
                step.done(nc.vector.tensor_reduce(w[:, 0, :], core.logits[:], AX.X, ALU.max))
                nc.vector.tensor_tensor(e[:], core.logits[:], per_token(w[:, 0, :]), ALU.subtract).then_inc(to_exp, 1)
                dve.wait_ge(exp_done, START + 1)
                step.done(nc.vector.tensor_reduce(w[:, 1, :], e[:], AX.X, ALU.add))
                step.done(nc.vector.reciprocal(w[:, 2, :], w[:, 1, :]))
                step.done(nc.vector.tensor_tensor(e[:], e[:], per_token(w[:, 2, :]), ALU.mult))
                scores = e
            for t in range(TILES):
                ins = nc.vector.max(best[:, t, :], scores[:, t, :])
            step.done(ins)
            for t in range(TILES):
                ins = nc.vector.max_index(place[:, t, :], best[:, t, :], scores[:, t, :])
            step.done(ins)
            if softmax_over_all:
                nc.vector.tensor_scalar(w[:, 2, :], best[:, :, 0], 0.5, None, ALU.mult)
                nc.vector.tensor_scalar(w[:, 3, :], best[:, :, 1], 0.5, None, ALU.mult)
            else:
                nc.vector.tensor_tensor(w[:, 0, :], best[:, :, 1], best[:, :, 0], ALU.subtract).then_inc(to_exp, 1)
                dve.wait_ge(exp_done, START + 1)
                step.done(nc.vector.tensor_scalar(w[:, 0, :], w[:, 1, :], 1.0, 2.0, ALU.add, ALU.mult))
                step.done(nc.vector.reciprocal(w[:, 2, :], w[:, 0, :]))
                nc.vector.tensor_tensor(w[:, 3, :], w[:, 1, :], w[:, 2, :], ALU.mult)
            step.done(nc.vector.tensor_copy(place_f[:], place[:, :, 0:2]))
            for k in range(2):
                ins = nc.vector.tensor_tensor(hot[:, k], core.iota8[:], per_token(place_f[:, :, k]), ALU.is_equal)
            step.done(ins)
            for k in range(2):
                ins = nc.vector.tensor_tensor(hot[:, k], hot[:, k], per_token(w[:, 2 + k, :]), ALU.mult)
            step.done(ins)
            step.done(nc.vector.tensor_tensor(core.gates[:], hot[:, 0], hot[:, 1], ALU.add))

        @st.block.scalar
        def _(act):
            act.wait_ge(to_exp, START + 1)
            if softmax_over_all:
                nc.scalar.activation(e[:], e[:], ACT.Exp).then_inc(exp_done, 1)
            else:
                nc.scalar.activation(w[:, 1, :], w[:, 0, :], ACT.Exp).then_inc(exp_done, 1)


def experts_ffn(core, tag, experts, hidden, function, w1, w2, weights_sem, weights_value, b1=None, b2=None,
                normed=None):
    nc = core.nc
    blocks = hidden // P
    per_chunk = experts * blocks
    assert per_chunk % 4 == 0 and experts % 2 == 0
    with core.stage(tag) as st:
        hidden_ps = [st.bank(f"hidden_ps{i}") for i in range(4)]
        out_ps = [st.bank(f"out_ps{i}") for i in range(2)]
        hT = [st.sb(f"hT{i}", [P, blocks, CH]) for i in range(2)]
        hidden_ready, hidden_active = st.sem("hidden_ready"), st.sem("hidden_active")
        out_ready, out_read = st.sem("out_ready"), st.sem("out_read")
        added = st.sem("added")

        @st.block.tensor
        def _(pe):
            pe.wait_ge(weights_sem, weights_value)
            with pe.Fori(0, CHUNKS) as c:
                def up(e):
                    for f in range(blocks):
                        k = e * blocks + f
                        pe.wait_ge(hidden_active, START + c * per_chunk + (k - 3 if k >= 4 else 0))
                        nc.tensor.matmul(hidden_ps[k % 4][:], w1[:, e, f * P:(f + 1) * P],
                                         core.xT[:, bass.ds(c * CH, CH)], start=True, stop=True
                                         ).then_inc(hidden_ready, 1)

                def down(e):
                    pe.wait_ge(hidden_active, START + c * per_chunk + (e + 1) * blocks)
                    pe.wait_ge(out_read, START + c * experts + (e - 1 if e >= 2 else 0))
                    for sub in range(SUB):
                        for f in range(blocks):
                            mm = nc.tensor.matmul(out_ps[e % 2][:, sub * P:(sub + 1) * P],
                                                  hT[e % 2][:, f, sub * P:(sub + 1) * P], w2[:, e, f, :],
                                                  start=f == 0, stop=f == blocks - 1)
                    mm.then_inc(out_ready, 1)

                up(0)
                for e in range(experts):
                    if e + 1 < experts:
                        up(e + 1)
                    down(e)

        if normed is None:
            plain_consumer(core, st, experts, out_ps, out_ready, out_read, added, b2, weights_sem, weights_value)
        else:
            normed_consumer(core, st, experts, out_ps, out_ready, out_read, added, b2, weights_sem,
                            weights_value, *normed)

        @st.block.scalar
        def _(act):
            if b1 is not None:
                act.wait_ge(weights_sem, weights_value)

            def root(number):
                variance, variance_ready, root_ready = core.root_of_variance
                act.wait_ge(variance_ready, START + number + 1)
                nc.scalar.activation(variance[:, 5, :], variance[:, 4, :], ACT.Sqrt).then_inc(root_ready, 1)

            with act.Fori(0, CHUNKS) as c:
                for e in range(experts):
                    act.wait_ge(out_ready, START + c * experts + (e - 1 if e >= 2 else 0))
                    for f in range(blocks):
                        k = e * blocks + f
                        act.wait_ge(hidden_ready, START + c * per_chunk + k + 1)
                        nc.scalar.activation(hT[e % 2][:, f, :], hidden_ps[k % 4][:], function,
                                             bias=0.0 if b1 is None else b1[:, e, f:f + 1]
                                             ).then_inc(hidden_active, 1)
                    if normed is not None and e + 1 == late_root(experts):
                        root(2 * c)
                if normed is not None:
                    root(2 * c + 1)


def plain_consumer(core, st, experts, out_ps, out_ready, out_read, added, b2, weights_sem, weights_value):
    nc = core.nc
    biased = [st.sb(f"biased{i}", [P, SUB, D]) for i in range(2)]

    @st.block.vector
    def _(dve):
        if b2 is not None:
            dve.wait_ge(weights_sem, weights_value)
        with dve.Fori(0, CHUNKS) as c:
            for e in range(experts):
                dve.wait_ge(out_ready, START + c * experts + e + 1)
                out = out_ps[e % 2][:].rearrange("p (s d) -> p s d", s=SUB)
                if b2 is not None:
                    nc.vector.tensor_tensor(biased[e % 2][:], out, b2[:, e, :].unsqueeze(1).to_broadcast([P, SUB, D]),
                                            ALU.add).then_inc(out_read, 1)
                    dve.wait_ge(out_read, START + c * experts + e + 1)
                    out = biased[e % 2]
                dve.wait_ge(added if b2 is not None else out_read, START + c * experts + e)
                for sub in range(SUB):
                    tile = c * SUB + sub
                    last = nc.vector.scalar_tensor_tensor(core.x[:, bass.ds(tile, 1), :], out[:, sub:sub + 1, :],
                                                          core.gates[:, bass.ds(tile, 1), e],
                                                          core.x[:, bass.ds(tile, 1), :], op0=ALU.mult, op1=ALU.add)
                last.then_inc(added if b2 is not None else out_read, 1)


def late_root(experts):
    return experts // 2 + 2


def normed_consumer(core, st, experts, out_ps, out_ready, out_read, added, b2, weights_sem, weights_value,
                    gamma, eps):
    nc = core.nc
    half = experts // 2
    n = half * SUB
    with_bias = [st.sb(f"with_bias{i}", [P, SUB, D]) for i in range(2)]
    result = st.sb("result", [P, half, SUB, D])
    scaled = [st.sb(f"scaled{i}", [P, SUB, D]) for i in range(2)]
    bn = st.sb("bn", [P, n, 6])
    w = st.sb("w", [P, 8, n])
    bias_added, passed, steps_done = st.sem("bias_added"), st.sem("passed"), st.sem("steps_done")
    variance_ready, root_ready = st.sem("variance_ready"), st.sem("root_ready")
    core.root_of_variance = (w, variance_ready, root_ready)

    @st.block.gpsimd
    def _(pool):
        pool.wait_ge(weights_sem, weights_value)
        with pool.Fori(0, CHUNKS) as c:
            for e in range(experts):
                pool.wait_ge(out_read, START + c * experts + (e - 1 if e >= 2 else 0))
                pool.sem_inc(passed, 1)
                nc.gpsimd.tensor_tensor(with_bias[e % 2][:], core.kept[:, bass.ds(c * SUB, SUB), :],
                                        b2[:, e, :].unsqueeze(1).to_broadcast([P, SUB, D]), ALU.add
                                        ).then_inc(bias_added, 1)

    @st.block.vector
    def _(dve):
        step = Steps(dve, steps_done)
        dve.wait_ge(weights_sem, weights_value)
        with step.loop(CHUNKS, 2 * (5 + 2 * half)) as c:
            for e in range(experts):
                k = e % half
                dve.wait_ge(out_ready, START + c * experts + e + 1)
                dve.wait_ge(bias_added, START + c * experts + e + 1)
                nc.vector.tensor_tensor(result[:, k], out_ps[e % 2][:].rearrange("p (s d) -> p s d", s=SUB),
                                        with_bias[e % 2][:], ALU.add).then_inc(out_read, 1)
                dve.wait_ge(out_read, START + c * experts + e + 1)
                for sub in range(SUB):
                    ins = nc.vector.bn_stats(bn[:, k * SUB + sub, :], result[:, k, sub, :])
                if k < half - 1:
                    continue
                first = e + 1 - half
                step.done(ins)
                nc.vector.tensor_tensor(w[:, 1, :], bn[:, :, 1], bn[:, :, 4], ALU.add)
                nc.vector.tensor_tensor(w[:, 2, :], bn[:, :, 1], bn[:, :, 4], ALU.subtract)
                step.done(nc.vector.tensor_tensor(w[:, 3, :], bn[:, :, 2], bn[:, :, 5], ALU.add))
                nc.vector.tensor_scalar(w[:, 0, :], w[:, 1, :], 0.5, None, ALU.mult)
                nc.vector.tensor_scalar(w[:, 4, :], w[:, 3, :], 1.0 / D, eps, ALU.mult, ALU.add)
                step.done(nc.vector.scalar_tensor_tensor(w[:, 5, :], w[:, 2, :], 0.25, w[:, 2, :],
                                                         op0=ALU.mult, op1=ALU.mult))
                nc.vector.tensor_tensor(w[:, 4, :], w[:, 4, :], w[:, 5, :], ALU.add).then_inc(variance_ready, 1)
                dve.wait_ge(root_ready, START + 2 * c + first // half + 1)
                step.done(nc.vector.reciprocal(w[:, 6, :], w[:, 5, :]))
                step.done(nc.vector.tensor_tensor(
                    w[:, 7, :].rearrange("p (e s) -> p e s", s=SUB), w[:, 6, :].rearrange("p (e s) -> p e s", s=SUB),
                    core.gates[:, bass.ds(c * SUB, SUB), first:first + half].rearrange("p s e -> p e s"), ALU.mult))
                for j in range(half):
                    for sub in range(SUB):
                        m = j * SUB + sub
                        ins = nc.vector.tensor_scalar(scaled[j % 2][:, sub, :], result[:, j, sub, :], w[:, 0, m:m + 1],
                                                      w[:, 7, m:m + 1], ALU.subtract, ALU.mult)
                    step.done(ins)
                    step.done(nc.vector.tensor_tensor(scaled[j % 2][:], scaled[j % 2][:],
                                                      gamma[:, first + j, :].unsqueeze(1).to_broadcast([P, SUB, D]), ALU.mult))
                    nc.vector.tensor_tensor(core.x[:, bass.ds(c * SUB, SUB), :], core.x[:, bass.ds(c * SUB, SUB), :],
                                            scaled[j % 2][:], ALU.add).then_inc(added, 1)


def add_gated_rows(core, tag, rows, weights_sem, weights_value):
    nc = core.nc
    with core.stage(tag) as st:
        gateT = st.sb("gateT", [8, TOKENS])
        turned = [st.bank(f"turned{s}") for s in range(2)]
        product = [st.bank(f"product{s}") for s in range(2)]
        turned_ready, stored, product_ready, added = (st.sem("turned_ready"), st.sem("stored"),
                                                      st.sem("product_ready"), st.sem("added"))

        @st.block.tensor
        def _(pe):
            pe.wait_ge(weights_sem, weights_value)
            for c in range(CHUNKS + 1):
                if c < CHUNKS:
                    if c >= 2:
                        pe.wait_ge(stored, START + c - 1)
                    for i in range(SUB):
                        mm = nc.tensor.transpose(turned[c % 2][0:8, i * P:(i + 1) * P],
                                                 core.gates[:, c * SUB + i, :], core.ident[:])
                    mm.then_inc(turned_ready, 1)
                if c >= 1:
                    pe.wait_ge(stored, START + c)
                    if c >= 3:
                        pe.wait_ge(added, START + c - 2)
                    for i in range(SUB):
                        t = (c - 1) * SUB + i
                        mm = nc.tensor.matmul(product[(c - 1) % 2][:, i * D:(i + 1) * D], gateT[:, t * P:(t + 1) * P],
                                              rows, start=True, stop=True)
                    mm.then_inc(product_ready, 1)

        @st.block.scalar
        def _(act):
            for c in range(CHUNKS):
                act.wait_ge(turned_ready, START + c + 1)
                nc.scalar.activation(gateT[:, c * CH:(c + 1) * CH], turned[c % 2][0:8, :], ACT.Copy).then_inc(stored, 1)

        @st.block.vector
        def _(dve):
            for c in range(CHUNKS):
                dve.wait_ge(product_ready, START + c + 1)
                x = core.x[:, c * SUB:(c + 1) * SUB, :]
                nc.vector.tensor_tensor(x, product[c % 2][:].rearrange("p (t d) -> p t d", t=SUB), x, ALU.add
                                        ).then_inc(added, 1)


def project_tokens(core, tag, src, tiles, weights, weights_sem, weights_value, out_tiles):
    nc = core.nc
    n = weights.shape[1]
    banks, groups = tiles * n // 4, tiles // SUB
    with core.stage(tag) as st:
        turned_sb = [st.sb(f"turned_sb{i}", [P, 4, P]) for i in range(4)]
        turned = [st.bank(f"turned{i}") for i in range(4)]
        product = [st.bank(f"product{i}") for i in range(2)]
        turned_ready, stored = st.sem("turned_ready"), st.sems("stored", 2)
        used, added = st.sem("used"), st.sem("added")

        def store(eng, b):
            eng.wait_ge(turned_ready, START + b + 1)
            if b >= 4:
                eng.wait_ge(used, START + b - 3)
            into, bank = turned_sb[b % 4][:].rearrange("p k d -> p (k d)"), turned[b % 4][:]
            if b % 2 == 0:
                nc.scalar.activation(into, bank, ACT.Copy).then_inc(stored[0], 1)
            else:
                nc.vector.tensor_copy(into, bank).then_inc(stored[1], 1)

        @st.block.tensor
        def _(pe):
            pe.wait_ge(weights_sem, weights_value)

            def multiply(b):
                pe.wait_ge(stored[b % 2], START + b // 2 + 1)
                for i in range(4):
                    t, k = divmod(4 * b + i, n)
                    if k == 0 and t % SUB == 0 and t // SUB >= 2:
                        pe.wait_ge(added, START + t // SUB - 1)
                    mm = nc.tensor.matmul(product[t // SUB % 2][:, t % SUB * D:(t % SUB + 1) * D],
                                          turned_sb[b % 4][:, i, :], weights[:, k, :], start=k == 0, stop=k == n - 1)
                mm.then_inc(used, 1)

            for b in range(banks):
                if b >= 4:
                    pe.wait_ge(stored[b % 2], START + b // 2 - 1)
                for i in range(4):
                    t, k = divmod(4 * b + i, n)
                    mm = nc.tensor.transpose(turned[b % 4][:, i * P:(i + 1) * P], src[:, t, k * P:(k + 1) * P],
                                             core.ident[:])
                mm.then_inc(turned_ready, 1)
                if b >= 1:
                    multiply(b - 1)
            multiply(banks - 1)

        @st.block.scalar
        def _(act):
            for b in range(0, banks, 2):
                store(act, b)

        @st.block.vector
        def _(dve):
            def add(g):
                dve.wait_ge(used, START + (g + 1) * n)
                out = out_tiles(g * SUB, (g + 1) * SUB)
                nc.vector.tensor_tensor(out, product[g % 2][:].rearrange("p (t d) -> p t d", t=SUB), out, ALU.add
                                        ).then_inc(added, 1)

            done = 0
            for b in range(1, banks, 2):
                store(dve, b)
                if b >= (done + 1) * n + 1:
                    add(done)
                    done += 1
            for g in range(done, groups):
                add(g)


def l0_ffn(core):
    w, sem, value = core.w, core.w_sem["l0_ffn"], core.w_value["l0_ffn"]
    layer_norm_and_transpose(core, core.x, 1e-5, "norm",
                            small=(w["l0_ffn.wg"], w["l0_ffn.bg_rep"], core.logits, sem, value))
    top2_gates(core, "gates", 6, softmax_over_all=False)
    experts_ffn(core, "ffn", 6, 256, ACT.Gelu, w["l0_ffn.w1"], w["l0_ffn.w2"], sem, value,
                b1=w["l0_ffn.b1"], b2=w["l0_ffn.b2_rep"])


def l0_attn(core):
    w, sem, value = core.w, core.w_sem["l0_attn"], core.w_value["l0_attn"]
    heads, hd = 16, 64
    layer_norm_and_transpose(core, core.x, 1e-5, "norm")
    for b in range(B):
        with ExitStack() as ctx:
            mixed = core.sb(f"mixed{core.stages}", [P, TPB, heads * hd], ctx=ctx)
            latent_attention(core, b, mixed, heads, hd)
            project_tokens(core, "wo", mixed, TPB, w["l0_attn.wo"], sem, value,
                           lambda t, end: core.x[:, b * TPB + t:b * TPB + end, :])


def latent_attention(core, b, mixed, heads, hd):
    nc, w, sem, value = core.nc, core.w, core.w_sem["l0_attn"], core.w_value["l0_attn"]
    halves = S // CH
    with core.stage("l0attn") as st:
        latT = st.sb("latT", [hd, S])
        wq = [st.sb(f"wq{i}", [D, 2 * hd]) for i in range(2)]
        wk = [st.sb(f"wk{i}", [hd, 2 * hd]) for i in range(2)]
        qT = [st.sb(f"qT{i}", [hd, S]) for i in range(2)]
        kT = [st.sb(f"kT{i}", [hd, S]) for i in range(2)]
        parts = [st.sb(f"part{i}", [hd, CH]) for i in range(2)]
        v = [st.sb(f"v{i}", [P, TPB, hd]) for i in range(2)]
        probs = [st.sb(f"probs{i}", [P, S]) for i in range(2)]
        probsT = [st.sb(f"probsT{i}", [P, TPB, P]) for i in range(2)]
        neg_max = st.sb("neg_max", [P, 4])
        total = st.sb("total", [P, 4])
        inverse = st.sb("inverse", [P, 4])
        scores_ps = [st.bank(f"scores_ps{i}", S) for i in range(2)]
        side_ps, out_ps = st.bank("side_ps"), st.bank("out_ps")
        turned_ps = [st.bank(f"turned_ps{i}") for i in range(2)]
        loaded = st.sems("loaded", 2)
        lat_ready, lat_stored = st.sem("lat_ready"), st.sem("lat_stored")
        side_ready, side_read = st.sem("side_ready"), st.sem("side_read")
        added = st.sem("added")
        scores_ready, max_ready, probs_ready = st.sem("scores_ready"), st.sem("max_ready"), st.sem("probs_ready")
        turned, stored = st.sem("turned"), st.sem("stored")
        out_ready, inverted, out_read, passed = (st.sem("out_ready"), st.sem("inverted"), st.sem("out_read"),
                                                 st.sem("passed"))
        side_steps = 5
        at_unit = [[], [], [0], [1], [2], [3], [4], []]
        banks_before = [sum(j // 4 + 1 for j in range(i)) for i in range(TPB + 1)]
        banks = banks_before[TPB]
        assert banks % 2 == 0

        @st.block.sync
        def _(sp):
            for h in range(2):
                sp.dma_start(wq[h][:], core.a["stream_l0.wq"][h]).then_inc(loaded[h], 16)
                sp.dma_start(wk[h][:], core.a["stream_l0.wk"][h]).then_inc(loaded[h], 16)
            with sp.Fori(0, heads // 2) as u:
                for s in range(2):
                    head = 2 * u + s
                    sp.wait_ge(side_ready, START + side_steps * (head + 1))
                    for dst, name in ((wq, "wq"), (wk, "wk")):
                        src = core.a[f"stream_l0.{name}"][bass.ds(head + 2, 1)].rearrange("h k c -> (h k) c")
                        sp.dma_start(dst[s][:], src).then_inc(loaded[s], 16)
            for s in range(2):
                sp.wait_ge(loaded[s], START + 32 * (heads // 2 + 1))

        @st.block.tensor
        def _(pe):
            pe.wait_ge(core.w_sem["l0_attn"], value)
            for half in range(halves):
                pe.wait_ge(lat_stored, START + half)
                nc.tensor.matmul(side_ps[0:hd, :], w["l0_attn.w_down"], core.xT[:, b * S + half * CH:b * S + (half + 1) * CH],
                                 start=True, stop=True).then_inc(lat_ready, 1)
            pe.wait_ge(lat_stored, START + halves)

            def side(slot, k, number, head, weights):
                half = slice(k % 2 * CH, (k % 2 + 1) * CH)
                if k == 0:
                    pe.wait_ge(loaded[slot], START + weights)
                pe.wait_ge(side_read, START + number)
                pe.sem_inc(passed, 1)
                if k < 2:
                    mm = nc.tensor.matmul(side_ps[:], wq[slot][:], core.xT[:, b * S + half.start:b * S + half.stop],
                                          start=True, stop=True)
                elif k < 4:
                    mm = nc.tensor.matmul(side_ps[:], wk[slot][:], latT[:, half], start=True, stop=True)
                else:
                    for t in range(TPB):
                        mm = nc.tensor.matmul(side_ps[:, t * hd:(t + 1) * hd], latT[:, t * P:(t + 1) * P],
                                              w["l0_attn.w_v"][:, bass.ds(head * hd, hd)], start=True, stop=True)
                mm.then_inc(side_ready, 1)

            def scores(slot, i):
                keys = (i + 1) * P
                for at in range(0, keys, CH):
                    end = min(keys, at + CH)
                    mm = nc.tensor.matmul(scores_ps[i % 2][:, at:end], qT[slot][:, i * P:(i + 1) * P],
                                          kT[slot][:, at:end], start=True, stop=end < keys)
                nc.tensor.matmul(scores_ps[i % 2][:, i * P:(i + 1) * P], core.ident16[:], core.causal16[:],
                                 start=False, stop=True).then_inc(scores_ready, 1)

            for k in range(side_steps):
                side(0, k, k, 0, 32)
            pe.wait_ge(side_read, START + side_steps)
            scores(0, 0)
            scores(0, 1)
            with pe.Fori(0, heads // 2) as u:
                for s in range(2):
                    head = 2 * u + s
                    for i in range(TPB):
                        unit = head * TPB + i
                        pe.wait_ge(probs_ready, START + unit + 1)
                        for g, at in enumerate(range(0, i + 1, 4)):
                            before = banks_before[i] + g
                            pe.wait_ge(stored, START + head * banks + before - 1 if s or before >= 1 else 2 * u * banks)
                            for j in range(at, min(at + 4, i + 1)):
                                mm = nc.tensor.transpose(turned_ps[before % 2][:, (j - at) * P:(j - at + 1) * P],
                                                         probs[i % 2][:, j * P:(j + 1) * P], core.ident[:])
                            mm.then_inc(turned, 1)
                        if i < TPB - 2:
                            scores(s, i + 2)
                        else:
                            if i == TPB - 2:
                                pe.wait_ge(side_read, START + (head + 1) * side_steps + 4)
                            scores(1 - s, i + 2 - TPB)
                        for k in at_unit[i]:
                            side(1 - s, k, side_steps * (head + 1) + k, head + 1, 32 * (u + 1 + s))
                        pe.wait_ge(stored, START + head * banks + banks_before[i] + 1)
                        pe.wait_ge(out_read, START + unit)
                        if i == 0:
                            pe.wait_ge(side_read, START + (head + 1) * side_steps)
                        for j in range(i + 1):
                            if j == 4:
                                pe.wait_ge(stored, START + head * banks + banks_before[i] + 2)
                            mm = nc.tensor.matmul(out_ps[:, :hd], probsT[i % 2][:, j, :], v[s][:, j, :], start=j == 0,
                                                  stop=j == i)
                        mm.then_inc(out_ready, 1)

        @st.block.scalar
        def _(act):
            for half in range(halves):
                act.wait_ge(lat_ready, START + half + 1)
                nc.scalar.activation(latT[:, half * CH:(half + 1) * CH], side_ps[0:hd, :], ACT.Copy
                                     ).then_inc(lat_stored, 1)

            def exponentials(i, unit):
                keys = (i + 1) * P
                act.wait_ge(max_ready, START + unit + 1)
                nc.scalar.activation(probs[i % 2][:, 0:keys], scores_ps[i % 2][:, 0:keys], ACT.Exp,
                                     bias=neg_max[:, i % 4:i % 4 + 1], accum_out=total[:, i % 4:i % 4 + 1]
                                     ).then_inc(probs_ready, 1)

            exponentials(0, 0)
            with act.Fori(0, heads // 2) as u:
                for s in range(2):
                    head = 2 * u + s
                    for i in range(TPB):
                        unit = head * TPB + i
                        act.wait_ge(turned, START + head * banks + banks_before[i])
                        act.wait_ge(out_read, START + unit - 2 if s or i >= 2 else 2 * u * TPB)
                        exponentials((i + 1) % TPB, unit + 1)
                        for g, at in enumerate(range(0, i + 1, 4)):
                            act.wait_ge(turned, START + head * banks + banks_before[i] + g + 1)
                            if g == 0:
                                act.wait_ge(out_ready, START + unit - 1 if s or i >= 1 else 2 * u * TPB)
                            end = min(at + 4, i + 1)
                            nc.scalar.activation(probsT[i % 2][:, at:end, :].rearrange("p j q -> p (j q)"),
                                                 turned_ps[(banks_before[i] + g) % 2][:, 0:(end - at) * P], ACT.Copy
                                                 ).then_inc(stored, 1)

        @st.block.vector
        def _(dve):
            dve.wait_ge(core.w_sem["l0_attn"], value)

            step = Steps(dve, added)

            def read_side(slot, k, number):
                half = slice(k % 2 * CH, (k % 2 + 1) * CH)
                dve.wait_ge(side_ready, START + number + 1)
                if k < 4:
                    for i in range(2):
                        rows = slice(i * hd, (i + 1) * hd)
                        ins = nc.vector.scalar_tensor_tensor(parts[i][:], side_ps[rows, :], hd ** -0.5 if k < 2 else 1.0,
                                                             w["l0_attn.rope"][rows, half], op0=ALU.mult, op1=ALU.mult)
                    step.done(ins)
                    ins = nc.vector.tensor_tensor((qT if k < 2 else kT)[slot][:, half], parts[0][:], parts[1][:], ALU.add)
                else:
                    ins = nc.vector.tensor_copy(v[slot][:].rearrange("p t d -> p (t d)"), side_ps[:])
                ins.then_inc(side_read, 1)
                dve.wait_ge(side_read, START + number + 1)

            def maximum(i, unit):
                dve.wait_ge(scores_ready, START + unit + 1)
                nc.vector.tensor_reduce(neg_max[:, i % 4:i % 4 + 1], scores_ps[i % 2][:, 0:(i + 1) * P], AX.X, ALU.max,
                                        negate=True).then_inc(max_ready, 1)

            for k in range(side_steps):
                read_side(0, k, k)
            maximum(0, 0)
            maximum(1, 1)
            with step.loop(heads // 2, 2 * 4) as u:
                for s in range(2):
                    head = 2 * u + s
                    for i in range(TPB):
                        unit = head * TPB + i
                        maximum((i + 2) % TPB, unit + 2)
                        for k in at_unit[i]:
                            read_side(1 - s, k, side_steps * (head + 1) + k)
                        dve.wait_ge(probs_ready, START + unit + 1)
                        nc.vector.reciprocal(inverse[:, i % 4:i % 4 + 1], total[:, i % 4:i % 4 + 1]).then_inc(inverted, 1)
                        dve.wait_ge(inverted, START + unit + 1)
                        dve.wait_ge(out_ready, START + unit + 1)
                        nc.vector.tensor_scalar(mixed[:, i, bass.ds(head * hd, hd)], out_ps[:, :hd],
                                                inverse[:, i % 4:i % 4 + 1], None, ALU.mult).then_inc(out_read, 1)


def l1_ffn(core):
    nc, w, sem, value = core.nc, core.w, core.w_sem["l1_ffn"], core.w_value["l1_ffn"]
    layer_norm_and_transpose(core, core.x, 1e-5, "norm")
    groups, width = 8, 64
    with core.stage("maskffn") as st:
        low = st.sb("low", [width + 1, TOKENS])
        top = [st.sb(f"top{s}", [P, groups]) for s in range(2)]
        hot = [st.sb(f"hot{s}", [P, groups, width]) for s in range(2)]
        kept = [st.sb(f"kept{s}", [P, groups * width]) for s in range(2)]
        keptT = [st.sb(f"keptT{s}", [P, 4, P]) for s in range(2)]
        half_b2 = st.sb("half_b2", [P, D])
        logits_ps = [st.bank(f"logits_ps{s}") for s in range(2)]
        mid_ps = [st.bank(f"mid_ps{s}") for s in range(2)]
        keptT_ps = [st.bank(f"keptT_ps{s}") for s in range(2)]
        result_ps = [st.bank(f"result_ps{s}") for s in range(2)]
        set_up, half_ready, bias_added = st.sem("set_up"), st.sem("half_ready"), st.sem("bias_added")
        low_ps_ready, low_ready, mid_ready = st.sem("low_ps_ready"), st.sem("low_ready"), st.sem("mid_ready")
        top_ready, hot_ready, kept_ready = st.sem("top_ready"), st.sem("hot_ready"), st.sem("kept_ready")
        keptT_ps_ready, keptT_ready = st.sem("keptT_ps_ready"), st.sem("keptT_ready")
        result_ready, x_done = st.sem("result_ready"), st.sem("x_done")

        @st.block.gpsimd
        def _(pool):
            nc.gpsimd.memset(low[width:width + 1, :], 1.0).then_inc(set_up, 1)
            pool.wait_ge(set_up, START + 1)
            pool.wait_ge(core.w_sem["l1_ffn"], value)
            nc.gpsimd.tensor_scalar(half_b2[:], w["l1_ffn.b2_rep"][:, :], 0.5, None, ALU.mult).then_inc(half_ready, 1)
            pool.wait_ge(half_ready, START + 1)
            for c in range(CHUNKS):
                x = core.x[:, c * SUB:(c + 1) * SUB, :]
                nc.gpsimd.tensor_tensor(x, x, half_b2[:].unsqueeze(1).to_broadcast([P, SUB, D]), ALU.add
                                        ).then_inc(bias_added, 1)
                pool.wait_ge(bias_added, START + c + 1)

        @st.block.vector
        def _(dve):
            def add(c):
                dve.wait_ge(result_ready, START + (c + 1) * SUB)
                dve.wait_ge(bias_added, START + c + 1)
                x = core.x[:, c * SUB:(c + 1) * SUB, :]
                nc.vector.scalar_tensor_tensor(x, result_ps[c % 2][:].rearrange("p (t d) -> p t d", t=SUB), 0.5, x,
                                               op0=ALU.mult, op1=ALU.add).then_inc(x_done, 1)

            for t in range(TILES):
                s = t % 2
                dve.wait_ge(mid_ready, START + t + 1)
                logits = logits_ps[s][:].rearrange("p (g w) -> p g w", g=groups)
                nc.vector.tensor_reduce(top[s][:], logits, AX.X, ALU.max).then_inc(top_ready, 1)
                dve.wait_ge(top_ready, START + t + 1)
                nc.vector.tensor_tensor(hot[s][:], logits, top[s][:].unsqueeze(2).to_broadcast([P, groups, width]),
                                        ALU.is_equal).then_inc(hot_ready, 1)
                dve.wait_ge(hot_ready, START + t + 1)
                if t >= 2:
                    dve.wait_ge(keptT_ps_ready, START + t - 1)
                nc.vector.scalar_tensor_tensor(kept[s][:], mid_ps[s][:], 0.0, hot[s][:].rearrange("p g w -> p (g w)"),
                                               op0=ALU.max, op1=ALU.mult).then_inc(kept_ready, 1)
                if t >= 1:
                    dve.wait_ge(kept_ready, START + t)
                if t % SUB == SUB - 2 and t >= SUB:
                    add(t // SUB - 1)
            add(CHUNKS - 1)

        @st.block.tensor
        def _(pe):
            pe.wait_ge(core.w_sem["l1_ffn"], value)
            pe.wait_ge(set_up, START + 1)
            for c in range(CHUNKS):
                if c >= 2:
                    pe.wait_ge(low_ready, START + c - 1)
                nc.tensor.matmul(keptT_ps[c % 2][0:width, :], w["l1_ffn.m1"], core.xT[:, c * CH:(c + 1) * CH],
                                 start=True, stop=True).then_inc(low_ps_ready, 1)

            def up(t):
                pe.wait_ge(low_ready, START + t // SUB + 1)
                if t >= 2:
                    pe.wait_ge(kept_ready, START + t - 1)
                nc.tensor.matmul(logits_ps[t % 2][:], low[:, t * P:(t + 1) * P], w["l1_ffn.m2"], start=True, stop=True)
                nc.tensor.matmul(mid_ps[t % 2][:], core.xT[:, t * P:(t + 1) * P], w["l1_ffn.w1"], start=True, stop=True
                                 ).then_inc(mid_ready, 1)

            def down(t):
                pe.wait_ge(keptT_ready, START + t + 1)
                if t % SUB == 0 and t >= 2 * SUB:
                    pe.wait_ge(x_done, START + t // SUB - 1)
                for k in range(4):
                    mm = nc.tensor.matmul(result_ps[t // SUB % 2][:, t % SUB * D:(t % SUB + 1) * D],
                                          keptT[t % 2][:, k, :], w["l1_ffn.w2"][:, k, :], start=k == 0, stop=k == 3)
                mm.then_inc(result_ready, 1)

            pe.wait_ge(low_ready, START + CHUNKS)
            up(0)
            up(1)
            for t in range(TILES):
                pe.wait_ge(kept_ready, START + t + 1)
                if t >= 2:
                    pe.wait_ge(keptT_ready, START + t - 1)
                for k in range(4):
                    mm = nc.tensor.transpose(keptT_ps[t % 2][:, k * P:(k + 1) * P], kept[t % 2][:, k * P:(k + 1) * P],
                                             core.ident[:])
                mm.then_inc(keptT_ps_ready, 1)
                if t + 2 < TILES:
                    up(t + 2)
                if t >= 1:
                    down(t - 1)
            down(TILES - 1)

        @st.block.scalar
        def _(act):
            for c in range(CHUNKS):
                act.wait_ge(low_ps_ready, START + c + 1)
                nc.scalar.activation(low[0:width, c * CH:(c + 1) * CH], keptT_ps[c % 2][0:width, :], ACT.Copy
                                     ).then_inc(low_ready, 1)
            for t in range(TILES):
                act.wait_ge(keptT_ps_ready, START + t + 1)
                if t >= 2:
                    act.wait_ge(result_ready, START + t - 1)
                nc.scalar.activation(keptT[t % 2][:].rearrange("p k d -> p (k d)"), keptT_ps[t % 2][:], ACT.Copy
                                     ).then_inc(keptT_ready, 1)


def l1_attn(core):
    w, sem, value = core.w, core.w_sem["l1_attn"], core.w_value["l1_attn"]
    heads, hd = 8, 64
    layer_norm_and_transpose(core, core.x, 1e-5, "norm")
    for b in range(B):
        with ExitStack() as ctx:
            mixed = core.sb(f"mixed{core.stages}", [P, TPB, heads * hd], ctx=ctx)
            grouped = core.sb(f"grouped{core.stages}", [P, TPB, D], ctx=ctx)
            sparse_attention(core, b, mixed, grouped, heads, hd)
            project_tokens(core, "groups", mixed, TPB, w["l1_attn.w_group"], sem, value, lambda t, end: grouped[:, t:end, :])
            project_tokens(core, "w_out", grouped, TPB, w["l1_attn.w_out"].unsqueeze(1), sem, value,
                           lambda t, end: core.x[:, b * TPB + t:b * TPB + end, :])


SIDE_CHAIN = 13


def sparse_attention(core, b, mixed, grouped, heads, hd):
    nc, w, sem, value = core.nc, core.w, core.w_sem["l1_attn"], core.w_value["l1_attn"]
    halves, blocks = S // CH, 32
    width = P + 64
    qk_heads = heads + 1
    with core.stage("l1attn") as st:
        lowT = st.sb("lowT", [32, S])
        qk = st.sb("qk", [P, TPB, qk_heads, hd])
        v = st.sb("v", [P, TPB, hd])
        rotated = [st.sb(f"rotated{i}", [P, qk_heads, 32]) for i in range(2)]
        square = [st.sb(f"square{i}", [P, qk_heads, hd]) for i in range(2)]
        mean_sq = st.sb("mean_sq", [P, TPB, qk_heads])
        rms_inv = st.sb("rms_inv", [P, TPB, qk_heads])
        kT = st.sb("kT", [hd, S])
        block_mean = st.sb("block_mean", [P, TPB, 4, blocks])
        kcT = st.sb("kcT", [hd, blocks + 3])
        vc = st.sb("vc", [P, 4 * hd])
        q_tiles = st.sb("q_tiles", [P, TPB, hd])
        qT = [st.sb(f"qT{i}", [hd, S]) for i in range(2)]
        block_scores = st.sb("block_scores", [P, TPB, blocks + 1])
        block_max = st.sb("block_max", [P, TPB])
        shifted = st.sb("shifted", [P, TPB, blocks + 1])
        block_sum = st.sb("block_sum", [P, TPB])
        gate_in = st.sb("gate_in", [P, TPB, 3])
        gate_sum = st.sb("gate_sum", [P, TPB])
        gate_inv = st.sb("gate_inv", [P, TPB])
        best = st.sb("best", [P, 4, 8])
        rest = st.sb("rest", [P, 4, blocks])
        gate = [st.sb(f"gate{i}", [P, TPB, 3]) for i in range(2)]
        block_probs = [st.sb(f"block_probs{i}", [P, TPB, blocks]) for i in range(2)]
        unselected = [st.sb(f"unselected{i}", [P, 4, blocks]) for i in range(2)]
        selected = [st.sb(f"selected{i}", [P, S]) for i in range(2)]
        window = [st.sb(f"window{i}", [P, width + 1]) for i in range(2)]
        probs = [st.sb(f"probs{i}", [P, S]) for i in range(2)]
        window_probs = [st.sb(f"window_probs{i}", [P, width + 1]) for i in range(2)]
        probsT = [st.sb(f"probsT{i}", [P, TPB, P]) for i in range(2)]
        blocksT = st.sb("blocksT", [P, 2, P])
        blocks_out = [st.sb(f"blocks_out{i}", [P, TPB, hd]) for i in range(2)]
        neg_max = st.sb("neg_max", [P, 4, 2])
        total = st.sb("total", [P, 4, 2])
        inverse = st.sb("inverse", [P, 4, 2])
        factor = st.sb("factor", [P, 4])
        ratio = st.sb("ratio", [P, 4])
        gate_ratio = [st.sb(f"gate_ratio{i}", [P, TPB]) for i in range(2)]
        scores_ps = [st.bank(f"scores_ps{i}", S) for i in range(2)]
        side_ps, out_ps = st.bank("side_ps"), st.bank("out_ps")
        turned_ps = [st.bank(f"turned_ps{i}") for i in range(2)]
        low_ready, low_stored, raw_ready, rotated_ready = (st.sem("low_ready"), st.sem("low_stored"), st.sem("raw_ready"),
                                                           st.sem("rotated_ready"))
        rest_stored, squared, summed, root_ready = (st.sem("rest_stored"), st.sem("squared"), st.sem("summed"),
                                                    st.sem("root_ready"))
        normalised, kT_ps_ready, kT_ready, vc_ready = (st.sem("normalised"), st.sem("kT_ps_ready"), st.sem("kT_ready"),
                                                       st.sem("vc_ready"))
        copied, block_exp_in, block_exp = st.sem("copied"), st.sem("block_exp_in"), st.sem("block_exp")
        side_ready, side_read, side_done = st.sem("side_ready"), st.sem("side_read"), st.sem("side_done")
        steps_done = st.sem("steps_done")
        scores_ready, max_ready, probs_ready = st.sem("scores_ready"), st.sem("max_ready"), st.sem("probs_ready")
        turned, stored, combined = st.sem("turned"), st.sem("stored"), st.sem("combined")
        out_ready, out_read, passed = st.sem("out_ready"), st.sem("out_read"), st.sem("passed")
        passed_dve = st.sem("passed_dve")
        side_steps = 5
        at_unit = [[0], [1], [2], [], [], [3], [4], []]
        sink = w["l1_attn.sink_rep"]
        long_next = (TPB - 2,)

        n_banks = [-(-(i + 1) // 4) for i in range(TPB)]
        banks_before = [sum(n_banks[:i]) for i in range(TPB + 1)]
        banks = banks_before[TPB]
        assert banks % 2 == 0

        @st.block.tensor
        def _(pe):
            pe.wait_ge(core.w_sem["l1_attn"], value)
            for half in range(halves):
                pe.wait_ge(low_stored, START + half)
                nc.tensor.matmul(side_ps[0:32, :], w["l1_attn.w_qc"], core.xT[:, b * S + half * CH:b * S + (half + 1) * CH],
                                 start=True, stop=True).then_inc(low_ready, 1)
            pe.wait_ge(low_stored, START + halves)
            for t in range(TPB):
                if t >= 2:
                    pe.wait_ge(rotated_ready, START + t - 1)
                    pe.wait_ge(rest_stored, START + t - 1)
                nc.tensor.matmul(scores_ps[t % 2][:, 0:CH], lowT[:, t * P:(t + 1) * P], w["l1_attn.w_qup"], start=True,
                                 stop=True)
                nc.tensor.matmul(scores_ps[t % 2][:, CH:CH + 2 * hd], core.xT[:, (b * TPB + t) * P:(b * TPB + t + 1) * P],
                                 w["l1_attn.w_kv"], start=True, stop=True).then_inc(raw_ready, 1)
            pe.wait_ge(normalised, START + 1)
            for t in range(TPB):
                mm = nc.tensor.transpose(turned_ps[t // 4][0:hd, t % 4 * P:(t % 4 + 1) * P], qk[:, t, heads, :],
                                         core.ident[:])
            mm.then_inc(kT_ps_ready, 1)
            for t in range(TPB):
                mm = nc.tensor.matmul(out_ps[:, 0:hd], block_mean[:, t].rearrange("p r n -> p (r n)"), v[:, t, :],
                                      start=t == 0, stop=t == TPB - 1)
            mm.then_inc(vc_ready, 1)
            pe.wait_ge(kT_ready, START + 2)

            def side(slot, k, number, head):
                pe.wait_ge(side_read, START + number)
                if k < 2:
                    pe.wait_ge(copied, START + head + 1)
                    pe.sem_inc(passed, 1)
                    for i in range(4):
                        mm = nc.tensor.transpose(side_ps[0:hd, i * P:(i + 1) * P], q_tiles[:, 4 * k + i, :],
                                                 core.ident[:])
                elif k == 2:
                    for t in range(TPB):
                        mm = nc.tensor.matmul(side_ps[:, t * (blocks + 3):(t + 1) * (blocks + 3)],
                                              qT[slot][:, t * P:(t + 1) * P], kcT[:], start=True, stop=True)
                elif k == 4:
                    for i in range(2):
                        mm = nc.tensor.matmul(side_ps[:, i * 4 * hd:(i + 1) * 4 * hd], blocksT[:, i, :], vc[:],
                                              start=True, stop=True)
                else:
                    pe.wait_ge(side_done, START + head + 1)
                    pe.sem_inc(passed, 1)
                    for i in range(2):
                        mm = nc.tensor.transpose(side_ps[:, i * P:(i + 1) * P],
                                                 block_probs[slot][:, 4 * i:4 * i + 4, :].rearrange("p t n -> p (t n)"),
                                                 core.ident[:])
                mm.then_inc(side_ready, 1)

            def scores(slot, i):
                keys = (i + 1) * P
                for at in range(0, keys, CH):
                    end = min(keys, at + CH)
                    nc.tensor.matmul(scores_ps[i % 2][:, at:end], qT[slot][:, i * P:(i + 1) * P], kT[:, at:end],
                                     start=True, stop=end < keys)
                nc.tensor.matmul(scores_ps[i % 2][:, i * P:(i + 1) * P], core.ident16[:], core.causal16[:],
                                 start=False, stop=True).then_inc(scores_ready, 1)

            for k in range(side_steps):
                side(0, k, k, 0)
            pe.wait_ge(side_read, START + side_steps)
            scores(0, 0)
            scores(0, 1)
            with pe.Fori(0, heads // 2) as u:
                for s in range(2):
                    head = 2 * u + s
                    for i in range(TPB):
                        unit = head * TPB + i
                        pe.wait_ge(combined, START + unit + 1)
                        for g in range(n_banks[i]):
                            bank = (banks_before[i] + g) % 2
                            pe.wait_ge(stored, head * banks + banks_before[i] + g - 1
                                       if s or banks_before[i] + g >= 1 else 2 * u * banks)
                            pe.sem_inc(passed, 1)
                            for j in range(4 * g, min(4 * g + 4, i + 1)):
                                mm = nc.tensor.transpose(turned_ps[bank][:, (j - 4 * g) * P:(j - 4 * g + 1) * P],
                                                         probs[i % 2][:, j * P:(j + 1) * P], core.ident[:])
                            mm.then_inc(turned, 1)
                        if i < TPB - 2:
                            scores(s, i + 2)
                        else:
                            if i == TPB - 2:
                                pe.wait_ge(side_read, START + (head + 1) * side_steps + 2)
                            scores(1 - s, i + 2 - TPB)
                        for k in at_unit[i]:
                            side(1 - s, k, side_steps * (head + 1) + k, head + 1)
                        pe.wait_ge(stored, START + head * banks + banks_before[i + 1])
                        pe.wait_ge(out_read, START + unit)
                        pe.sem_inc(passed, 1)
                        for j in range(i + 1):
                            mm = nc.tensor.matmul(out_ps[:, 0:hd], probsT[i % 2][:, j, :], v[:, j, :], start=j == 0,
                                                  stop=j == i)
                        mm.then_inc(out_ready, 1)

        @st.block.scalar
        def _(act):
            for half in range(halves):
                act.wait_ge(low_ready, START + half + 1)
                nc.scalar.activation(lowT[:, half * CH:(half + 1) * CH], side_ps[0:32, :], ACT.Copy
                                     ).then_inc(low_stored, 1)
            for t in range(TPB):
                act.wait_ge(raw_ready, START + t + 1)
                act.wait_ge(rotated_ready, START + t + 1)
                raw = scores_ps[t % 2][:, 0:qk_heads * hd].rearrange("p (h d) -> p h d", d=hd)
                nc.scalar.activation(qk[:, t, :, 32:hd], raw[:, :, 32:hd], ACT.Copy)
                nc.scalar.activation(v[:, t, :], scores_ps[t % 2][:, qk_heads * hd:(qk_heads + 1) * hd], ACT.Copy
                                     ).then_inc(rest_stored, 1)
                act.wait_ge(rest_stored, START + t + 1)
                if t >= 2:
                    act.wait_ge(summed, START + t - 1)
                nc.scalar.activation(square[t % 2][:], qk[:, t], ACT.Square).then_inc(squared, 1)
            act.wait_ge(summed, START + TPB + 1)
            nc.scalar.activation(mean_sq[:], mean_sq[:], ACT.Sqrt).then_inc(root_ready, 1)
            act.wait_ge(kT_ps_ready, START + 1)
            for half in range(halves):
                ins = nc.scalar.activation(kT[:, half * CH:(half + 1) * CH], turned_ps[half][0:hd, :], ACT.Copy)
            ins.then_inc(kT_ready, 1)

            def exponentials(i, unit):
                keys, first = (i + 1) * P, width - P if i == 0 else 0
                act.wait_ge(max_ready, START + unit + 1)
                nc.scalar.activation(probs[i % 2][:, 0:keys], (selected if i >= 4 else scores_ps)[i % 2][:, 0:keys],
                                     ACT.Exp, bias=neg_max[:, i % 4, 0:1], accum_out=total[:, i % 4, 0:1])
                nc.scalar.activation(window_probs[i % 2][:, first:], window[i % 2][:, first:], ACT.Exp,
                                     bias=neg_max[:, i % 4, 1:2], accum_out=total[:, i % 4, 1:2]).then_inc(probs_ready, 1)

            def side_exponentials(number):
                act.wait_ge(block_exp_in, START + number)
                nc.scalar.activation(shifted[:], shifted[:], ACT.Exp)
                nc.scalar.activation(gate_in[:], gate_in[:], ACT.Exp, scale=-1.0).then_inc(block_exp, 1)

            def read_side(slot, k, number):
                act.wait_ge(side_ready, START + number + 1)
                src, dst = {0: (side_ps[0:hd, :], qT[slot][:, 0:CH]), 1: (side_ps[0:hd, :], qT[slot][:, CH:S]),
                            3: (side_ps[:, 0:2 * P], blocksT[:].rearrange("p i q -> p (i q)")),
                            4: (side_ps[:], blocks_out[slot][:].rearrange("p t d -> p (t d)"))}[k]
                nc.scalar.activation(dst, src, ACT.Copy).then_inc(side_read, 1)

            for k in range(2):
                read_side(0, k, k)
            side_exponentials(1)
            for k in (3, 4):
                read_side(0, k, k)
            exponentials(0, 0)
            with act.Fori(0, heads // 2) as u:
                for s in range(2):
                    head = 2 * u + s
                    for i in range(TPB):
                        unit = head * TPB + i
                        if i not in long_next:
                            act.wait_ge(turned, START + head * banks + banks_before[i])
                            exponentials((i + 1) % TPB, unit + 1)
                        for g in range(n_banks[i]):
                            act.wait_ge(turned, START + head * banks + banks_before[i] + g + 1)
                            if g == 0:
                                act.wait_ge(out_ready, START + unit - 1 if s or i >= 1 else 2 * u * TPB)
                            end = min(4 * g + 4, i + 1)
                            nc.scalar.activation(probsT[i % 2][:, 4 * g:end, :].rearrange("p j q -> p (j q)"),
                                                 turned_ps[(banks_before[i] + g) % 2][:, 0:(end - 4 * g) * P], ACT.Copy
                                                 ).then_inc(stored, 1)
                        if i in long_next:
                            exponentials((i + 1) % TPB, unit + 1)
                        for k in at_unit[i]:
                            if k != 2:
                                read_side(1 - s, k, side_steps * (head + 1) + k)
                        if i == 3:
                            side_exponentials(head + 2)

        @st.block.gpsimd
        def _(pool):
            pool.wait_ge(normalised, START + 1)
            nc.gpsimd.tensor_copy(q_tiles[:], qk[:, :, 0, :]).then_inc(copied, 1)
            nc.gpsimd.memset(grouped[:], 0.0)
            with pool.Fori(0, heads // 2) as u:
                for s in range(2):
                    head = 2 * u + s
                    pool.wait_ge(side_ready, START + side_steps * head + 2)
                    nc.gpsimd.tensor_copy(q_tiles[:], qk[:, :, head + 1, :]).then_inc(copied, 1)

        @st.block.vector
        def _(dve):
            step = Steps(dve, steps_done)
            dve.wait_ge(core.w_sem["l1_attn"], value)
            nc.vector.tensor_copy(block_mean[:], w["l1_attn.block_mean"].unsqueeze(2).to_broadcast([P, TPB, 4, blocks]))
            for t in range(TPB):
                dve.wait_ge(raw_ready, START + t + 1)
                raw = scores_ps[t % 2][:, 0:qk_heads * hd].rearrange("p (h d) -> p h d", d=hd)
                for i in range(2):
                    ins = nc.vector.tensor_tensor(
                        rotated[i][:].rearrange("p h (c d) -> p h c d", c=2),
                        raw[:, :, 16 * i:16 * i + 16].unsqueeze(2).to_broadcast([P, qk_heads, 2, 16]),
                        w["l1_attn.rope"][:, i, t, :].rearrange("p (c d) -> p c d", c=2).unsqueeze(1)
                        .to_broadcast([P, qk_heads, 2, 16]), ALU.mult)
                step.done(ins)
                nc.vector.tensor_tensor(qk[:, t, :, 0:32], rotated[0][:], rotated[1][:], ALU.add
                                        ).then_inc(rotated_ready, 1)
                dve.wait_ge(rotated_ready, START + t + 1)
                dve.wait_ge(squared, START + t + 1)
                nc.vector.tensor_reduce(mean_sq[:, t, :], square[t % 2][:], AX.X, ALU.add).then_inc(summed, 1)
            dve.wait_ge(summed, START + TPB)
            nc.vector.tensor_scalar(mean_sq[:], mean_sq[:], 1.0 / hd, 1e-6, ALU.mult, ALU.add).then_inc(summed, 1)
            dve.wait_ge(root_ready, START + 1)
            step.done(nc.vector.reciprocal(rms_inv[:], mean_sq[:]))
            for t in range(TPB):
                ins = nc.vector.tensor_tensor(qk[:, t], qk[:, t],
                                              rms_inv[:, t, :].unsqueeze(2).to_broadcast([P, qk_heads, hd]), ALU.mult)
            step.done(ins)
            for t in range(TPB):
                nc.vector.tensor_tensor(qk[:, t, 0:heads, :], qk[:, t, 0:heads, :],
                                        w["l1_attn.g_q_rep"].unsqueeze(1).to_broadcast([P, heads, hd]), ALU.mult)
                ins = nc.vector.scalar_tensor_tensor(qk[:, t, heads, :], qk[:, t, heads, :], hd ** -0.5,
                                                     w["l1_attn.g_k_rep"], op0=ALU.mult, op1=ALU.mult)
            ins.then_inc(normalised, 1)
            dve.wait_ge(vc_ready, START + 1)
            step.done(nc.vector.memset(vc[:], 0.0))
            for i in range(4):
                rows = slice(i * blocks, (i + 1) * blocks)
                nc.vector.tensor_copy(vc[rows, i * hd:(i + 1) * hd], out_ps[rows, 0:hd])
            nc.vector.tensor_copy(kcT[:, blocks:], w["l1_attn.w_gate"])
            dve.wait_ge(kT_ready, START + 1)
            step.done(nc.vector.tensor_reduce(kcT[:, 0:blocks], kT[:].rearrange("p (n c) -> p n c", c=S // blocks), AX.X, ALU.add))
            nc.vector.tensor_scalar(kcT[:, 0:blocks], kcT[:, 0:blocks], blocks / S, None, ALU.mult).then_inc(kT_ready, 1)

            def block_scores_of(slot, number, head):
                dve.wait_ge(side_ready, START + number + 1)
                made = side_ps[:, 0:TPB * (blocks + 3)].rearrange("p (t n) -> p t n", n=blocks + 3)
                nc.vector.tensor_tensor(block_scores[:, :, 0:blocks], made[:, :, 0:blocks],
                                        w["l1_attn.block_mask"], ALU.add)
                nc.vector.tensor_copy(block_scores[:, :, blocks], sink[:, bass.ds(head, 1)].to_broadcast([P, TPB]))
                nc.vector.tensor_tensor(gate_in[:], made[:, :, blocks:],
                                        w["l1_attn.b_gate_rep"].unsqueeze(1).to_broadcast([P, TPB, 3]), ALU.add
                                        ).then_inc(side_read, 1)
                dve.wait_ge(side_read, START + number + 1)
                step.done(nc.vector.tensor_reduce(block_max[:], block_scores[:], AX.X, ALU.max))
                nc.vector.tensor_tensor(shifted[:], block_scores[:],
                                        block_max[:].unsqueeze(2).to_broadcast([P, TPB, blocks + 1]), ALU.subtract
                                        ).then_inc(block_exp_in, 1)

            def select(slot):
                for t in range(4):
                    ins = nc.vector.max(best[:, t, :], block_scores[:, 4 + t, 0:blocks])
                step.done(ins)
                dve.sem_inc(passed_dve, 1)
                for t in range(4):
                    ins = nc.vector.match_replace(rest[:, t, :], best[:, t, :], block_scores[:, 4 + t, 0:blocks], -3e38)
                step.done(ins)
                dve.sem_inc(passed_dve, 1)
                for t in range(4):
                    ins = nc.vector.max(best[:, t, :], rest[:, t, :])
                step.done(ins)
                step.done(nc.vector.tensor_tensor(unselected[slot][:], block_scores[:, 4:, 0:blocks],
                                                  best[:, :, 7:8].to_broadcast([P, 4, blocks]), ALU.is_lt))
                nc.vector.tensor_scalar(unselected[slot][:], unselected[slot][:], NEG, None, ALU.mult)

            def mix(slot, head):
                dve.wait_ge(block_exp, START + head + 1)
                step.done(nc.vector.tensor_scalar(gate_in[:], gate_in[:], 1.0, None, ALU.add))
                nc.vector.tensor_reduce(block_sum[:], shifted[:], AX.X, ALU.add)
                step.done(nc.vector.reciprocal(gate[slot][:], gate_in[:]))
                step.done(nc.vector.tensor_scalar(gate[slot][:, :, 1], gate[slot][:, :, 1], 1e-30, None, ALU.max))
                nc.vector.reciprocal(gate_ratio[slot][:], gate[slot][:, :, 1])
                step.done(nc.vector.tensor_reduce(gate_sum[:], gate[slot][:], AX.X, ALU.add))
                step.done(nc.vector.tensor_scalar(gate_sum[:], gate_sum[:], 1e-6, None, ALU.max))
                nc.vector.tensor_tensor(gate_ratio[slot][:], gate_ratio[slot][:], gate[slot][:, :, 2], ALU.mult)
                nc.vector.reciprocal(block_max[:], block_sum[:])
                step.done(nc.vector.reciprocal(gate_inv[:], gate_sum[:]))
                step.done(nc.vector.tensor_tensor(gate[slot][:], gate[slot][:],
                                                  gate_inv[:].unsqueeze(2).to_broadcast([P, TPB, 3]), ALU.mult))
                step.done(nc.vector.tensor_tensor(block_max[:], block_max[:], gate[slot][:, :, 0], ALU.mult))
                nc.vector.tensor_tensor(block_probs[slot][:], shifted[:, :, 0:blocks],
                                        block_max[:].unsqueeze(2).to_broadcast([P, TPB, blocks]), ALU.mult
                                        ).then_inc(side_done, 1)
                dve.wait_ge(side_done, START + head + 1)

            def maxima(slot, i, unit, head):
                keys, first = (i + 1) * P, width - P if i == 0 else 0
                dve.wait_ge(scores_ready, START + unit + 1)
                seen = scores_ps[i % 2]
                if i >= 4:
                    nc.vector.tensor_tensor(selected[i % 2][:, 0:keys].rearrange("p (n c) -> p n c", c=32),
                                            seen[:, 0:keys].rearrange("p (n c) -> p n c", c=32),
                                            unselected[slot][:, i - 4, 0:keys // 32].unsqueeze(2)
                                            .to_broadcast([P, keys // 32, 32]), ALU.add)
                    seen = selected[i % 2]
                nc.vector.tensor_tensor(window[i % 2][:, first:width], scores_ps[i % 2][:, keys - width + first:keys],
                                        w["l1_attn.window_mask"][:, 2 * P - width + first:], ALU.add)
                step.done(nc.vector.tensor_copy(window[i % 2][:, width:], sink[:, bass.ds(head, 1)]))
                nc.vector.tensor_reduce(neg_max[:, i % 4, 0:1], seen[:, 0:keys], AX.X, ALU.max, negate=True)
                nc.vector.tensor_reduce(neg_max[:, i % 4, 1:2], window[i % 2][:, first:], AX.X, ALU.max, negate=True
                                        ).then_inc(max_ready, 1)

            def combine(slot, i, unit):
                first, n = width - P if i == 0 else 0, i % 4
                dve.wait_ge(probs_ready, START + unit + 1)
                step.done(nc.vector.reciprocal(inverse[:, n, :], total[:, n, :]))
                nc.vector.tensor_tensor(factor[:, n:n + 1], inverse[:, n, 0:1], gate[slot][:, i, 1:2], ALU.mult)
                step.done(nc.vector.scalar_tensor_tensor(ratio[:, n:n + 1], total[:, n, 0:1],
                                                         gate_ratio[slot][:, i:i + 1], inverse[:, n, 1:2],
                                                         op0=ALU.mult, op1=ALU.mult))
                both = probs[i % 2][:, (i + 1) * P - width + first:(i + 1) * P]
                nc.vector.scalar_tensor_tensor(both, window_probs[i % 2][:, first:width], ratio[:, n:n + 1], both,
                                               op0=ALU.mult, op1=ALU.add).then_inc(combined, 1)

            block_scores_of(0, 2, 0)
            select(0)
            mix(0, 0)
            maxima(0, 0, 0, 0)
            maxima(0, 1, 1, 0)
            combine(0, 0, 0)
            with step.loop(heads // 2, 2 * (SIDE_CHAIN + 3 * TPB)) as u:
                for s in range(2):
                    head = 2 * u + s
                    for i in range(TPB):
                        unit = head * TPB + i
                        if i < TPB - 1:
                            combine(s, i + 1, unit + 1)
                        else:
                            combine(1 - s, 0, unit + 1)
                        if i < TPB - 2:
                            maxima(s, i + 2, unit + 2, head)
                        else:
                            maxima(1 - s, i + 2 - TPB, unit + 2, head + 1)
                        if i == 2:
                            block_scores_of(1 - s, side_steps * (head + 1) + 2, head + 1)
                        if i == 3:
                            select(1 - s)
                        if i == 4:
                            mix(1 - s, head + 1)
                        dve.wait_ge(out_ready, START + unit + 1)
                        nc.vector.scalar_tensor_tensor(mixed[:, i, bass.ds(head * hd, hd)], out_ps[:, 0:hd],
                                                       factor[:, i % 4:i % 4 + 1], blocks_out[s][:, i, :],
                                                       op0=ALU.mult, op1=ALU.add).then_inc(out_read, 1)


def l2_ffn(core):
    w, sem, value = core.w, core.w_sem["l2_ffn"], core.w_value["l2_ffn"]
    layer_norm_and_transpose(core, core.x, 1e-5, "norm", keep=True,
                            small=(w["l2_ffn.wg"], None, core.logits, sem, value))
    top2_gates(core, "gates", 8, softmax_over_all=False)
    add_gated_rows(core, "beta", w["l2_ffn.beta"], sem, value)
    experts_ffn(core, "ffn", 8, 512, ACT.Gelu, w["l2_ffn.w1"], w["l2_ffn.w2"], sem, value,
                b1=w["l2_ffn.b1"], b2=w["l2_ffn.b2_rep"], normed=(w["l2_ffn.gamma_rep"], 1e-6))


def l2_attn(core):
    nc, w, sem, value = core.nc, core.w, core.w_sem["l2_attn"], core.w_value["l2_attn"]
    heads, hd = 16, 64
    layer_norm_and_transpose(core, core.x, 1e-5, "norm", rms_eps=float(np.finfo(np.float32).eps),
                             gain=w["l2_attn.norm_w"][:, 0:1], shift=0.0, gain_sem=sem, gain_value=value)
    for b in range(B):
        with ExitStack() as ctx:
            mixed = core.sb(f"mixed{core.stages}", [P, TPB, heads * hd], ctx=ctx)
            softclamped_attention(core, b, mixed, heads, hd)
            project_tokens(core, "wo", mixed, TPB, w["l2_attn.wo"], sem, value,
                           lambda t, end: core.x[:, b * TPB + t:b * TPB + end, :])


def softclamped_attention(core, b, mixed, heads, hd):
    nc, w, sem, value = core.nc, core.w, core.w_sem["l2_attn"], core.w_value["l2_attn"]
    halves = S // CH
    with core.stage("l2attn") as st:
        norms = st.sb("norms", [P, TPB, heads, 2])
        inverse = st.sb("inverse", [P, TPB, 2, 32])
        gain = st.sb("gain", [hd, heads + 1])
        gain1 = st.sb("gain1", [hd, 2, heads])
        w_slot = [st.sb(f"w_slot{i}", [P, 2 * hd]) for i in range(2)]
        k_scale = [st.sb(f"k_scale{i}", [P, TPB]) for i in range(2)]
        selector = st.sb("selector", [96, heads + 1, hd], BF16)
        parts = st.sb("parts", [96, S], BF16)
        q_scale = [core.kept[0:hd, SUB * i:SUB * (i + 1), :].rearrange("p t d -> p (t d)") for i in range(halves)]
        v_slot = [st.sb(f"v_slot{i}", [P, TPB, hd + 1]) for i in range(2)]
        qT = [st.sb(f"qT{i}", [hd, S]) for i in range(2)]
        kT = [st.sb(f"kT{i}", [hd, S]) for i in range(2)]
        clamped = [st.sb(f"clamped{i}", [P, S]) for i in range(2)]
        probs = [st.sb(f"probs{i}", [P, S]) for i in range(2)]
        sums = st.sb("sums", [P, 2, 4])
        scores_ps = [st.bank(f"scores_ps{i}", S) for i in range(2)]
        out_ps = [st.bank(f"out_ps{i}") for i in range(halves)]
        side_ps = [st.bank(f"side_ps{i}") for i in range(2)]
        raw_ready, squared, summed, root_ready = (st.sem("raw_ready"), st.sem("squared"), st.sem("summed"),
                                                  st.sem("root_ready"))
        steps_done, passed = st.sem("steps_done"), st.sem("passed")
        inverse_ready, inverse_turned, parts_ready, w_ready = (st.sem("inverse_ready"), st.sem("inverse_turned"),
                                                               st.sem("parts_ready"), st.sem("w_ready"))
        side_ready, side_read = st.sem("side_ready"), st.sem("side_read")
        scores_ready, clamped_ready, probs_ready = st.sem("scores_ready"), st.sem("clamped_ready"), st.sem("probs_ready")
        probs_used, out_read, summed_out = st.sem("probs_used"), st.sem("out_read"), st.sem("summed_out")
        side_steps = 5
        at_unit = [[0], [1], [2, 3], [], [4], [], [], []]
        square = [clamped[i][:, 0:CH] for i in range(2)]
        raw_bank = lambda n: scores_ps[n // 2 % 2][:, n % 2 * CH:(n % 2 + 1) * CH]
        tiles_T = lambda t: core.xT[:, (b * TPB + t) * P:(b * TPB + t + 1) * P]

        @st.block.tensor
        def _(pe):
            pe.wait_ge(core.w_sem["l2_attn"], value)
            for t in range(TPB):
                for g in range(heads // 4):
                    n = t * heads // 4 + g
                    if n >= 4:
                        pe.wait_ge(squared, START + n - 3)
                    nc.tensor.matmul(raw_bank(n), tiles_T(t), w["l2_attn.wqkv"][:, 4 * g:4 * g + 4, 0:2 * hd],
                                     start=True, stop=True).then_inc(raw_ready, 1)

            pe.wait_ge(inverse_ready, START + 1)
            for t in range(TPB):
                mm = nc.tensor.transpose(side_ps[t // 4][0:32, t % 4 * P:(t % 4 + 1) * P], inverse[:, t, 0, :],
                                         core.ident[:])
            mm.then_inc(inverse_turned, 1)
            pe.wait_ge(parts_ready, START + 1)

            def side(slot, k, number, head):
                half = slice(k % 2 * CH, (k % 2 + 1) * CH)
                bank = side_ps[(slot + k) % 2]
                if number is not None:
                    pe.wait_ge(side_read, START + number)
                    pe.sem_inc(passed, 1)
                if k < 2:
                    mm = nc.tensor.matmul(bank[0:hd, :], selector[:, bass.ds(head, 1), :].rearrange("p h c -> p (h c)"),
                                          parts[:, half], start=True, stop=True)
                elif k < 4:
                    pe.wait_ge(w_ready, START + head + 1)
                    pe.sem_inc(passed, 1)
                    mm = nc.tensor.matmul(bank[:], w_slot[slot][:], core.xT[:, b * S + half.start:b * S + half.stop],
                                          start=True, stop=True)
                else:
                    for t in range(TPB):
                        mm = nc.tensor.matmul(bank[:, t * hd:(t + 1) * hd], tiles_T(t),
                                              w["l2_attn.wqkv"][:, bass.ds(head, 1), 2 * hd:3 * hd], start=True,
                                              stop=True)
                mm.then_inc(side_ready, 1)

            def scores(slot, j, unit, prepared):
                pe.wait_ge(side_read, START + prepared)
                pe.wait_ge(clamped_ready, START + unit)
                for half in range(halves):
                    mm = nc.tensor.matmul(scores_ps[j % 2][:, half * CH:(half + 1) * CH],
                                          kT[slot][:, j * P:(j + 1) * P], qT[slot][:, half * CH:(half + 1) * CH],
                                          start=True, stop=True)
                mm.then_inc(scores_ready, 1)

            for k in range(side_steps):
                side(0, k, k - 1 if k >= 1 else None, 0)
            scores(0, 0, 0, side_steps)
            with pe.Fori(0, heads // 2) as u:
                for s in range(2):
                    head = 2 * u + s
                    before = side_steps * (head + 1)
                    for j in range(TPB):
                        unit = head * TPB + j
                        if j < TPB - 1:
                            scores(s, j + 1, unit, before)
                        else:
                            scores(1 - s, 0, unit, before + side_steps)
                        for k in at_unit[j]:
                            side(1 - s, k, before + k - 1, head + 1)
                        pe.wait_ge(probs_ready, START + unit + 1)
                        if j == 0:
                            pe.wait_ge(out_read, START + head)
                        for i in range(TPB):
                            mm = nc.tensor.matmul(out_ps[i // 4][:, i % 4 * (hd + 1):(i % 4 + 1) * (hd + 1)],
                                                  probs[j % 2][:, i * P:(i + 1) * P], v_slot[s][:, j, :],
                                                  start=j == 0 and i % 4 == 0, stop=j == TPB - 1,
                                                  skip_group_check=True)
                        mm.then_inc(probs_used, 1)

        @st.block.scalar
        def _(act):
            for n in range(TPB * heads // 4):
                act.wait_ge(raw_ready, START + n + 1)
                if n >= 2:
                    act.wait_ge(summed, START + n - 1)
                nc.scalar.activation(square[n % 2], raw_bank(n), ACT.Square).then_inc(squared, 1)
            act.wait_ge(summed, START + TPB * heads // 4)
            nc.scalar.activation(norms[:].rearrange("p t h c -> p (t h c)"),
                                 norms[:].rearrange("p t h c -> p (t h c)"), ACT.Sqrt).then_inc(root_ready, 1)
            with act.Fori(0, heads // 2) as u:
                for s in range(2):
                    for j in range(TPB):
                        unit = (2 * u + s) * TPB + j
                        act.wait_ge(scores_ready, START + unit + 1)
                        nc.scalar.activation(clamped[j % 2][:], scores_ps[j % 2][:], ACT.Tanh,
                                             scale=k_scale[s][:, j:j + 1]).then_inc(clamped_ready, 1)
                        act.wait_ge(clamped_ready, START + unit + 1)
                        act.wait_ge(probs_used, START + unit - 1 if s or j >= 1 else 2 * u * TPB)
                        nc.scalar.activation(probs[j % 2][:], clamped[j % 2][:], ACT.Exp, scale=50.0 * hd ** -0.5
                                             ).then_inc(probs_ready, 1)

        @st.block.gpsimd
        def _(pool):
            pool.wait_ge(core.w_sem["l2_attn"], value)
            for i in range(2):
                nc.gpsimd.tensor_copy(w_slot[i][:], w["l2_attn.wqkv"][:, i, 0:2 * hd]).then_inc(w_ready, 1)
            with pool.Fori(0, heads // 2) as u:
                for s in range(2):
                    head = 2 * u + s
                    pool.wait_ge(side_ready, START + side_steps * (head + 1))
                    nc.gpsimd.tensor_copy(w_slot[s][:], w["l2_attn.wqkv"][:, head + 2, 0:2 * hd]).then_inc(w_ready, 1)

        @st.block.vector
        def _(dve):
            step = Steps(dve, steps_done)
            dve.wait_ge(core.w_sem["l2_attn"], value)
            nc.vector.memset(gain[:, heads:heads + 1], 0.0)
            nc.vector.memset(inverse[:], 0.0)
            for i in range(3):
                rows = slice(32 * i, 32 * (i + 1))
                nc.vector.tensor_copy(selector[rows], core.ident16[rows, 32 * i:32 * i + heads + 1].unsqueeze(2)
                                      .to_broadcast([32, heads + 1, hd]))
            for i in range(2):
                nc.vector.memset(v_slot[i][:, :, hd:hd + 1], 1.0)
            step.done(nc.vector.tensor_scalar(gain1[:], w["l2_attn.gammas"], 1.0, float(hd) ** 0.5, ALU.add, ALU.mult))
            step.done(nc.vector.tensor_tensor(gain[:, 0:heads], gain1[:, 0, :], gain1[:, 1, :], ALU.mult))
            for t in range(TPB):
                for g in range(heads // 4):
                    n = t * heads // 4 + g
                    dve.wait_ge(squared, START + n + 1)
                    nc.vector.tensor_reduce(norms[:, t, 4 * g:4 * (g + 1), :],
                                            square[n % 2].rearrange("p (h c d) -> p h c d", h=4, c=2), AX.X, ALU.add
                                            ).then_inc(summed, 1)
            dve.wait_ge(root_ready, START + 1)
            step.done(nc.vector.tensor_scalar(norms[:], norms[:], 1e-12, None, ALU.max))
            for i in range(2):
                ins = nc.vector.reciprocal(inverse[:, :, i, 0:heads], norms[:, :, :, i])
            ins.then_inc(inverse_ready, 1)
            dve.wait_ge(inverse_ready, START + 1)
            dve.wait_ge(inverse_turned, START + 1)
            rest, middle = clamped[0], probs[0]
            for i in range(halves):
                part, bank = slice(i * CH, (i + 1) * CH), side_ps[i][0:32, :]
                step.done(nc.vector.tensor_copy(parts[0:32, part], bank))
                step.done(nc.vector.tensor_tensor(rest[0:32, part], bank, parts[0:32, part], ALU.subtract))
                step.done(nc.vector.tensor_copy(parts[32:64, part], rest[0:32, part]))
                step.done(nc.vector.tensor_copy(middle[0:32, part], parts[32:64, part]))
                step.done(nc.vector.tensor_tensor(parts[64:96, part], rest[0:32, part], middle[0:32, part], ALU.subtract))
            dve.sem_inc(parts_ready, 1)

            def read_side(slot, k, number, head):
                half = slice(k % 2 * CH, (k % 2 + 1) * CH)
                bank = side_ps[(slot + k) % 2]
                dve.wait_ge(side_ready, START + number + 1)
                if k < 2:
                    ins = nc.vector.tensor_copy(q_scale[k % 2], bank[0:hd, :])
                elif k < 4:
                    nc.vector.scalar_tensor_tensor(qT[slot][:, half], bank[0:hd, :], gain[:, bass.ds(head, 1)],
                                                   q_scale[k % 2], op0=ALU.mult, op1=ALU.mult)
                    ins = nc.vector.tensor_copy(kT[slot][:, half], bank[hd:2 * hd, :])
                else:
                    nc.vector.tensor_scalar(k_scale[slot][:], inverse[:, :, 1, bass.ds(head, 1)]
                                            .rearrange("p t h -> p (t h)"), 1.0 / 50.0, None, ALU.mult)
                    ins = nc.vector.tensor_copy(v_slot[slot][:, :, 0:hd], bank[:].rearrange("p (t d) -> p t d", t=TPB))
                ins.then_inc(side_read, 1)
                dve.wait_ge(side_read, START + number + 1)

            for k in range(side_steps):
                read_side(0, k, k, 0)
            with dve.Fori(0, heads // 2) as u:
                for s in range(2):
                    head = 2 * u + s
                    before = side_steps * (head + 1)
                    for k in range(side_steps):
                        read_side(1 - s, k, before + k, head + 1)
                    dve.wait_ge(probs_used, START + (head + 1) * TPB)
                    for half in range(halves):
                        out = out_ps[half][:, :4 * (hd + 1)].rearrange("p (t c) -> p t c", t=4)
                        nc.vector.reciprocal(sums[:, half, :], out[:, :, hd]).then_inc(summed_out, 1)
                    dve.wait_ge(summed_out, START + head * 2 + 2)
                    for half in range(halves):
                        out = out_ps[half][:, :4 * (hd + 1)].rearrange("p (t c) -> p t c", t=4)
                        ins = nc.vector.tensor_tensor(mixed[:, 4 * half:4 * half + 4, bass.ds(head * hd, hd)],
                                                      out[:, :, 0:hd],
                                                      sums[:, half, :].unsqueeze(2).to_broadcast([P, 4, hd]), ALU.mult)
                    ins.then_inc(out_read, 1)


def l3_ffn(core):
    nc, w, sem, value = core.nc, core.w, core.w_sem["l3_ffn"], core.w_value["l3_ffn"]
    column = lambda i: w["l3_ffn.columns"][:, i:i + 1]
    heads, kv_heads, hd = 16, 4, 8
    with ExitStack() as ctx:
        qkv = core.sb(f"qkv{core.stages}", [P, TILES, 192], ctx=ctx)
        mixed = core.sb(f"mixed{core.stages}", [P, TILES, D], ctx=ctx)
        layer_norm_and_transpose(core, core.x, 1e-5, "ln1", keep_plain=True, rms_eps=1e-5, gain=column(0),
                                 shift=column(1), gain_sem=sem, gain_value=value,
                                 small=(w["l3_ffn.wqkv"], None, qkv, sem, value))
        with core.stage("pairs") as st:
            product = st.sb("product", [P, 2, TPB, heads, hd])
            scores = st.sb("scores", [P, 2, TPB, heads])
            work = st.sb("work", [P, 2, TPB, heads])
            steps_done, to_exp, exp_done = st.sem("steps_done"), st.sem("to_exp"), st.sem("exp_done")
            rep = heads // kv_heads
            late = slice(TPB, 2 * TPB)

            def kv(position, first, k):
                at = position * TPB
                return qkv[:, at:at + TPB, first + k * hd:first + (k + 1) * hd].unsqueeze(2).to_broadcast(
                    [P, TPB, rep, hd])

            @st.block.vector
            def _(dve):
                step = Steps(dve, steps_done)
                for position in range(2):
                    for k in range(kv_heads):
                        q = qkv[:, late, k * rep * hd:(k + 1) * rep * hd].rearrange("p t (r d) -> p t r d", r=rep)
                        ins = nc.vector.tensor_tensor(product[:, position, :, k * rep:(k + 1) * rep, :], q,
                                                      kv(position, D, k), ALU.mult)
                step.done(ins)
                for position in range(2):
                    ins = nc.vector.tensor_reduce(scores[:, position], product[:, position], AX.X, ALU.add)
                step.done(ins)
                step.done(nc.vector.tensor_tensor(work[:, 0], scores[:, 0], scores[:, 1], ALU.max))
                for position in range(2):
                    ins = nc.vector.tensor_tensor(scores[:, position], scores[:, position], work[:, 0], ALU.subtract)
                ins.then_inc(to_exp, 1)
                dve.wait_ge(exp_done, START + 1)
                step.done(nc.vector.tensor_tensor(work[:, 0], scores[:, 0], scores[:, 1], ALU.add))
                step.done(nc.vector.reciprocal(work[:, 1], work[:, 0]))
                for position in range(2):
                    ins = nc.vector.tensor_tensor(scores[:, position], scores[:, position], work[:, 1], ALU.mult)
                step.done(ins)
                for position in range(2):
                    for k in range(kv_heads):
                        p = scores[:, position, :, k * rep:(k + 1) * rep].unsqueeze(3).to_broadcast([P, TPB, rep, hd])
                        ins = nc.vector.tensor_tensor(product[:, position, :, k * rep:(k + 1) * rep, :], p,
                                                      kv(position, D + kv_heads * hd, k), ALU.mult)
                step.done(ins)
                nc.vector.tensor_tensor(mixed[:, late, :], product[:, 0].rearrange("p t h d -> p t (h d)"),
                                        product[:, 1].rearrange("p t h d -> p t (h d)"), ALU.add)
                for k in range(kv_heads):
                    nc.vector.tensor_copy(mixed[:, 0:TPB, k * rep * hd:(k + 1) * rep * hd].rearrange(
                        "p t (r d) -> p t r d", r=rep), kv(0, D + kv_heads * hd, k))

            @st.block.scalar
            def _(act):
                act.wait_ge(to_exp, START + 1)
                nc.scalar.activation(scores[:], scores[:], ACT.Exp, scale=hd ** -0.5).then_inc(exp_done, 1)

        project_tokens(core, "proj", mixed, TILES, w["l3_ffn.wproj"].unsqueeze(1), sem, value,
                       lambda t, end: core.kept[:, t:end, :])
    layer_norm_and_transpose(core, core.kept, 1e-5, "ln2", gain=column(2), shift=column(3), gain_sem=sem,
                             gain_value=value,
                             small=(w["l3_ffn.wg"], None, core.logits, sem, value))
    top2_gates(core, "gates", 8, softmax_over_all=True)
    with core.stage("residual") as st:
        @st.block.vector
        def _(dve):
            nc.vector.scalar_tensor_tensor(core.x[:].rearrange("p t d -> p (t d)"),
                                           core.kept[:].rearrange("p t d -> p (t d)"), 0.5,
                                           core.x[:].rearrange("p t d -> p (t d)"), op0=ALU.mult, op1=ALU.add)
    experts_ffn(core, "ffn", 8, 256, ACT.Gelu_apprx_tanh, w["l3_ffn.w1"], w["l3_ffn.w2"], sem, value)


def l3_attn(core):
    nc, w, sem, value = core.nc, core.w, core.w_sem["l3_attn"], core.w_value["l3_attn"]
    layer_norm_and_transpose(core, core.x, 1e-5, "norm")
    with core.stage("gru") as st:
        z = st.sb("z", [P, TOKENS])
        a = st.sb("a", [P, TOKENS])
        b = st.sb("b", [P, TOKENS])
        h = st.sb("h", [P, TOKENS])
        gate_ps = [st.bank(f"gate_ps{i}") for i in range(2)]
        value_ps = [st.bank(f"value_ps{i}") for i in range(2)]
        y_ps = [st.bank(f"y_ps{i}") for i in range(4)]
        gate_ready, value_ready = st.sem("gate_ready"), st.sem("value_ready")
        z_ready, b_ready, h_ready = st.sem("z_ready"), st.sem("b_ready"), st.sem("h_ready")
        swish_ready, y_ready, y_turned = st.sem("swish_ready"), st.sem("y_ready"), st.sem("y_turned")
        bz, bh = w["l3_attn.columns"][:, 0:1], w["l3_attn.columns"][:, 1:2]
        beta = w["l3_attn.swish_rep"][:, 0:1]

        @st.block.tensor
        def _(pe):
            pe.wait_ge(core.w_sem["l3_attn"], value)
            with pe.Fori(0, CHUNKS // 2) as u:
                for s in range(2):
                    pe.wait_ge(b_ready, START + 2 * u)
                    xt = core.xT[:, bass.ds((2 * u + s) * CH, CH)]
                    nc.tensor.matmul(gate_ps[s][:], w["l3_attn.wz"], xt, start=True, stop=True).then_inc(gate_ready, 1)
                    nc.tensor.matmul(value_ps[s][:], w["l3_attn.wh"], xt, start=True, stop=True
                                     ).then_inc(value_ready, 1)
            for t in range(TILES):
                if t % TPB == 0:
                    pe.wait_ge(y_ready, START + t // TPB + 1)
                mm = nc.tensor.transpose(y_ps[t // 4][:, t % 4 * P:(t % 4 + 1) * P], core.xT[:, t * P:(t + 1) * P],
                                         core.ident[:])
                if t % 4 == 3:
                    mm.then_inc(y_turned, 1)

        @st.block.scalar
        def _(act):
            act.wait_ge(core.w_sem["l3_attn"], value)
            with act.Fori(0, CHUNKS // 2) as u:
                for s in range(2):
                    act.wait_ge(gate_ready, START + 2 * u + s + 1)
                    nc.scalar.activation(z[:, bass.ds((2 * u + s) * CH, CH)], gate_ps[s][:], ACT.Sigmoid, bias=bz
                                         ).then_inc(z_ready, 1)
            for i in range(B):
                act.wait_ge(h_ready, START + i + 1)
                nc.scalar.activation(z[:, i * S:(i + 1) * S], h[:, i * S:(i + 1) * S], ACT.Sigmoid, scale=beta
                                     ).then_inc(swish_ready, 1)
            for i in range(4):
                act.wait_ge(y_turned, START + i + 1)
                nc.scalar.activation(core.kept[:, 4 * i:4 * i + 4, :].rearrange("p t d -> p (t d)"), y_ps[i][:],
                                     ACT.Copy)

        @st.block.vector
        def _(dve):
            dve.wait_ge(core.w_sem["l3_attn"], value)
            with dve.Fori(0, CHUNKS // 2) as u:
                for s in range(2):
                    c = 2 * u + s
                    dve.wait_ge(z_ready, START + c + 1)
                    dve.wait_ge(value_ready, START + c + 1)
                    nc.vector.tensor_scalar(a[:, bass.ds(c * CH, CH)], z[:, bass.ds(c * CH, CH)], -1.0, 1.0, ALU.mult,
                                            ALU.add)
                    nc.vector.scalar_tensor_tensor(b[:, bass.ds(c * CH, CH)], value_ps[s][:], bh,
                                                   z[:, bass.ds(c * CH, CH)], op0=ALU.add, op1=ALU.mult
                                                   ).then_inc(b_ready, 1)
            dve.wait_ge(b_ready, START + CHUNKS)
            for i in range(B):
                part = slice(i * S, (i + 1) * S)
                nc.vector.tensor_tensor_scan(h[:, part], a[:, part], b[:, part], 0.0, ALU.mult, ALU.add
                                             ).then_inc(h_ready, 1)
            for i in range(B):
                part = slice(i * S, (i + 1) * S)
                dve.wait_ge(swish_ready, START + i + 1)
                nc.vector.scalar_tensor_tensor(core.xT[:, part], h[:, part], beta, z[:, part], op0=ALU.mult,
                                               op1=ALU.mult).then_inc(y_ready, 1)
    layer_norm_stats(core, core.kept, 1e-5, "stats")
    with core.stage("affine") as st:
        normed = [st.sb(f"normed{s}", [P, D]) for s in range(2)]
        scaled = [st.sb(f"scaled{s}", [P, D]) for s in range(2)]
        normed_ready, scaled_ready, moved, x_done = (st.sems("normed_ready", 2), st.sems("scaled_ready", 2),
                                                     st.sems("moved", 2), st.sems("x_done", 2))
        gamma, shift = w["l3_attn.affine_rep"][:, 0, :], w["l3_attn.affine_rep"][:, 1, :]

        @st.block.gpsimd
        def _(pool):
            with pool.Fori(0, TILES // 2) as u:
                for s in range(2):
                    nc.gpsimd.tensor_tensor(core.x[:, 2 * u + s, :], core.x[:, 2 * u + s, :], shift, ALU.add
                                            ).then_inc(moved[s], 1)

        @st.block.vector
        def _(dve):
            with dve.Fori(0, TILES // 2) as u:
                for s in range(2):
                    t = 2 * u + s
                    nc.vector.tensor_scalar(normed[s][:], core.kept[:, t, :], core.mean[:, bass.ds(t, 1)],
                                            core.rstd[:, bass.ds(t, 1)], ALU.subtract, ALU.mult
                                            ).then_inc(normed_ready[s], 1)
                for s in range(2):
                    dve.wait_ge(normed_ready[s], START + u + 1)
                    dve.wait_ge(x_done[s], START + u)
                    nc.vector.tensor_tensor(scaled[s][:], normed[s][:], gamma, ALU.mult).then_inc(scaled_ready[s], 1)
                for s in range(2):
                    dve.wait_ge(scaled_ready[s], START + u + 1)
                    dve.wait_ge(moved[s], START + u + 1)
                    nc.vector.tensor_tensor(core.x[:, 2 * u + s, :], core.x[:, 2 * u + s, :], scaled[s][:], ALU.add
                                            ).then_inc(x_done[s], 1)


SUBLAYERS = [l0_ffn, l0_attn, l0_ffn, l1_ffn, l1_attn, l1_ffn, l2_ffn, l2_attn, l2_ffn, l3_ffn, l3_attn, l3_ffn]
LOAD_SECOND = 5
LOAD_LAST = 6


def heads_beside_rolled(w, heads, rows):
    w = w.T.reshape(rows, heads, 64)
    both = np.concatenate([w, np.concatenate([w[:, :, 32:], w[:, :, :32]], 2)], 2)
    return np.concatenate([both, np.zeros((rows, 2, 128), w.dtype)], 1)


def rope_tables():
    f32 = np.float32
    inv = (f32(1.0) / (f32(10000.0) ** (np.arange(0, 64, 2, dtype=f32) / f32(64)))).astype(f32)
    angle = np.arange(S, dtype=f32)[None, :] * inv[:, None]
    cos, sin = np.cos(angle), np.sin(angle)
    full = np.concatenate([cos, cos, -sin, sin]).astype(f32)
    inv = (f32(1.0) / f32(10000.0) ** (np.arange(16, dtype=f32) * f32(2.0) / f32(32))).astype(f32)
    angle = np.arange(S, dtype=f32)[:, None] * inv[None, :]
    partial = np.stack([np.cos(angle), np.sin(angle)], 1).astype(f32)
    return full, partial.reshape(TPB, P, 2, 16).transpose(1, 0, 2, 3)


def lay_out(v):
    blocks = lambda w: w.reshape(w.shape[0], -1, P, w.shape[-1]).transpose(2, 0, 1, 3)
    full_rope, partial_rope = rope_tables()
    out = {"x": v["L0_attn_x"]}
    out["l0_ffn.wg"] = v["L0_ffn_Wg"]
    out["l0_ffn.bg_rep"] = v["L0_ffn_bg"][None]
    out["l0_ffn.w1"] = v["L0_ffn_W1"].transpose(1, 0, 2)
    out["l0_ffn.w2"] = blocks(v["L0_ffn_W2"])
    out["l0_ffn.b1"] = v["L0_ffn_b1"].reshape(6, 2, P).transpose(2, 0, 1)
    out["l0_ffn.b2_rep"] = v["L0_ffn_b2"][None]
    out["stream_l0.wq"] = heads_beside_rolled(v["L0_attn_wq"], 16, D).transpose(1, 0, 2)
    out["stream_l0.wk"] = heads_beside_rolled(v["L0_attn_w_k_up"], 16, 64).transpose(1, 0, 2)
    out["l0_attn.w_down"] = v["L0_attn_w_kv_down"].T
    out["l0_attn.w_v"] = np.concatenate([v["L0_attn_w_v_up"].T, np.zeros((64, 64), np.float32)], 1)
    out["l0_attn.wo"] = v["L0_attn_wo"].T.reshape(8, P, D).transpose(1, 0, 2)
    out["l0_attn.rope"] = full_rope
    out["l1_ffn.m1"] = v["L1_ffn_m1"]
    out["l1_ffn.m2"] = np.concatenate([v["L1_ffn_m2"].reshape(64, 512), v["L1_ffn_mb"].reshape(1, 512)])
    out["l1_ffn.w1"] = v["L1_ffn_w1"].reshape(D, 512)
    out["l1_ffn.w2"] = v["L1_ffn_w2"].transpose(1, 0, 2).reshape(4, P, D).transpose(1, 0, 2)
    out["l1_ffn.b2_rep"] = v["L1_ffn_b2"][None]
    out["l1_attn.w_qc"] = v["L1_attn_w_qc"]
    out["l1_attn.w_qup"] = v["L1_attn_w_qup"]
    out["l1_attn.w_kv"] = np.concatenate([v["L1_attn_w_k"], v["L1_attn_w_v"]], 1)
    out["l1_attn.g_q_rep"] = v["L1_attn_g_qnorm"][None]
    out["l1_attn.g_k_rep"] = v["L1_attn_g_knorm"][None]
    query, block, key = np.arange(P), np.arange(32), np.arange(2 * P)
    tile = np.arange(TPB)
    position = tile[None, :, None] * P + query[:, None, None]
    out["l1_attn.block_mask"] = np.where((block + 1) * 32 - 1 <= position, 0.0, NEG).astype(np.float32)
    behind = query[:, None] + P - key[None, :]
    out["l1_attn.window_mask"] = np.where((behind >= 0) & (behind < 64), 0.0, NEG).astype(np.float32)
    out["l1_attn.block_mean"] = np.where(block == (4 * tile[None, :, None] + query[:, None, None] // 32), 1 / 32, 0.0
                                         ).astype(np.float32)
    out["l1_attn.w_gate"] = v["L1_attn_w_gate"]
    out["l1_attn.b_gate_rep"] = v["L1_attn_b_gate"][None]
    out["l1_attn.sink_rep"] = np.concatenate([v["L1_attn_sink_logit"], np.zeros(2, np.float32)])[None]
    group = v["L1_attn_w_out_group"]
    zeros = np.zeros((256, 64), group.dtype)
    diagonal = np.concatenate([np.concatenate([group[0], zeros], 1), np.concatenate([zeros, group[1]], 1)])
    out["l1_attn.w_group"] = diagonal.reshape(4, P, D).transpose(1, 0, 2)
    out["l1_attn.w_out"] = v["L1_attn_w_out"]
    cos, sin = partial_rope[:, :, 0], partial_rope[:, :, 1]
    out["l1_attn.rope"] = np.stack([np.stack([cos, sin], 2), np.stack([-sin, cos], 2)], 1).reshape(P, 2, TPB, 32)
    wkv = v["L2_attn_Wkv"]
    heads = np.concatenate([w.reshape(D, 16, 64) for w in (v["L2_attn_Wq"], wkv[:, :1024], wkv[:, 1024:])], 2)
    out["l2_attn.wqkv"] = np.concatenate([heads, np.zeros((D, 2, 192), heads.dtype)], 1)
    out["l2_attn.wo"] = v["L2_attn_Wo"].reshape(8, P, D).transpose(1, 0, 2)
    out["l2_attn.norm_w"] = v["L2_attn_norm_w"][:, None]
    out["l2_attn.gammas"] = np.stack([v["L2_attn_q_gamma"].T, v["L2_attn_k_gamma"].T], 1)
    out["l2_ffn.wg"] = v["L2_ffn_router_w"]
    out["l2_ffn.w1"] = v["L2_ffn_w1"].transpose(1, 0, 2)
    out["l2_ffn.w2"] = blocks(v["L2_ffn_w2"])
    out["l2_ffn.b1"] = v["L2_ffn_b1"].reshape(8, 4, P).transpose(2, 0, 1)
    out["l2_ffn.b2_rep"] = v["L2_ffn_b2"][None]
    out["l2_ffn.gamma_rep"] = v["L2_ffn_gamma"][None]
    out["l2_ffn.beta"] = v["L2_ffn_beta"]
    out["l3_attn.wz"] = v["L3_attn_Wz"]
    out["l3_attn.wh"] = v["L3_attn_Wh"]
    out["l3_attn.columns"] = np.stack([v["L3_attn_bz"], v["L3_attn_bh"]], 1)
    out["l3_attn.swish_rep"] = v["L3_attn_swish_beta"].reshape(1, 1)
    out["l3_attn.affine_rep"] = np.stack([v["L3_attn_ln_gamma"], v["L3_attn_ln_beta"]])[None]
    out["l3_ffn.columns"] = np.stack([v[f"L3_ffn_{n}"] for n in ("ln1_weight", "ln1_bias", "ln2_weight", "ln2_bias")], 1)
    out["l3_ffn.wqkv"] = v["L3_ffn_qkv_weight"].T
    out["l3_ffn.wproj"] = v["L3_ffn_proj_weight"].T
    out["l3_ffn.wg"] = v["L3_ffn_router_weight"].T
    out["l3_ffn.w1"] = v["L3_ffn_moe_w1"].transpose(1, 0, 2)
    out["l3_ffn.w2"] = blocks(v["L3_ffn_moe_w2"])
    return out


def store_everything(core, out):
    with core.stage("store") as st:
        out_stored = core.sem("out_stored")

        @st.block.sync
        def _(sp):
            sp.dma_start(out.rearrange("b (t p) d -> p (b t) d", p=P), core.x[:]).then_inc(out_stored, 16)
            sp.wait_ge(out_stored, 16)


def build(nc, a, out):
    with ExitStack() as ctx:
        core = Core(nc, ctx, a)
        used = {layer.__name__ for layer in SUBLAYERS}
        first, second, last = [[n for n in names if n in used] for names in (
            ["l0_ffn", "l0_attn", "l1_ffn", "l1_attn"], ["l2_ffn", "l2_attn"], ["l3_ffn", "l3_attn"])]
        size = lambda groups: sum(math.prod(ap.shape[1:]) for key, ap in a.items() if key.partition(".")[0] in groups)
        arena = core.sb("arena", [P, max(size(first), size(last), 1)])
        load_everything(core, core.place_weights(first, arena))
        for n, layer in enumerate(SUBLAYERS):
            if n == LOAD_SECOND:
                arena2 = core.sb("arena2", [P, max(size(second), 1)])
                load_weights(core, core.place_weights(second, arena2))
            if n == LOAD_LAST:
                load_weights(core, core.place_weights(last, arena))
            layer(core)
        store_everything(core, out)


def kernel(**inputs):
    import concourse.bacc as _bacc
    from concourse.bass_utils import run_bass_kernel_spmd as _run

    laid_out = lay_out({k: np.asarray(v) for k, v in inputs.items()})
    nc = _bacc.Bacc("TRN2", target_bir_lowering=False, num_devices=1)
    arrays, aps = {}, {}
    for name, array in laid_out.items():
        arrays[f"in_{name.replace('.', '_')}"] = np.ascontiguousarray(array)
        aps[name] = nc.dram_tensor(f"in_{name.replace('.', '_')}", array.shape, mybir.dt.from_np(array.dtype),
                                   kind="ExternalInput").ap()
    out = nc.dram_tensor("out_tokens", (B, S, D), FP32, kind="ExternalOutput").ap()
    build(nc, aps, out)
    return _run(nc, [arrays], core_ids=[0]).results[0]["out_tokens"]
```
